# Optimizing a Trainium2 kernel written in Bass

```python
import numpy as np
import jax
import jax.numpy as jnp

def _softmax(x, axis=-1):
    return jax.nn.softmax(x, axis=axis)

def _gelu(x):
    return jax.nn.gelu(x, approximate=True)

def _silu(x):
    return jax.nn.silu(x)

def _sigmoid(x):
    return jax.nn.sigmoid(x)

def _layernorm(x, axis=-1, eps=1e-05):
    m = jnp.mean(x, axis=axis, keepdims=True)
    v = jnp.var(x, axis=axis, keepdims=True)
    return (x - m) / jnp.sqrt(v + eps)

def _scatter_add(tgt, idx, src, axis=0):
    return tgt.at[idx].add(src)

def _segment_sum(src, seg, n):
    return jax.ops.segment_sum(src, seg, n)
kernel_name = 'mk_xattn_ffn_d4_seqx_r8_cc85b9'

def setup_inputs(seed: int=0):
    np.random.seed(seed)
    _w = jnp.asarray

    def _rec_inputs():
        import jax
        import jax.numpy as jnp
        _rk = jax.random.key(seed)
        x = 6.313e-05 + 0.9998 * jax.random.normal(jax.random.fold_in(_rk, 1), (32, 64, 128), jnp.float32)
        _lenS = 64 - jax.random.randint(jax.random.fold_in(_rk, 7), (32,), 0, max(1, 64 // 4) + 1, jnp.int32)
        _lenS2 = 64 - jax.random.randint(jax.random.fold_in(_rk, 8), (32,), 0, max(1, 64 // 4) + 1, jnp.int32)
        _ctx_1024P = jax.random.normal(jax.random.fold_in(_rk, 11), (32, 16, 128), jnp.float32)
        _ctx_1024c = jax.random.dirichlet(jax.random.fold_in(_rk, 511), 0.3 * jnp.ones((16,), jnp.float32), (32, 64))
        _ctx_1024t = jnp.einsum('bsk,bkd->bsd', _ctx_1024c, _ctx_1024P)
        _ctx_1024t = _ctx_1024t * jax.lax.rsqrt(jnp.mean(jnp.square(_ctx_1024t)) + 1e-12) * 0.953939
        ctx_1024 = -0.000214406 + 1.00034 * (_ctx_1024t + 0.3 * jax.random.normal(jax.random.fold_in(_rk, 611), (32, 64, 128), jnp.float32))
        _validS = jnp.arange(64)[None, :] < _lenS[:, None]
        _validS2 = jnp.arange(64)[None, :] < _lenS2[:, None]
        _causal = jnp.tril(jnp.ones((64, 64), dtype=bool))
        mask_Bx1xSxS2_ik0 = jnp.where(jnp.broadcast_to(_validS2[:, None, None, :], (32, 1, 64, 64)), 0, 1).astype(jnp.int32)
        return (x, ctx_1024, mask_Bx1xSxS2_ik0)
    x, ctx_1024, mask_Bx1xSxS2_ik0 = _rec_inputs()

    def _L0_xattn_setup():
        import jax, jax.numpy as jnp
        import numpy as np
        from jax import lax
        BIG = jnp.float32(1e+30)

        def _pairwise_euclidean(a, b):
            aa = jnp.sum(a * a, axis=-1)[:, None]
            bb = jnp.sum(b * b, axis=-1)[None, :]
            ab = a @ b.T
            return jnp.sqrt(jnp.maximum(aa + bb - 2.0 * ab, 0.0))

        def _dtw_cost(D):
            row0 = jnp.cumsum(D[0])

            def row_step(prev_row, d_row):
                first = d_row[0] + prev_row[0]

                def col_step(left, inp):
                    d_ij, up, diag = inp
                    r = d_ij + jnp.minimum(jnp.minimum(up, left), diag)
                    return (r, r)
                _, rest = lax.scan(col_step, first, (d_row[1:], prev_row[1:], prev_row[:-1]))
                row = jnp.concatenate([first[None], rest])
                return (row, row)
            _, rows = lax.scan(row_step, row0, D[1:])
            return jnp.concatenate([row0[None], rows], axis=0)

        def _backtrack(R, T1, T2):
            L = T1 + T2 - 1

            def step(carry, _):
                i, j, done = carry
                valid = jnp.logical_not(done)
                cd = jnp.where((i > 0) & (j > 0), R[jnp.maximum(i - 1, 0), jnp.maximum(j - 1, 0)], BIG)
                cu = jnp.where(i > 0, R[jnp.maximum(i - 1, 0), j], BIG)
                cl = jnp.where(j > 0, R[i, jnp.maximum(j - 1, 0)], BIG)
                choice = jnp.argmin(jnp.stack([cd, cu, cl]))
                ni = jnp.where(choice <= 1, i - 1, i)
                nj = jnp.where((choice == 0) | (choice == 2), j - 1, j)
                at_origin = (i == 0) & (j == 0)
                ni = jnp.where(at_origin, 0, ni)
                nj = jnp.where(at_origin, 0, nj)
                return ((ni, nj, done | at_origin), (i, j, valid))
            init = (jnp.int32(T1 - 1), jnp.int32(T2 - 1), jnp.bool_(False))
            _, (i_idx, j_idx, valid) = lax.scan(step, init, None, length=L)
            return (i_idx, j_idx, valid)

        def _align_one(small, large):
            T_small, d = small.shape
            T_large = large.shape[0]
            D = _pairwise_euclidean(small, large)
            R = _dtw_cost(D)
            i_idx, j_idx, valid = _backtrack(R, T_small, T_large)
            contrib = small[i_idx] * valid[:, None].astype(small.dtype)
            expanded = jnp.zeros((T_large, d), dtype=small.dtype).at[j_idx].add(contrib)
            return expanded
        key = jax.random.key(seed)
        k1, k2 = jax.random.split(key)
        teacher = jax.random.normal(k1, (16, 50, 128), dtype=jnp.float32)
        student = jax.random.normal(k2, (16, 75, 128), dtype=jnp.float32)
        return {'teacher_features': teacher, 'student_features': student}
    _L0_xattn_all = _L0_xattn_setup()
    _L0_xattn_in = {k: v for k, v in _L0_xattn_all.items() if k in ()}
    del _L0_xattn_all

    def _L0_ffn_setup():
        import jax, jax.numpy as jnp
        import numpy as np
        B, S, D_MODEL, D_HIDDEN = (4, 256, 128, 512)

        def act_quant(x):
            scale = 127.0 / jnp.clip(jnp.max(jnp.abs(x), axis=-1, keepdims=True), 1e-05)
            return jnp.clip(jnp.round(x * scale), -128, 127) / scale

        def weight_quant(w):
            scale = 1.0 / jnp.clip(jnp.mean(jnp.abs(w)), 1e-05)
            return jnp.clip(jnp.round(w * scale), -1, 1) / scale

        def bit_linear(x, w):
            xq = x + jax.lax.stop_gradient(act_quant(x) - x)
            wq = w + jax.lax.stop_gradient(weight_quant(w) - w)
            return jnp.einsum('bsd,hd->bsh', xq, wq)

        def depthwise_conv1d(x_bcl, w, b):
            y = jax.lax.conv_general_dilated(x_bcl, w, window_strides=(1,), padding=[(1, 1)], dimension_numbers=('NCH', 'OIH', 'NCH'), feature_group_count=x_bcl.shape[1])
            return y + b[None, :, None]
        key = jax.random.key(seed)
        ks = jax.random.split(key, 5)
        lim1 = 1.0 / np.sqrt(D_MODEL)
        lim2 = 1.0 / np.sqrt(D_HIDDEN)
        limc = 1.0 / np.sqrt(3.0)
        return {'x': jax.random.normal(ks[0], (B, S, D_MODEL), dtype=jnp.float32), 'w1': jax.random.uniform(ks[1], (D_HIDDEN, D_MODEL), jnp.float32, -lim1, lim1), 'conv_w': jax.random.uniform(ks[2], (D_HIDDEN, 1, 3), jnp.float32, -limc, limc), 'conv_b': jax.random.uniform(ks[3], (D_HIDDEN,), jnp.float32, -limc, limc), 'w2': jax.random.uniform(ks[4], (D_MODEL, D_HIDDEN), jnp.float32, -lim2, lim2)}
    _L0_ffn_all = _L0_ffn_setup()
    _L0_ffn_in = {k: v for k, v in _L0_ffn_all.items() if k in ('w1', 'conv_w', 'conv_b', 'w2')}
    del _L0_ffn_all

    def _L1_xattn_setup():
        import jax, jax.numpy as jnp
        import numpy as np
        key = jax.random.key(seed)
        ks = jax.random.split(key, 8)
        b, l, d_model, h = (4, 256, 128, 8)
        std = 0.1
        return {'keys': jax.random.normal(ks[0], (b, l, d_model), dtype=jnp.float32), 'queries': jax.random.normal(ks[1], (b, l, d_model), dtype=jnp.float32), 'values': jax.random.normal(ks[2], (b, l, d_model), dtype=jnp.float32), 'Wk': std * jax.random.normal(ks[3], (d_model, d_model), dtype=jnp.float32), 'Wq': std * jax.random.normal(ks[4], (d_model, d_model), dtype=jnp.float32), 'Wv': std * jax.random.normal(ks[5], (d_model, d_model), dtype=jnp.float32), 'Wu': std * jax.random.normal(ks[6], (d_model, d_model), dtype=jnp.float32), 'bu': std * jax.random.normal(ks[7], (d_model,), dtype=jnp.float32), 'n_heads': h}
    _L1_xattn_all = _L1_xattn_setup()
    _L1_xattn_in = {k: v for k, v in _L1_xattn_all.items() if k in ('Wk', 'Wq', 'Wv', 'Wu', 'bu')}
    del _L1_xattn_all

    def _L1_ffn_setup():
        import jax, jax.numpy as jnp
        import numpy as np
        TOP_K = 2
        TEMP = 1.0
        key = jax.random.key(seed)
        ks = jax.random.split(key, 5)
        B, S, D, E = (4, 256, 128, 8)
        F = 4 * D
        x = jax.random.normal(ks[0], (B, S, D), dtype=jnp.float32)
        Wg = jax.random.normal(ks[1], (D, E), dtype=jnp.float32) * (1.0 / np.sqrt(D))
        bg = jnp.zeros((E,), dtype=jnp.float32)
        W1 = jax.random.normal(ks[2], (E, D, F), dtype=jnp.float32) * (1.0 / np.sqrt(D))
        b1 = jnp.zeros((E, F), dtype=jnp.float32)
        W2 = jax.random.normal(ks[3], (E, F, D), dtype=jnp.float32) * (1.0 / np.sqrt(F))
        b2 = jnp.zeros((E, D), dtype=jnp.float32)
        return {'x': x, 'Wg': Wg, 'bg': bg, 'W1': W1, 'b1': b1, 'W2': W2, 'b2': b2}
    _L1_ffn_all = _L1_ffn_setup()
    _L1_ffn_in = {k: v for k, v in _L1_ffn_all.items() if k in ('Wg', 'bg', 'W1', 'b1', 'W2', 'b2')}
    del _L1_ffn_all

    def _L2_xattn_setup():
        import jax, jax.numpy as jnp
        import numpy as np
        N, T, E, H = (2, 256, 128, 16)
        DH = E // H
        key = jax.random.key(seed)
        ks = jax.random.split(key, 8)
        query = jax.random.normal(ks[0], (N, T, E), dtype=jnp.float32)
        k_in = jax.random.normal(ks[1], (N, T, E), dtype=jnp.float32)
        v_in = jax.random.normal(ks[2], (N, T, E), dtype=jnp.float32)
        mask = jnp.broadcast_to(jnp.tril(jnp.ones((T, T), dtype=jnp.int32))[None, None], (N, 1, T, T))
        s = 1.0 / np.sqrt(E)
        Wq = jax.random.normal(ks[3], (H, E, DH), dtype=jnp.float32) * s
        Wk = jax.random.normal(ks[4], (H, E, DH), dtype=jnp.float32) * s
        Wv = jax.random.normal(ks[5], (H, E, DH), dtype=jnp.float32) * s
        Wo = jax.random.normal(ks[6], (E, H * DH), dtype=jnp.float32) * s
        bo = jax.random.normal(ks[7], (E,), dtype=jnp.float32) * s
        return {'query': query, 'key': k_in, 'value': v_in, 'mask': mask, 'Wq': Wq, 'Wk': Wk, 'Wv': Wv, 'Wo': Wo, 'bo': bo}
    _L2_xattn_all = _L2_xattn_setup()
    _L2_xattn_in = {k: v for k, v in _L2_xattn_all.items() if k in ('Wq', 'Wk', 'Wv', 'Wo', 'bo')}
    del _L2_xattn_all

    def _L2_ffn_setup():
        import jax, jax.numpy as jnp
        import numpy as np
        B, M, D = (4, 256, 128)
        N, P = (64, 32)
        key = jax.random.key(seed)
        k1, k2, k3, k4 = jax.random.split(key, 4)
        x = jax.random.normal(k1, (B, M, D), dtype=jnp.float32)
        phi = jax.random.normal(k2, (D, N, P), dtype=jnp.float32) * (1.0 / np.sqrt(D))
        W = jax.random.normal(k3, (N, D, D), dtype=jnp.float32) * (1.0 / np.sqrt(D))
        b = jax.random.normal(k4, (N, D), dtype=jnp.float32) * 0.01
        return {'x': x, 'phi': phi, 'W': W, 'b': b}
    _L2_ffn_all = _L2_ffn_setup()
    _L2_ffn_in = {k: v for k, v in _L2_ffn_all.items() if k in ('phi', 'W', 'b')}
    del _L2_ffn_all

    def _L3_xattn_setup():
        import jax, jax.numpy as jnp
        import numpy as np
        D_MODEL = 128
        NUM_HEADS = 16
        D_K = D_MODEL // NUM_HEADS
        key = jax.random.key(seed)
        ks = jax.random.split(key, 11)
        B, S, D = (4, 256, D_MODEL)
        s = 1.0 / np.sqrt(D)
        return {'query': jax.random.normal(ks[0], (B, S, D), jnp.float32), 'key': jax.random.normal(ks[1], (B, S, D), jnp.float32), 'value': jax.random.normal(ks[2], (B, S, D), jnp.float32), 'Wq': jax.random.normal(ks[3], (D, D), jnp.float32) * s, 'bq': jnp.zeros((D,), jnp.float32), 'Wk': jax.random.normal(ks[4], (D, D), jnp.float32) * s, 'bk': jnp.zeros((D,), jnp.float32), 'Wv': jax.random.normal(ks[5], (D, D), jnp.float32) * s, 'bv': jnp.zeros((D,), jnp.float32), 'Wo': jax.random.normal(ks[6], (D, D), jnp.float32) * s, 'bo': jnp.zeros((D,), jnp.float32)}
    _L3_xattn_all = _L3_xattn_setup()
    _L3_xattn_in = {k: v for k, v in _L3_xattn_all.items() if k in ('Wq', 'bq', 'Wk', 'bk', 'Wv', 'bv', 'Wo', 'bo')}
    del _L3_xattn_all

    def _L3_ffn_setup():
        import jax, jax.numpy as jnp
        import numpy as np
        B, T, D_MODEL = (4, 256, 128)
        N_EXPERTS, TOP_K, D_EXPERT = (6, 2, 64)
        QUANT_TEMP = 0.3
        _ANCHOR_IDS = [63, 6, 0, 18, 45, 27]

        def _q6_idx_to_vertex(idx):
            bits = [idx >> 5 - b & 1 for b in range(6)]
            return [2.0 * b - 1.0 for b in bits]

        def _anchors():
            return jnp.asarray(np.array([_q6_idx_to_vertex(i) for i in _ANCHOR_IDS], dtype=np.float32))

        def _router(x, proj_w, anchors, routing_temp):
            z = jnp.einsum('btd,ed->bte', x, proj_w)
            q = jnp.tanh(z / QUANT_TEMP)
            dot = jnp.einsum('btd,ed->bte', q, anchors)
            hamming = (6.0 - dot) * 0.5
            logits = -hamming / jnp.clip(routing_temp, 0.1)
            topk_logits, topk_idx = jax.lax.top_k(logits, TOP_K)
            topk_w = jax.nn.softmax(topk_logits, axis=-1)
            onehot = jax.nn.one_hot(topk_idx, N_EXPERTS, dtype=x.dtype)
            expert_weights = jnp.einsum('btke,btk->bte', onehot, topk_w)
            return (expert_weights, q)
        key = jax.random.key(seed)
        k_x, k_p, k_w1, k_w2 = jax.random.split(key, 4)
        x = jax.random.normal(k_x, (B, T, D_MODEL), dtype=jnp.float32)
        proj_w = jax.random.normal(k_p, (6, D_MODEL), dtype=jnp.float32) * 0.02
        anchors = _anchors()
        routing_temp = jnp.array(1.0, dtype=jnp.float32)
        s1 = 1.0 / np.sqrt(D_MODEL)
        s2 = 1.0 / np.sqrt(D_EXPERT)
        w1 = jax.random.uniform(k_w1, (N_EXPERTS, D_MODEL, D_EXPERT), jnp.float32, -s1, s1)
        w2 = jax.random.uniform(k_w2, (N_EXPERTS, D_EXPERT, D_MODEL), jnp.float32, -s2, s2)
        return {'x': x, 'proj_w': proj_w, 'anchors': anchors, 'routing_temp': routing_temp, 'w1': w1, 'w2': w2}
    _L3_ffn_all = _L3_ffn_setup()
    _L3_ffn_in = {k: v for k, v in _L3_ffn_all.items() if k in ('proj_w', 'anchors', 'routing_temp', 'w1', 'w2')}
    del _L3_ffn_all
    return {'x': x, 'ctx_1024': ctx_1024, 'mask_Bx1xSxS2_ik0': mask_Bx1xSxS2_ik0, 'L0_ffn_w1': _L0_ffn_in['w1'], 'L0_ffn_conv_w': _L0_ffn_in['conv_w'], 'L0_ffn_conv_b': _L0_ffn_in['conv_b'], 'L0_ffn_w2': _L0_ffn_in['w2'], 'L1_xattn_Wk': _L1_xattn_in['Wk'], 'L1_xattn_Wq': _L1_xattn_in['Wq'], 'L1_xattn_Wv': _L1_xattn_in['Wv'], 'L1_xattn_Wu': _L1_xattn_in['Wu'], 'L1_xattn_bu': _L1_xattn_in['bu'], 'L1_ffn_Wg': _L1_ffn_in['Wg'], 'L1_ffn_bg': _L1_ffn_in['bg'], 'L1_ffn_W1': _L1_ffn_in['W1'], 'L1_ffn_b1': _L1_ffn_in['b1'], 'L1_ffn_W2': _L1_ffn_in['W2'], 'L1_ffn_b2': _L1_ffn_in['b2'], 'L2_xattn_Wq': _L2_xattn_in['Wq'], 'L2_xattn_Wk': _L2_xattn_in['Wk'], 'L2_xattn_Wv': _L2_xattn_in['Wv'], 'L2_xattn_Wo': _L2_xattn_in['Wo'], 'L2_xattn_bo': _L2_xattn_in['bo'], 'L2_ffn_phi': _L2_ffn_in['phi'], 'L2_ffn_W': _L2_ffn_in['W'], 'L2_ffn_b': _L2_ffn_in['b'], 'L3_xattn_Wq': _L3_xattn_in['Wq'], 'L3_xattn_bq': _L3_xattn_in['bq'], 'L3_xattn_Wk': _L3_xattn_in['Wk'], 'L3_xattn_bk': _L3_xattn_in['bk'], 'L3_xattn_Wv': _L3_xattn_in['Wv'], 'L3_xattn_bv': _L3_xattn_in['bv'], 'L3_xattn_Wo': _L3_xattn_in['Wo'], 'L3_xattn_bo': _L3_xattn_in['bo'], 'L3_ffn_proj_w': _L3_ffn_in['proj_w'], 'L3_ffn_anchors': _L3_ffn_in['anchors'], 'L3_ffn_routing_temp': _L3_ffn_in['routing_temp'], 'L3_ffn_w1': _L3_ffn_in['w1'], 'L3_ffn_w2': _L3_ffn_in['w2']}

def reference(x, ctx_1024, mask_Bx1xSxS2_ik0, L0_ffn_w1, L0_ffn_conv_w, L0_ffn_conv_b, L0_ffn_w2, L1_xattn_Wk, L1_xattn_Wq, L1_xattn_Wv, L1_xattn_Wu, L1_xattn_bu, L1_ffn_Wg, L1_ffn_bg, L1_ffn_W1, L1_ffn_b1, L1_ffn_W2, L1_ffn_b2, L2_xattn_Wq, L2_xattn_Wk, L2_xattn_Wv, L2_xattn_Wo, L2_xattn_bo, L2_ffn_phi, L2_ffn_W, L2_ffn_b, L3_xattn_Wq, L3_xattn_bq, L3_xattn_Wk, L3_xattn_bk, L3_xattn_Wv, L3_xattn_bv, L3_xattn_Wo, L3_xattn_bo, L3_ffn_proj_w, L3_ffn_anchors, L3_ffn_routing_temp, L3_ffn_w1, L3_ffn_w2):
    import jax
    import jax.numpy as jnp

    def _L0_xattn_ref(teacher_features, student_features):
        import jax, jax.numpy as jnp
        import numpy as np
        from jax import lax
        BIG = jnp.float32(1e+30)

        def _pairwise_euclidean(a, b):
            aa = jnp.sum(a * a, axis=-1)[:, None]
            bb = jnp.sum(b * b, axis=-1)[None, :]
            ab = a @ b.T
            return jnp.sqrt(jnp.maximum(aa + bb - 2.0 * ab, 0.0))

        def _dtw_cost(D):
            row0 = jnp.cumsum(D[0])

            def row_step(prev_row, d_row):
                first = d_row[0] + prev_row[0]

                def col_step(left, inp):
                    d_ij, up, diag = inp
                    r = d_ij + jnp.minimum(jnp.minimum(up, left), diag)
                    return (r, r)
                _, rest = lax.scan(col_step, first, (d_row[1:], prev_row[1:], prev_row[:-1]))
                row = jnp.concatenate([first[None], rest])
                return (row, row)
            _, rows = lax.scan(row_step, row0, D[1:])
            return jnp.concatenate([row0[None], rows], axis=0)

        def _backtrack(R, T1, T2):
            L = T1 + T2 - 1

            def step(carry, _):
                i, j, done = carry
                valid = jnp.logical_not(done)
                cd = jnp.where((i > 0) & (j > 0), R[jnp.maximum(i - 1, 0), jnp.maximum(j - 1, 0)], BIG)
                cu = jnp.where(i > 0, R[jnp.maximum(i - 1, 0), j], BIG)
                cl = jnp.where(j > 0, R[i, jnp.maximum(j - 1, 0)], BIG)
                choice = jnp.argmin(jnp.stack([cd, cu, cl]))
                ni = jnp.where(choice <= 1, i - 1, i)
                nj = jnp.where((choice == 0) | (choice == 2), j - 1, j)
                at_origin = (i == 0) & (j == 0)
                ni = jnp.where(at_origin, 0, ni)
                nj = jnp.where(at_origin, 0, nj)
                return ((ni, nj, done | at_origin), (i, j, valid))
            init = (jnp.int32(T1 - 1), jnp.int32(T2 - 1), jnp.bool_(False))
            _, (i_idx, j_idx, valid) = lax.scan(step, init, None, length=L)
            return (i_idx, j_idx, valid)

        def _align_one(small, large):
            T_small, d = small.shape
            T_large = large.shape[0]
            D = _pairwise_euclidean(small, large)
            R = _dtw_cost(D)
            i_idx, j_idx, valid = _backtrack(R, T_small, T_large)
            contrib = small[i_idx] * valid[:, None].astype(small.dtype)
            expanded = jnp.zeros((T_large, d), dtype=small.dtype).at[j_idx].add(contrib)
            return expanded
        return jax.vmap(_align_one)(teacher_features, student_features)

    def _L0_ffn_ref(x, w1, conv_w, conv_b, w2):
        import jax, jax.numpy as jnp
        import numpy as np
        B, S, D_MODEL, D_HIDDEN = (4, 256, 128, 512)

        def act_quant(x):
            scale = 127.0 / jnp.clip(jnp.max(jnp.abs(x), axis=-1, keepdims=True), 1e-05)
            return jnp.clip(jnp.round(x * scale), -128, 127) / scale

        def weight_quant(w):
            scale = 1.0 / jnp.clip(jnp.mean(jnp.abs(w)), 1e-05)
            return jnp.clip(jnp.round(w * scale), -1, 1) / scale

        def bit_linear(x, w):
            xq = x + jax.lax.stop_gradient(act_quant(x) - x)
            wq = w + jax.lax.stop_gradient(weight_quant(w) - w)
            return jnp.einsum('bsd,hd->bsh', xq, wq)

        def depthwise_conv1d(x_bcl, w, b):
            y = jax.lax.conv_general_dilated(x_bcl, w, window_strides=(1,), padding=[(1, 1)], dimension_numbers=('NCH', 'OIH', 'NCH'), feature_group_count=x_bcl.shape[1])
            return y + b[None, :, None]
        h = bit_linear(x, w1)
        h = depthwise_conv1d(h.transpose(0, 2, 1), conv_w, conv_b)
        h = h.transpose(0, 2, 1)
        h = jax.nn.silu(h)
        return bit_linear(h, w2)

    def _L1_xattn_ref(keys, queries, values, Wk, Wq, Wv, Wu, bu, n_heads):
        import jax, jax.numpy as jnp
        import numpy as np
        b, l, d_model = keys.shape
        h = n_heads
        dk = d_model // h

        def proj_split(x, W):
            y = x @ W.T
            y = jnp.transpose(y, (0, 2, 1))
            return y.reshape(b * h, l, dk)
        K = proj_split(keys, Wk)
        Q = proj_split(queries, Wq)
        V = proj_split(values, Wv)
        scale = dk ** (-0.25)
        Qs = Q * scale
        Vs = V * scale
        Ks = K * scale
        dot1 = jax.nn.softmax(jnp.einsum('blk,bmk->blm', Qs, Ks), axis=-1) * 0.5
        dot2 = jax.nn.softmax(jnp.einsum('blk,bmk->blm', Vs, Ks), axis=-1) * 0.5
        out = jnp.einsum('blm,bmk->blk', dot1, K) + jnp.einsum('blm,bmk->blk', dot2, K)
        out = out.reshape(b, h, l, dk)
        out = jnp.transpose(out, (0, 2, 1, 3)).reshape(b, l, h * dk)
        return out @ Wu.T + bu

    def _L1_ffn_ref(x, Wg, bg, W1, b1, W2, b2):
        import jax, jax.numpy as jnp
        import numpy as np
        TOP_K = 2
        TEMP = 1.0
        gates = (jnp.einsum('bsd,de->bse', x, Wg) + bg) / (TEMP + 1e-06)
        weights, indices = jax.lax.top_k(gates, TOP_K)
        weights = jax.nn.softmax(weights, axis=-1)
        h = jax.nn.silu(jnp.einsum('bsd,edf->bsef', x, W1) + b1)
        all_out = jnp.einsum('bsef,efd->bsed', h, W2) + b2
        gathered = jnp.take_along_axis(all_out, indices[..., None], axis=2)
        out = jnp.sum(gathered * weights[..., None], axis=2)
        return out

    def _L2_xattn_ref(query, key, value, mask, Wq, Wk, Wv, Wo, bo):
        import jax, jax.numpy as jnp
        import numpy as np
        N, T, E, H = (2, 256, 128, 16)
        DH = E // H
        q = jnp.einsum('nte,hed->nhtd', query, Wq)
        k = jnp.einsum('nte,hed->nhtd', key, Wk)
        v = jnp.einsum('nte,hed->nhtd', value, Wv)
        energy = jnp.einsum('nhqd,nhkd->nhqk', q, k)
        energy = jnp.where(mask == 0, jnp.float32(-1e+20), energy)
        attn = jax.nn.softmax(energy / jnp.float32(np.sqrt(DH)), axis=-1)
        out = jnp.einsum('nhqk,nhkd->nhqd', attn, v)
        concat = out.transpose(0, 2, 1, 3).reshape(query.shape[0], query.shape[1], H * DH)
        return concat @ Wo.T + bo

    def _L2_ffn_ref(x, phi, W, b):
        import jax, jax.numpy as jnp
        import numpy as np
        B, M, D = (4, 256, 128)
        N, P = (64, 32)
        logits = jnp.einsum('bmd,dnp->bmnp', x, phi)
        dispatch = jax.nn.softmax(logits, axis=0)
        bsz, m, n, p = logits.shape
        combine = jax.nn.softmax(logits.reshape(bsz, m, n * p), axis=-1).reshape(bsz, m, n, p)
        slots = jnp.einsum('bmd,bmnp->bnpd', x, dispatch)
        y = jnp.einsum('bnpd,nde->bnpe', slots, W) + b[None, :, None, :]
        out = jnp.einsum('bnpd,bmnp->bmd', y, combine)
        return out

    def _L3_xattn_ref(query, key, value, Wq, bq, Wk, bk, Wv, bv, Wo, bo):
        import jax, jax.numpy as jnp
        import numpy as np
        D_MODEL = 128
        NUM_HEADS = 16
        D_K = D_MODEL // NUM_HEADS
        B, S, D = query.shape
        H, dk = (NUM_HEADS, D_K)
        Q = (query @ Wq + bq).reshape(B, S, H, dk).transpose(0, 2, 1, 3)
        K = (key @ Wk + bk).reshape(B, S, H, dk).transpose(0, 2, 1, 3)
        V = (value @ Wv + bv).reshape(B, S, H, dk).transpose(0, 2, 1, 3)
        scores = jnp.einsum('bhqd,bhkd->bhqk', Q, K) / np.sqrt(dk).astype(np.float32)
        attn = jax.nn.softmax(scores, axis=-1)
        out = jnp.einsum('bhqk,bhkd->bhqd', attn, V)
        out = out.transpose(0, 2, 1, 3).reshape(B, S, D)
        return out @ Wo + bo

    def _L3_ffn_ref(x, proj_w, anchors, routing_temp, w1, w2):
        import jax, jax.numpy as jnp
        import numpy as np
        B, T, D_MODEL = (4, 256, 128)
        N_EXPERTS, TOP_K, D_EXPERT = (6, 2, 64)
        QUANT_TEMP = 0.3
        _ANCHOR_IDS = [63, 6, 0, 18, 45, 27]

        def _q6_idx_to_vertex(idx):
            bits = [idx >> 5 - b & 1 for b in range(6)]
            return [2.0 * b - 1.0 for b in bits]

        def _anchors():
            return jnp.asarray(np.array([_q6_idx_to_vertex(i) for i in _ANCHOR_IDS], dtype=np.float32))

        def _router(x, proj_w, anchors, routing_temp):
            z = jnp.einsum('btd,ed->bte', x, proj_w)
            q = jnp.tanh(z / QUANT_TEMP)
            dot = jnp.einsum('btd,ed->bte', q, anchors)
            hamming = (6.0 - dot) * 0.5
            logits = -hamming / jnp.clip(routing_temp, 0.1)
            topk_logits, topk_idx = jax.lax.top_k(logits, TOP_K)
            topk_w = jax.nn.softmax(topk_logits, axis=-1)
            onehot = jax.nn.one_hot(topk_idx, N_EXPERTS, dtype=x.dtype)
            expert_weights = jnp.einsum('btke,btk->bte', onehot, topk_w)
            return (expert_weights, q)
        expert_weights, q = _router(x, proj_w, anchors, routing_temp)
        h = jax.nn.gelu(jnp.einsum('btd,edh->bteh', x, w1))
        out = jnp.einsum('bteh,ehd,bte->btd', h, w2, expert_weights)
        return out
    x = x + _L0_xattn_ref(ctx_1024, _layernorm(x, axis=-1))
    x = x + _L0_ffn_ref(_layernorm(x, axis=-1), L0_ffn_w1, L0_ffn_conv_w, L0_ffn_conv_b, L0_ffn_w2)
    x = x + _L1_xattn_ref(ctx_1024, _layernorm(x, axis=-1), ctx_1024, L1_xattn_Wk, L1_xattn_Wq, L1_xattn_Wv, L1_xattn_Wu, L1_xattn_bu, 8)
    x = x + _L1_ffn_ref(_layernorm(x, axis=-1), L1_ffn_Wg, L1_ffn_bg, L1_ffn_W1, L1_ffn_b1, L1_ffn_W2, L1_ffn_b2)
    x = x + _L2_xattn_ref(_layernorm(x, axis=-1), ctx_1024, ctx_1024, mask_Bx1xSxS2_ik0, L2_xattn_Wq, L2_xattn_Wk, L2_xattn_Wv, L2_xattn_Wo, L2_xattn_bo)
    x = x + _L2_ffn_ref(_layernorm(x, axis=-1), L2_ffn_phi, L2_ffn_W, L2_ffn_b)
    x = x + _L3_xattn_ref(_layernorm(x, axis=-1), ctx_1024, ctx_1024, L3_xattn_Wq, L3_xattn_bq, L3_xattn_Wk, L3_xattn_bk, L3_xattn_Wv, L3_xattn_bv, L3_xattn_Wo, L3_xattn_bo)
    x = x + _L3_ffn_ref(_layernorm(x, axis=-1), L3_ffn_proj_w, L3_ffn_anchors, L3_ffn_routing_temp, L3_ffn_w1, L3_ffn_w2)
    return x

_drawn_inputs = setup_inputs


def setup_inputs(seed=0):
    import zlib

    import numpy as np

    out = dict(_drawn_inputs(seed))
    spreads = {'L1_ffn_bg': (0.0, 0.1),
     'L1_ffn_b1': (0.0, 0.285),
     'L1_ffn_b2': (0.0, 0.1),
     'L3_xattn_bq': (0.0, 0.503),
     'L3_xattn_bk': (0.0, 2.0),
     'L3_xattn_bv': (0.0, 0.1),
     'L3_xattn_bo': (0.0, 0.1)}
    factors = {'L2_ffn_b': 57.032}
    for name, (base, spread) in spreads.items():
        noise = np.random.default_rng([zlib.crc32(name.encode()), seed]).standard_normal(out[name].shape)
        drawn = base * np.exp(spread * noise) if base else spread * noise
        out[name] = jnp.asarray(drawn.astype(out[name].dtype))
    for name, factor in factors.items():
        out[name] = (out[name] * factor).astype(out[name].dtype)
    return out
```

```python
from contextlib import ExitStack

import concourse.bass as bass
from concourse import mybir

STAGES = [0, 1, 2, 3, 4, 5, 6, 7]

F32 = mybir.dt.float32
BF16 = mybir.dt.bfloat16
I32 = mybir.dt.int32
ALU = mybir.AluOpType
ACT = mybir.ActivationFunctionType
AX = mybir.AxisListType

B, S, D = 32, 64, 128
N = B * S
T = N // 128
G = 4
BIG = 1e30
EPS = 1e-5
ROUND = 1.5 * 2.0 ** 23


class Core:
    pass


class Step:

    def __init__(self, nc, name):
        self.nc, self.name, self.ctx = nc, name, ExitStack()

    def __enter__(self):
        return self

    def __exit__(self, *exc):
        self.ctx.close()

    def sb(self, name, shape, dt=F32):
        return self.ctx.enter_context(self.nc.sbuf_tensor(f"{self.name}_{name}", shape, dt))

    def ps(self, name, shape, dt=F32):
        return self.ctx.enter_context(self.nc.psum_tensor(f"{self.name}_{name}", shape, dt))

    def sem(self, name):
        return self.ctx.enter_context(self.nc.semaphore(f"{self.name}_{name}"))

    def block(self):
        return self.ctx.enter_context(self.nc.Block())


def layernorm(nc, core, name):
    x, xn, xnT = core.x, core.xn, core.xnT
    with Step(nc, name) as st:
        stats = st.sb("stats", [128, T, 6])
        meanvar = st.sb("meanvar", [128, T, 2])
        std = st.sb("std", [128, T])
        rstd = st.sb("rstd", [128, T])
        turned = [st.ps(f"turned{i}", [128, 512]) for i in range(G)]
        stats_done = st.sem("stats_done")
        var_done = st.sem("var_done")
        std_done = st.sem("std_done")
        rstd_done = st.sem("rstd_done")
        xn_done = st.sem("xn_done")
        turned_done = st.sem("turned_done")
        block = st.block()

        @block.vector
        def _(dve):
            if core.wait_x:
                dve.wait_ge(core.loaded["x"], 16)
            for t in range(T):
                last = nc.vector.bn_stats(stats[:, t, :], x[:, t, :])
            last.then_inc(stats_done, 1)
            dve.wait_ge(stats_done, 1)
            for t in range(T):
                last = nc.vector.bn_aggr(meanvar[:, t, :], stats[:, t, :])
            last.then_inc(var_done, 1)
            dve.wait_ge(std_done, 1)
            nc.vector.reciprocal(rstd[:], std[:]).then_inc(rstd_done, 1)
            dve.wait_ge(rstd_done, 1)
            for t in range(T):
                nc.vector.tensor_scalar(xn[:, t, :], x[:, t, :], meanvar[:, t, 0:1], rstd[:, t:t + 1],
                                        ALU.subtract, ALU.mult).then_inc(xn_done, 1)

        @block.scalar
        def _(act):
            act.wait_ge(var_done, 1)
            if core.wait_consts:
                act.wait_ge(core.loaded["consts"], core.consts_count)
            nc.scalar.activation(std[:], meanvar[:, :, 1], ACT.Sqrt, bias=core.eps[:, 0:1]).then_inc(std_done, 1)
            for g in range(G):
                act.wait_ge(turned_done, g + 1)
                nc.scalar.activation(xnT[:, 512 * g:512 * g + 512], turned[g][:], ACT.Copy)

        @block.tensor
        def _(pe):
            if core.wait_consts:
                pe.wait_ge(core.loaded["consts"], core.consts_count)
            for t in range(T):
                pe.wait_ge(xn_done, t + 1)
                last = nc.tensor.transpose(turned[t // 4][:, 128 * (t % 4):128 * (t % 4) + 128], xn[:, t, :],
                                           core.ident[:])
                if t % 4 == 3:
                    last.then_inc(turned_done, 1)
    core.wait_x = core.wait_consts = False


def warp_costs(nc, core, costs_dram):
    ctx, ctxT, xnT = core.ctx_tok, core.ctxT, core.xnT
    with Step(nc, "costs") as st:
        xsq = st.sb("xsq", [128, N])
        csq = st.sb("csq", [128, T, D])
        ctx_norm = st.sb("ctx_norm", [128, T])
        norms = st.sb("norms", [128, T, S])
        dist2 = st.sb("dist2", [128, T, S])
        root = st.sb("root", [128, T, S])
        inv = st.sb("inv", [128, T, S])
        cost = st.sb("cost", [128, T, S])
        dots = st.ps("dots", [128, T, S])
        xnorm = st.ps("xnorm", [128, T, S])
        xsq_done = st.sem("xsq_done")
        xnorm_done = st.sem("xnorm_done")
        dots_done = st.sem("dots_done")
        dist2_done = st.sem("dist2_done")
        root_done = st.sem("root_done")
        vector_step = st.sem("vector_step")
        cost_done = st.sem("cost_done")
        cost_out = st.sem("cost_out")
        block = st.block()

        @block.scalar
        def _(act):
            nc.scalar.activation(xsq[:], xnT[:], ACT.Square).then_inc(xsq_done, 1)
            act.wait_ge(dist2_done, 1)
            nc.scalar.activation(root[:], dist2[:], ACT.Sqrt).then_inc(root_done, 1)

        @block.tensor
        def _(pe):
            pe.wait_ge(core.loaded["ctxT"], 16)
            for t in range(T):
                for h in range(2):
                    tok = slice(128 * t + S * h, 128 * t + S * h + S)
                    last = nc.tensor.matmul(dots[S * h:S * h + S, t, :], ctxT[:, tok], xnT[:, tok], start=True, stop=True)
            last.then_inc(dots_done, 1)
            pe.wait_ge(xsq_done, 1)
            sq = xsq[:].rearrange("p (t h j) -> p t h j", h=2, j=S)
            for h in range(2):
                for k in range(2):
                    last = nc.tensor.matmul(xnorm[S * h:S * h + S, 8 * k:8 * k + 8, :], core.ones[:, 0:S],
                                            sq[:, 8 * k:8 * k + 8, h, :], start=True, stop=True)
            last.then_inc(xnorm_done, 1)

        @block.vector
        def _(dve):
            n = 0

            dve.wait_ge(core.loaded["ctx"], 16)
            nc.vector.tensor_tensor(csq[:], ctx[:], ctx[:], ALU.mult).then_inc(vector_step, 1)
            dve.wait_ge(vector_step, 1)
            nc.vector.tensor_reduce(ctx_norm[:], csq[:], AX.X, ALU.add).then_inc(vector_step, 1)
            dve.wait_ge(vector_step, 2)
            dve.wait_ge(xnorm_done, 1)
            nc.vector.tensor_tensor(norms[:], xnorm[:], ctx_norm[:].unsqueeze(2).broadcast_to([128, T, S]),
                                    ALU.add).then_inc(vector_step, 1)
            dve.wait_ge(vector_step, 3)
            dve.wait_ge(dots_done, 1)
            nc.vector.scalar_tensor_tensor(dist2[:], dots[:], -2.0, norms[:], ALU.mult, ALU.add).then_inc(vector_step, 1)
            dve.wait_ge(vector_step, 4)
            nc.vector.tensor_scalar_max(dist2[:], dist2[:], 0.0).then_inc(dist2_done, 1)
            dve.wait_ge(root_done, 1)
            nc.vector.tensor_scalar_max(inv[:], root[:], 1e-30).then_inc(vector_step, 1)
            dve.wait_ge(vector_step, 5)
            nc.vector.reciprocal(cost[:], inv[:]).then_inc(vector_step, 1)
            dve.wait_ge(vector_step, 6)
            nc.vector.tensor_tensor(inv[:], dist2[:], cost[:], ALU.mult).then_inc(vector_step, 1)
            dve.wait_ge(vector_step, 7)
            nc.vector.tensor_tensor(norms[:], inv[:], root[:], ALU.add).then_inc(vector_step, 1)
            dve.wait_ge(vector_step, 8)
            nc.vector.tensor_scalar_mul(cost[:], norms[:], 0.5).then_inc(cost_done, 1)

        @block.sync
        def _(sp):
            sp.wait_ge(cost_done, 1)
            sp.dma_start(costs_dram.rearrange("(t h) i j -> (h i) t j", h=2), cost[:]).then_inc(cost_out, 16)
            sp.wait_ge(cost_out, 16)


def warp_path(nc, core, costs_dram, path_dram):
    W = S + 1
    with Step(nc, "warp") as st:
        cost = st.sb("cost", [B, S, S])
        table = st.sb("table", [B, W, W])
        best = st.sb("best", [B, S, S])
        left = st.sb("left", [B, S, W])
        over = st.sb("over", [B, 2, 8, S])
        stay = st.sb("stay", [B, 8, S])
        diag = st.sb("diag", [B, 8, S])
        go = st.sb("go", [B, 2, S, S])
        path = st.sb("path", [B, S, S])
        leave = st.sb("leave", [B, 2, W])
        enter = st.sb("enter", [B, S])
        cost_in = st.sem("cost_in")
        border_done = st.sem("border_done")
        corner_done = st.sem("corner_done")
        best_done = st.sem("best_done")
        row_done = st.sem("row_done")
        over_done = st.sem("over_done")
        left_done = st.sem("left_done")
        stay_done = st.sem("stay_done")
        diag_done = st.sem("diag_done")
        godiag_done = st.sem("godiag_done")
        goup_done = st.sem("goup_done")
        leave_done = st.sem("leave_done")
        enter_done = st.sem("enter_done")
        path_done = st.sem("path_done")
        path_out = st.sem("path_out")
        R = 8
        block = st.block()

        @block.sync
        def _(sp):
            sp.dma_start(cost[:], costs_dram).then_inc(cost_in, 16)
            sp.wait_ge(path_done, S)
            sp.dma_start(path_dram, path[:]).then_inc(path_out, 16)
            sp.wait_ge(path_out, 16)

        @block.gpsimd
        def _(pool):
            nc.gpsimd.memset(left[:, :, 0:1], 0.0)
            nc.gpsimd.memset(leave[:], 0.0)
            for c in range(S // R):
                rows, up, here = slice(c * R, c * R + R), slice(c * R, c * R + R), slice(c * R + 1, c * R + R + 1)
                pool.wait_ge(row_done, c * R + R)
                nc.gpsimd.tensor_tensor(over[:, 0], table[:, here, 0:S], best[:, rows, :],
                                        ALU.subtract).then_inc(over_done, 1)
                nc.gpsimd.tensor_tensor(over[:, 1], table[:, up, 0:S], table[:, up, 1:W],
                                        ALU.subtract).then_inc(over_done, 1)
                pool.wait_ge(over_done, 2 * c + 2)
                nc.gpsimd.tensor_scalar(left[:, rows, 1:W], over[:, 0, :, ::-1], 0.0, None,
                                        ALU.is_lt).then_inc(left_done, 1)
                nc.gpsimd.tensor_scalar(stay[:], over[:, 0, :, ::-1], 0.0, None, ALU.is_ge).then_inc(stay_done, 1)
                nc.gpsimd.tensor_scalar(diag[:], over[:, 1, :, ::-1], 0.0, None, ALU.is_le).then_inc(diag_done, 1)
                pool.wait_ge(stay_done, c + 1)
                pool.wait_ge(diag_done, c + 1)
                nc.gpsimd.tensor_tensor(go[:, 0, rows, :], stay[:], diag[:], ALU.mult).then_inc(godiag_done, 1)
                pool.wait_ge(godiag_done, c + 1)
                nc.gpsimd.tensor_tensor(go[:, 1, rows, :], stay[:], go[:, 0, rows, :],
                                        ALU.subtract).then_inc(goup_done, 1)

        @block.vector
        def _(dve):
            nc.vector.memset(table[:], BIG).then_inc(border_done, 1)
            dve.wait_ge(border_done, 1)
            nc.vector.memset(table[:, 0, 0:1], 0.0).then_inc(corner_done, 1)
            nc.vector.memset(enter[:, 1:S], 0.0)
            nc.vector.memset(enter[:, 0:1], 1.0).then_inc(corner_done, 1)
            dve.wait_ge(corner_done, 2)
            dve.wait_ge(cost_in, 16)
            flat = table[:].rearrange("b i j -> b (i j)")
            fcost = cost[:].rearrange("b i j -> b (i j)")
            fbest = best[:].rearrange("b i j -> b (i j)")
            for i in range(S):
                row, above, here = i * S, i * W, (i + 1) * W + 1
                if i:
                    dve.wait_ge(row_done, i)
                nc.vector.tensor_tensor(fbest[:, row:row + S], flat[:, above:above + S],
                                        flat[:, above + 1:above + 1 + S], ALU.min).then_inc(best_done, 1)
                dve.wait_ge(best_done, i + 1)
                nc.vector.tensor_tensor_scan(flat[:, here:here + S], fbest[:, row:row + S],
                                             fcost[:, row:row + S], BIG, ALU.min, ALU.add).then_inc(row_done, 1)
            for k in range(S):
                row = S - 1 - k
                if k == 0:
                    dve.wait_ge(goup_done, S // R)
                if k:
                    dve.wait_ge(enter_done, k)
                nc.vector.tensor_tensor_scan(path[:, row, :], left[:, row, 0:S], enter[:],
                                             0.0, ALU.mult, ALU.add).then_inc(path_done, 1)
                dve.wait_ge(path_done, k + 1)
                nc.vector.tensor_tensor(leave[:, :, 1:W], go[:, :, row, :],
                                        path[:, row, :].unsqueeze(1).broadcast_to([B, 2, S]),
                                        ALU.mult).then_inc(leave_done, 1)
                dve.wait_ge(leave_done, k + 1)
                nc.vector.tensor_tensor(enter[:], leave[:, 1, 1:W], leave[:, 0, 0:S], ALU.add).then_inc(enter_done, 1)


def warp_add(nc, core, path_dram):
    with Step(nc, "expand") as st:
        back = st.sb("back", [128, T, S])
        path = st.sb("path", [128, T, S])
        moved = [st.ps(f"moved{i}", [128, 8 // 2, D]) for i in range(8)]
        path_in = st.sem("path_in")
        path_turned = st.sem("path_turned")
        moved_done = st.sem("moved_done")
        block = st.block()

        @block.sync
        def _(sp):
            sp.dma_start(back[:], path_dram.rearrange("(t h) i j -> (h i) t j", h=2)).then_inc(path_in, 16)

        @block.scalar
        def _(act):
            act.wait_ge(path_in, 16)
            nc.scalar.activation(path[:], back[:, :, ::-1], ACT.Copy).then_inc(path_turned, 1)

        @block.tensor
        def _(pe):
            pe.wait_ge(path_turned, 1)
            for t in range(T):
                for h in range(2):
                    half = slice(S * h, S * h + S)
                    nc.tensor.matmul(moved[2 * (t // 4) + h][half, t % 4, :], path[half, t, :],
                                     core.ctx_tok[half, t, :], start=True, stop=True).then_inc(moved_done, 1)

        @block.vector
        def _(dve):
            for q in range(T // 4):
                dve.wait_ge(moved_done, 8 * q + 8)
                for h in range(2):
                    half = slice(S * h, S * h + S)
                    xs = core.x[half, 4 * q:4 * q + 4, :]
                    nc.vector.tensor_tensor(xs, moved[2 * q + h][half], xs, ALU.add)


def bit_ffn(nc, core):
    H, C = 512, 4
    w1T, w2T, conv = core.w1T, core.w2T, core.conv
    with ExitStack() as life:
        core.wholeT = life.enter_context(nc.sbuf_tensor("wholeT", [128, N], BF16))
        core.row_step = life.enter_context(nc.sbuf_tensor("row_step", [128, N], F32))
        with Step(nc, "bitw") as st:
            sums = st.sb("sums", [128, 2])
            core_scale = [core.bit_mean, core.bit_scale]
            scaled = st.sb("scaled", [128, 2, H])
            total = st.ps("total", [128, 2])
            sums_done, total_done = st.sem("sums_done"), st.sem("total_done")
            mean_done, scale_done = st.sem("mean_done"), st.sem("scale_done")
            scaled_done, clipped = st.sem("scaled_done"), st.sem("clipped")
            peak = st.sb("peak", [128, T])
            per = st.sb("per", [128, T])
            lifted = st.sb("lifted", [128, T, D])
            whole = st.sb("whole", [128, T, D], BF16)
            peak_done, floor_done, per_done = st.sem("peak_done"), st.sem("floor_done"), st.sem("per_done")
            inv_done, lifted_done, whole_done = st.sem("inv_done"), st.sem("lifted_done"), st.sem("whole_done")
            turned = [st.ps(f"turned{i}", [128, 512], BF16) for i in range(2)]
            turned_done, taken = st.sem("turned_done"), st.sem("taken")
            diag = st.sb("diag", [128, T, 128])
            diag_done, spread_done = st.sem("diag_done"), st.sem("spread_done")
            spread = [st.ps(f"spread{i}", [128, 512]) for i in range(4)]
            block = st.block()

            @block.vector
            def _(dve):
                dve.wait_ge(core.loaded["w1T"], 16)
                nc.vector.tensor_reduce(sums[:, 0:1], w1T[:], AX.X, ALU.add, apply_absolute_value=True)
                dve.wait_ge(core.loaded["w2T"], 16)
                nc.vector.tensor_reduce(sums[:, 1:2], w2T[:].rearrange("p c d -> p (c d)"), AX.X, ALU.add,
                                        apply_absolute_value=True).then_inc(sums_done, 1)
                dve.wait_ge(total_done, 1)
                nc.vector.tensor_scalar(core.bit_mean[:], total[:], 1.0 / (H * D), EPS, ALU.mult, ALU.max).then_inc(mean_done, 1)
                dve.wait_ge(mean_done, 1)
                nc.vector.reciprocal(core.bit_scale[:], core.bit_mean[:]).then_inc(scale_done, 1)
                dve.wait_ge(scale_done, 1)
                for n, w in enumerate((w1T[:], w2T[:].rearrange("p c d -> p (c d)"))):
                    nc.vector.tensor_scalar(scaled[:, n, :], w, core.bit_scale[:, n:n + 1], ROUND, ALU.mult,
                                            ALU.add).then_inc(scaled_done, 1)
                dve.wait_ge(scaled_done, 2)
                nc.vector.tensor_scalar(scaled[:], scaled[:], ROUND, 1.0, ALU.subtract, ALU.min).then_inc(clipped, 1)
                dve.wait_ge(clipped, 1)
                nc.vector.tensor_scalar_max(core.bit_w[:], scaled[:], -1.0)
                nc.vector.tensor_reduce(peak[:], core.xn[:], AX.X, ALU.max, apply_absolute_value=True).then_inc(peak_done, 1)
                dve.wait_ge(peak_done, 1)
                nc.vector.tensor_scalar_max(peak[:], peak[:], EPS).then_inc(floor_done, 1)
                dve.wait_ge(floor_done, 1)
                nc.vector.reciprocal(per[:], peak[:]).then_inc(inv_done, 1)
                dve.wait_ge(inv_done, 1)
                nc.vector.tensor_scalar_mul(per[:], per[:], 127.0).then_inc(per_done, 1)
                dve.wait_ge(per_done, 1)
                for t in range(T):
                    nc.vector.tensor_scalar(lifted[:, t, :], core.xn[:, t, :], per[:, t:t + 1], ROUND, ALU.mult,
                                            ALU.add).then_inc(lifted_done, 1)
                nc.vector.tensor_scalar(peak[:], peak[:], 1.0 / 127.0, core.bit_mean[:, 0:1], ALU.mult,
                                        ALU.mult).then_inc(lifted_done, 1)
                dve.wait_ge(lifted_done, T + 1)
                nc.vector.tensor_scalar_sub(whole[:], lifted[:], ROUND).then_inc(whole_done, 1)
                for t in range(T):
                    nc.vector.tensor_scalar_mul(diag[:, t, :], core.ident[:], peak[:, t:t + 1]).then_inc(diag_done, 1)
                for g in range(G):
                    dve.wait_ge(spread_done, g + 1)
                    nc.vector.tensor_copy(core.row_step[:, 512 * g:512 * g + 512], spread[g][:])

            @block.tensor
            def _(pe):
                pe.wait_ge(sums_done, 1)
                nc.tensor.matmul(total[:], core.ones[:], sums[:], start=True, stop=True).then_inc(total_done, 1)
                pe.wait_ge(whole_done, 1)
                for t in range(T):
                    g = t // 4
                    if t % 4 == 0 and g >= 2:
                        pe.wait_ge(taken, g - 1)
                    last = nc.tensor.transpose(turned[g % 2][:, 128 * (t % 4):128 * (t % 4) + 128], whole[:, t, :],
                                               core.ident16[:])
                    if t % 4 == 3:
                        last.then_inc(turned_done, 1)
                pe.wait_ge(diag_done, T)
                for g in range(G):
                    nc.tensor.matmul(spread[g][:], core.ones[:], diag[:, 4 * g:4 * g + 4, :], start=True,
                                     stop=True).then_inc(spread_done, 1)

            @block.scalar
            def _(act):
                for g in range(G):
                    act.wait_ge(turned_done, g + 1)
                    nc.scalar.activation(core.wholeT[:, 512 * g:512 * g + 512], turned[g % 2][:], ACT.Copy).then_inc(taken, 1)

        NB = 8
        with Step(nc, "bit") as st:
            up = [st.ps(f"up{i}", [128, 512]) for i in range(2)]
            h = st.sb("h", [128, 2, NB, S])
            mid = st.sb("mid", [128, 2, NB, S])
            act_out = st.sb("act_out", [128, C, 512])
            tok = [st.ps(f"tok{i}", [128, H]) for i in range(2)]
            peak = st.sb("peak", [128, 2])
            per = st.sb("per", [128, 2])
            lifted = st.sb("lifted", [128, H])
            whole = st.sb("whole", [128, 2, H], BF16)
            wholeT_ps = [st.ps(f"wholeT{i}", [128, H], BF16) for i in range(2)]
            wholeT = st.sb("wholeT", [128, 2, H], BF16)
            down = [st.ps(f"down{i}", [128, D]) for i in range(2)]
            up_done, h_done, mid_done = st.sem("up_done"), st.sem("h_done"), st.sem("mid_done")
            before_done, conv_done, silu_done = st.sem("before_done"), st.sem("conv_done"), st.sem("silu_done")
            tok_done, peak_done, floor_done = st.sem("tok_done"), st.sem("peak_done"), st.sem("floor_done")
            inv_done, per_done, lifted_done = st.sem("inv_done"), st.sem("per_done"), st.sem("lifted_done")
            whole_done, turned_done, taken = st.sem("whole_done"), st.sem("turned_done"), st.sem("taken")
            down_done, added = st.sem("down_done"), st.sem("added")
            block = st.block()

            def add_tile(dve, t):
                b = t % 2
                dve.wait_ge(down_done, t + 1)
                nc.vector.scalar_tensor_tensor(core.x[:, t, :], down[b][:], peak[:, b:b + 1], core.x[:, t, :],
                                               ALU.mult, ALU.add).then_inc(added, 1)

            @block.tensor
            def _(pe):
                def raise_chunk(i):
                    g, c = divmod(i, C)
                    if i >= 2:
                        pe.wait_ge(h_done, i - 1)
                    nc.tensor.matmul(up[i % 2][:], core.bit_w[:, 0, 128 * c:128 * c + 128],
                                     core.wholeT[:, 512 * g:512 * g + 512], start=True, stop=True).then_inc(up_done, 1)

                def turn_tile(t):
                    g, k = divmod(t, 4)
                    pe.wait_ge(silu_done, C * g + C)
                    if t >= 2:
                        pe.wait_ge(lifted_done, t - 1)
                    for c in range(C):
                        last = nc.tensor.transpose(tok[t % 2][:, 128 * c:128 * c + 128],
                                                   act_out[:, c, 128 * k:128 * k + 128], core.ident[:])
                    last.then_inc(tok_done, 1)

                def finish_tile(t):
                    pe.wait_ge(whole_done, t + 1)
                    if t >= 2:
                        pe.wait_ge(taken, t - 1)
                    for c in range(C):
                        last = nc.tensor.transpose(wholeT_ps[t % 2][:, 128 * c:128 * c + 128],
                                                   whole[:, t % 2, 128 * c:128 * c + 128], core.ident16[:])
                    last.then_inc(turned_done, 1)
                    pe.wait_ge(taken, t + 1)
                    if t >= 2:
                        pe.wait_ge(added, t - 1)
                    for c in range(C):
                        last = nc.tensor.matmul(down[t % 2][:], wholeT[:, t % 2, 128 * c:128 * c + 128],
                                                core.bit_w[:, 1, 128 * c:128 * c + 128], start=(c == 0), stop=(c == C - 1))
                    last.then_inc(down_done, 1)

                for g in range(G):
                    for c in range(C):
                        raise_chunk(C * g + c)
                    for k in range(4):
                        turn_tile(4 * g + k)
                        if k:
                            finish_tile(4 * g + k - 1)
                    finish_tile(4 * g + 3)

            @block.vector
            def _(dve):
                dve.wait_ge(core.loaded["conv"], 16)
                for g in range(G):
                    for c in range(C):
                        i = C * g + c
                        b = i % 2
                        dve.wait_ge(up_done, i + 1)
                        nc.vector.tensor_tensor(h[:, b].rearrange("p b s -> p (b s)"), up[b][:],
                                                core.row_step[:, 512 * g:512 * g + 512], ALU.mult).then_inc(h_done, 1)
                        dve.wait_ge(h_done, i + 1)
                        dve.wait_ge(mid_done, i + 1)
                        nc.vector.scalar_tensor_tensor(mid[:, b, :, 1:S], h[:, b, :, 0:S - 1], conv[:, c, 0:1],
                                                       mid[:, b, :, 1:S], ALU.mult, ALU.add).then_inc(before_done, 1)
                        dve.wait_ge(before_done, i + 1)
                        nc.vector.scalar_tensor_tensor(mid[:, b, :, 0:S - 1], h[:, b, :, 1:S], conv[:, c, 2:3],
                                                       mid[:, b, :, 0:S - 1], ALU.mult, ALU.add).then_inc(conv_done, 1)
                    for k in range(4):
                        t = 4 * g + k
                        b = t % 2
                        dve.wait_ge(tok_done, t + 1)
                        if t >= 2:
                            dve.wait_ge(added, t - 1)
                        nc.vector.tensor_reduce(peak[:, b:b + 1], tok[b][:], AX.X, ALU.max,
                                                apply_absolute_value=True).then_inc(peak_done, 1)
                        dve.wait_ge(peak_done, t + 1)
                        nc.vector.tensor_scalar_max(peak[:, b:b + 1], peak[:, b:b + 1], EPS).then_inc(floor_done, 1)
                        dve.wait_ge(floor_done, t + 1)
                        nc.vector.reciprocal(per[:, b:b + 1], peak[:, b:b + 1]).then_inc(inv_done, 1)
                        dve.wait_ge(inv_done, t + 1)
                        nc.vector.tensor_scalar_mul(per[:, b:b + 1], per[:, b:b + 1], 127.0).then_inc(per_done, 1)
                        nc.vector.tensor_scalar(peak[:, b:b + 1], peak[:, b:b + 1], 1.0 / 127.0,
                                                core.bit_mean[:, 1:2], ALU.mult, ALU.mult).then_inc(per_done, 1)
                        dve.wait_ge(per_done, 2 * t + 2)
                        nc.vector.tensor_scalar(lifted[:], tok[b][:], per[:, b:b + 1], ROUND, ALU.mult,
                                                ALU.add).then_inc(lifted_done, 1)
                        dve.wait_ge(lifted_done, t + 1)
                        if t >= 2:
                            dve.wait_ge(turned_done, t - 1)
                        nc.vector.tensor_scalar_sub(whole[:, b, :], lifted[:], ROUND).then_inc(whole_done, 1)
                        if k:
                            add_tile(dve, t - 1)
                    add_tile(dve, 4 * g + 3)

            @block.scalar
            def _(act):
                act.wait_ge(core.loaded["conv"], 16)
                for g in range(G):
                    for c in range(C):
                        i = C * g + c
                        b = i % 2
                        act.wait_ge(h_done, i + 1)
                        nc.scalar.activation(mid[:, b], h[:, b], ACT.Identity, bias=conv[:, c, 3:4],
                                             scale=conv[:, c, 1:2]).then_inc(mid_done, 1)
                        act.wait_ge(conv_done, i + 1)
                        if g:
                            act.wait_ge(tok_done, 4 * g)
                        nc.scalar.activation(act_out[:, c, :], mid[:, b].rearrange("p b s -> p (b s)"),
                                             ACT.Silu).then_inc(silu_done, 1)
                    for k in range(4):
                        t = 4 * g + k
                        act.wait_ge(turned_done, t + 1)
                        if t >= 2:
                            act.wait_ge(down_done, t - 1)
                        nc.scalar.activation(wholeT[:, t % 2, :], wholeT_ps[t % 2][:], ACT.Copy).then_inc(taken, 1)


def l1_attention(nc, core):
    H, DK, Q = 8, 16, 4
    SCALE = DK ** -0.5
    V1 = DK + 1
    wk, wq, wv, wu, bu = core.l1["Wk"], core.l1["Wq"], core.l1["Wv"], core.l1["Wu"], core.l1["bu"]
    with ExitStack() as life:
        asked = life.enter_context(nc.sbuf_tensor("l1_asked", [128, G, H, 2, DK, Q], F32))
        keys = life.enter_context(nc.sbuf_tensor("l1_keys", [128, G, 2, Q, D], F32))
        values = life.enter_context(nc.sbuf_tensor("l1_values", [128, B, Q, 2, V1], F32))
        with Step(nc, "l1prep") as st:
            keysT = st.sb("keysT", [128, N])
            xq = st.sb("xq", [128, Q, B, DK])
            cq = st.sb("cq", [128, Q, B, DK])
            flat = [st.ps(f"flat{i}", [128, 512]) for i in range(2)]
            moved = [st.ps(f"moved{i}", [128, B, DK]) for i in range(2)]
            part = [st.ps(f"part{i}", [128, Q, D]) for i in range(4)]
            flat_done, keysT_done = st.sem("flat_done"), st.sem("keysT_done")
            moved_done, moved_read, set_done = st.sem("moved_done"), st.sem("moved_read"), st.sem("set_done")
            part_done, q_read, v_read, k_read = st.sem("part_done"), st.sem("q_read"), st.sem("v_read"), st.sem("k_read")
            xq_done, cq_done = st.sem("xq_done"), st.sem("cq_done")
            block = st.block()

            @block.gpsimd
            def _(pool):
                pool.wait_ge(core.loaded["ctxT"], 16)
                nc.gpsimd.tensor_copy(cq[:].rearrange("p q b k -> p b q k"),
                                      core.ctxT[:].rearrange("p (b q k) -> p b q k", q=Q, k=DK)).then_inc(cq_done, 1)
                nc.gpsimd.memset(values[:], 0.0).then_inc(set_done, 1)
                pool.wait_ge(set_done, 1)
                for g in range(2):
                    last = nc.gpsimd.memset(values[64 * g:64 * g + 64, :, :, g, DK:V1], 1.0)
                last.then_inc(set_done, 1)

            @block.tensor
            def _(pe):
                pe.wait_ge(core.loaded["l1"], core.l1["loads"])
                pe.wait_ge(core.loaded["ctxT"], 16)
                for g in range(G):
                    if g >= 2:
                        pe.wait_ge(keysT_done, g - 1)
                    nc.tensor.matmul(flat[g % 2][:], wk[:], core.ctxT[:, 512 * g:512 * g + 512], start=True, stop=True).then_inc(flat_done, 1)
                pe.wait_ge(keysT_done, G)
                kv = keysT[:].rearrange("p (b q k) -> p b q k", q=Q, k=DK)
                for m in range(4):
                    if m >= 2:
                        pe.wait_ge(moved_read, m - 1)
                    for q in range(Q):
                        last = nc.tensor.matmul(moved[m % 2][:], core.spread[:, m, q, :], kv[:, :, q, :], start=(q == 0), stop=(q == Q - 1))
                    last.then_inc(moved_done, 1)
                pe.wait_ge(xq_done, 1)
                pe.wait_ge(cq_done, 1)
                n = 0
                for g in range(G):
                    for src, w in ((xq, wq), (cq, wv), (cq, wk)):
                        if n >= 4:
                            pe.wait_ge((q_read, v_read, k_read)[(n - 4) % 3], (n - 4) // 3 + 1)
                        for q in range(Q):
                            last = nc.tensor.matmul(part[n % 4][:, q, :], src[:, q, 8 * g:8 * g + 8, :], w[:], start=True, stop=True)
                        last.then_inc(part_done, 1)
                        n += 1

            def by_head(bank):
                return bank[:].rearrange("p q (h d) -> p h d q", h=H)

            @block.scalar
            def _(act):
                nc.scalar.activation(xq[:].rearrange("p q b k -> p b q k"),
                                     core.xnT[:].rearrange("p (b q k) -> p b q k", q=Q, k=DK), ACT.Copy).then_inc(xq_done, 1)
                for g in range(G):
                    act.wait_ge(flat_done, g + 1)
                    nc.scalar.activation(keysT[:, 512 * g:512 * g + 512], flat[g % 2][:], ACT.Copy).then_inc(keysT_done, 1)
                act.wait_ge(set_done, 2)
                for m in range(4):
                    act.wait_ge(moved_done, m + 1)
                    for g in range(2):
                        rows = slice(64 * g, 64 * g + 64)
                        last = nc.scalar.activation(values[rows, :, m, g, 0:DK], moved[m % 2][rows], ACT.Copy)
                    last.then_inc(moved_read, 1)
                for g in range(G):
                    act.wait_ge(part_done, 3 * g + 1)
                    nc.scalar.activation(asked[:, g, :, 0], by_head(part[(3 * g) % 4]), ACT.Copy).then_inc(q_read, 1)
                    act.wait_ge(part_done, 3 * g + 2)
                    nc.scalar.activation(asked[:, g, :, 1], by_head(part[(3 * g + 1) % 4]), ACT.Copy).then_inc(v_read, 1)

            @block.vector
            def _(dve):
                dve.wait_ge(core.loaded["l1"], core.l1["loads"])
                for g in range(G):
                    dve.wait_ge(part_done, 3 * g + 3)
                    for r in range(2):
                        last = nc.vector.tensor_scalar_mul(keys[:, g, r], part[(3 * g + 2) % 4][:], core.parity[:, r:r + 1])
                    last.then_inc(k_read, 1)

        with Step(nc, "l1") as st:
            top = [st.sb(f"top{p}", [128, 2 * H]) for p in range(2)]
            shifted = [st.sb(f"shifted{p}", [128, 2 * H, S]) for p in range(2)]
            prob = [st.sb(f"prob{p}", [128, 2 * H, S]) for p in range(2)]
            probT = [st.sb(f"probT{p}", [128, 8, 128]) for p in range(2)]
            inv = [st.sb(f"inv{p}", [128, 2 * H]) for p in range(2)]
            mixed = [st.sb(f"mixed{p}", [128, 2, 128]) for p in range(2)]
            mixedT = [st.sb(f"mixedT{p}", [128, 2, 2, S]) for p in range(2)]
            score = [st.ps(f"score{p}", [128, 2 * H, S]) for p in range(2)]
            turned = [st.ps(f"turned{j}", [128, 4, 128]) for j in range(2)]
            joint = st.ps("joint", [128, 512])
            pv = st.ps("pv", [128, 8, 2, V1])
            s = {n: st.sem(n) for n in (
                "score_done", "top_done", "shifted_done", "prob_done", "turned_a", "turned_b", "probT_a", "probT_b",
                "pv_done", "inv_done", "mixed_done", "mixed_turned", "mixedT_done", "out_done", "added")}
            block = st.block()

            @block.tensor
            def _(pe):
                def scores(t):
                    p, g, rows = t % 2, t // 4, slice(32 * (t % 4), 32 * (t % 4) + 32)
                    if t >= 2:
                        pe.wait_ge(s["shifted_done"], t - 1)
                    for j in range(2):
                        for h in range(H):
                            f = slice(DK * h, DK * h + DK)
                            last = nc.tensor.matmul(score[p][:, H * j + h, :],
                                                    asked[rows, g, h].rearrange("p a d q -> p (a d q)"),
                                                    keys[rows, g, j, :, f].rearrange("p q d -> p d q"), start=True, stop=True)
                    last.then_inc(s["score_done"], 1)

                def turn(t):
                    pe.wait_ge(s["prob_done"], t + 1)
                    for j, n in enumerate("ab"):
                        if t:
                            pe.wait_ge(s["probT_" + n], t)
                        for i in range(4):
                            m = 4 * j + i
                            last = nc.tensor.transpose(turned[j][:, i, :], prob[t % 2][:, 2 * m:2 * m + 2, :], core.ident[:])
                        last.then_inc(s["turned_" + n], 1)

                def mix(t):
                    pe.wait_ge(s["probT_a"], t + 1)
                    pe.wait_ge(s["probT_b"], t + 1)
                    if t:
                        pe.wait_ge(s["mixed_done"], t)
                    for m in range(8):
                        last = nc.tensor.matmul(pv[:, m], probT[t % 2][:, m, :], values[:, 2 * t + m // 4, m % 4], start=True, stop=True)
                    last.then_inc(s["pv_done"], 1)

                def turn_mixed(t):
                    pe.wait_ge(s["mixed_done"], t + 1)
                    if t:
                        pe.wait_ge(s["added"], t)
                    for j in range(2):
                        last = nc.tensor.transpose(joint[:, 128 * j:128 * j + 128], mixed[t % 2][:, j, :], core.ident[:])
                    last.then_inc(s["mixed_turned"], 1)

                def output(t):
                    pe.wait_ge(s["mixedT_done"], t + 1)
                    for j in range(2):
                        o = joint[64 * j:64 * j + 64, 256:384]
                        for c in range(2):
                            nc.tensor.matmul(o, mixedT[t % 2][:, j, c, :], wu[:], start=(c == 0), stop=False)
                        last = nc.tensor.matmul(o, core.ones[0:1, 0:S], bu[:], start=False, stop=True)
                    last.then_inc(s["out_done"], 1)

                scores(0)
                for t in range(T):
                    if t:
                        turn_mixed(t - 1)
                    if t + 1 < T:
                        scores(t + 1)
                    turn(t)
                    if t:
                        output(t - 1)
                    mix(t)
                turn_mixed(T - 1)
                output(T - 1)

            @block.scalar
            def _(act):
                def copy_mixed(t):
                    act.wait_ge(s["mixed_turned"], t + 1)
                    nc.scalar.activation(mixedT[t % 2][:].rearrange("p j c s -> p (j c s)"), joint[:, 0:256], ACT.Copy).then_inc(s["mixedT_done"], 1)

                for t in range(T):
                    p = t % 2
                    act.wait_ge(s["shifted_done"], t + 1)
                    if t >= 2:
                        act.wait_ge(s["turned_b"], t - 1)
                    nc.scalar.activation(prob[p][:], shifted[p][:], ACT.Exp, scale=SCALE).then_inc(s["prob_done"], 1)
                    if t:
                        copy_mixed(t - 1)
                    act.wait_ge(s["turned_a"], t + 1)
                    if t >= 2:
                        act.wait_ge(s["pv_done"], t - 1)
                    nc.scalar.activation(probT[p][:, 0:4, :], turned[0][:], ACT.Copy).then_inc(s["probT_a"], 1)
                copy_mixed(T - 1)

            @block.vector
            def _(dve):
                def add(t):
                    dve.wait_ge(s["out_done"], t + 1)
                    nc.vector.tensor_tensor(core.x[:, t, :], joint[:, 256:384], core.x[:, t, :], ALU.add).then_inc(s["added"], 1)

                for t in range(T):
                    p = t % 2
                    dve.wait_ge(s["score_done"], t + 1)
                    nc.vector.tensor_reduce(top[p][:], score[p][:], AX.X, ALU.max).then_inc(s["top_done"], 1)
                    dve.wait_ge(s["top_done"], t + 1)
                    if t >= 2:
                        dve.wait_ge(s["prob_done"], t - 1)
                    nc.vector.tensor_tensor(shifted[p][:], score[p][:], top[p][:].unsqueeze(2).broadcast_to([128, 2 * H, S]),
                                            ALU.subtract).then_inc(s["shifted_done"], 1)
                    dve.wait_ge(s["turned_b"], t + 1)
                    if t >= 2:
                        dve.wait_ge(s["pv_done"], t - 1)
                    nc.vector.tensor_copy(probT[p][:, 4:8, :], turned[1][:]).then_inc(s["probT_b"], 1)
                    if t:
                        add(t - 1)
                    dve.wait_ge(s["pv_done"], t + 1)
                    nc.vector.reciprocal(inv[p][:].rearrange("p (m g) -> p m g", g=2), pv[:, :, :, DK]).then_inc(s["inv_done"], 1)
                    dve.wait_ge(s["inv_done"], t + 1)
                    if t >= 2:
                        dve.wait_ge(s["mixed_turned"], t - 1)
                    nc.vector.scalar_tensor_tensor(mixed[p][:].rearrange("p j (h d) -> p (j h) d", d=DK),
                                                   pv[:].rearrange("p m g v -> p (m g) v")[:, :, 0:DK], 0.5,
                                                   inv[p][:].unsqueeze(2).broadcast_to([128, 2 * H, DK]),
                                                   ALU.mult, ALU.mult).then_inc(s["mixed_done"], 1)
                add(T - 1)


def choose_two(nc, st, dve, act_exp, done, logits, first, weights, E):
    K = T * E
    top = st.sb("top", [128, 2, T])
    equal = st.sb("equal", [128, T, E])
    rank = st.sb("rank", [128, T])
    pick = [st.sb(f"pick{i}", [128, T, E]) for i in range(2)]
    rest = st.sb("rest", [128, T, E])
    step = st.sem("choose_step")
    n = 0
    wide = lambda v: v.unsqueeze(2).broadcast_to([128, T, E])

    for i, src in enumerate((logits, rest)):
        nc.vector.tensor_reduce(top[:, i, :], src[:], AX.X, ALU.max).then_inc(step, 1)
        dve.wait_ge(step, n + 1)
        nc.vector.tensor_tensor(equal[:], src[:], wide(top[:, i, :]), ALU.is_equal).then_inc(step, 1)
        dve.wait_ge(step, n + 2)
        nc.vector.tensor_tensor(equal[:], equal[:], first, ALU.mult).then_inc(step, 1)
        dve.wait_ge(step, n + 3)
        nc.vector.tensor_reduce(rank[:], equal[:], AX.X, ALU.max).then_inc(step, 1)
        dve.wait_ge(step, n + 4)
        nc.vector.tensor_tensor(pick[i][:], equal[:], wide(rank[:]), ALU.is_equal).then_inc(step, 1)
        dve.wait_ge(step, n + 5)
        n += 5
        if i == 0:
            nc.vector.scalar_tensor_tensor(rest[:], pick[0][:], -3e38, src[:], ALU.mult, ALU.add).then_inc(step, 1)
            dve.wait_ge(step, n + 1)
            n += 1
    share = st.sb("share", [128, 4, T])
    nc.vector.tensor_tensor(share[:, 0], top[:, 1], top[:, 0], ALU.subtract).then_inc(act_exp[0], 1)
    dve.wait_ge(act_exp[1], 1)
    nc.vector.tensor_scalar_add(share[:, 2], share[:, 1], 1.0).then_inc(step, 1)
    dve.wait_ge(step, n + 1)
    nc.vector.reciprocal(share[:, 3], share[:, 2]).then_inc(step, 1)
    dve.wait_ge(step, n + 2)
    nc.vector.tensor_tensor(share[:, 2], share[:, 1], share[:, 3], ALU.mult).then_inc(step, 1)
    nc.vector.tensor_tensor(pick[0][:], pick[0][:], wide(share[:, 3]), ALU.mult).then_inc(step, 1)
    dve.wait_ge(step, n + 3)
    nc.vector.tensor_tensor(pick[1][:], pick[1][:], wide(share[:, 2]), ALU.mult).then_inc(step, 1)
    dve.wait_ge(step, n + 5)
    nc.vector.tensor_tensor(weights, pick[0][:], pick[1][:], ALU.add).then_inc(done, 1)
    return share


def moe(nc, core):
    E, F, C = 8, 512, 4
    a = core.a
    with Step(nc, "gate") as st:
        gates_ps = st.ps("gates_ps", [128, T, E])
        gates = st.sb("gates", [128, T, E])
        small = st.sb("small", [1, E])
        gates_done, gates_read = st.sem("gates_done"), st.sem("gates_read")
        gap_done, exp_done, weights_done = st.sem("gap_done"), st.sem("exp_done"), st.sem("weights_done")
        turned_done, weightsT_done = st.sem("turned_done"), st.sem("weightsT_done")
        bias_done, bias_free = st.sem("bias_done"), st.sem("bias_free")
        turned = st.ps("turned", [E, 512])
        weightsT = st.sb("weightsT", [E, N])
        bias = [st.ps(f"bias{i}", [128, 4, D]) for i in range(2)]
        block = st.block()
        share = []

        @block.tensor
        def _(pe):
            pe.wait_ge(core.loaded["gate"], 48)
            for t in range(T):
                nc.tensor.matmul(gates_ps[:, t, :], core.xnT[:, 128 * t:128 * t + 128], core.Wg[:], start=True, stop=False)
                last = nc.tensor.matmul(gates_ps[:, t, :], core.ones[0:1, :], core.bg[:], start=False, stop=True)
            last.then_inc(gates_done, 1)
            pe.wait_ge(weights_done, 1)
            for g in range(G):
                if g:
                    pe.wait_ge(weightsT_done, g)
                for k in range(4):
                    last = nc.tensor.transpose(turned[:, 128 * k:128 * k + 128], core.route[:, 4 * g + k, :], core.ident[:])
                last.then_inc(turned_done, 1)
                pe.wait_ge(weightsT_done, g + 1)
                if g >= 2:
                    pe.wait_ge(bias_free, g - 1)
                for k in range(4):
                    t = 4 * g + k
                    last = nc.tensor.matmul(bias[g % 2][:, k, :], weightsT[:, 128 * t:128 * t + 128], core.b2[:], start=True, stop=True)
                last.then_inc(bias_done, 1)

        @block.vector
        def _(dve):
            dve.wait_ge(gates_done, 1)
            nc.vector.tensor_scalar_mul(gates[:], gates_ps[:], 1.0 / (1.0 + 1e-6)).then_inc(gates_read, 1)
            dve.wait_ge(gates_read, 1)
            dve.wait_ge(core.loaded["first8"], 16)
            first = core.first8[:].unsqueeze(1).broadcast_to([128, T, E])
            share.append(choose_two(nc, st, dve, (gap_done, exp_done), weights_done, gates, first, core.route[:], E))
            for g in range(G):
                dve.wait_ge(bias_done, g + 1)
                nc.vector.tensor_tensor(core.x[:, 4 * g:4 * g + 4, :], bias[g % 2][:], core.x[:, 4 * g:4 * g + 4, :],
                                        ALU.add).then_inc(bias_free, 1)

        @block.scalar
        def _(act):
            act.wait_ge(gap_done, 1)
            nc.scalar.activation(share[0][:, 1], share[0][:, 0], ACT.Exp).then_inc(exp_done, 1)
            for g in range(G):
                act.wait_ge(turned_done, g + 1)
                nc.scalar.activation(weightsT[:, 512 * g:512 * g + 512], turned[:], ACT.Copy).then_inc(weightsT_done, 1)

    with Step(nc, "expert") as st:
        w1 = [st.sb(f"w1_{p}", [128, F]) for p in range(2)]
        w2 = [st.sb(f"w2_{p}", [128, C, D]) for p in range(2)]
        b1 = [st.sb(f"b1_{p}", [128, C]) for p in range(2)]
        up = [st.ps(f"up{i}", [128, 512]) for i in range(4)]
        hidden = [st.sb(f"hidden{i}", [128, C, 512]) for i in range(2)]
        down = [st.ps(f"down{i}", [128, 4, D]) for i in range(2)]
        weights_in = [st.sem(f"weights_in{p}") for p in range(2)]
        up_done, hidden_done = st.sem("up_done"), st.sem("hidden_done")
        down_done, down_free = st.sem("down_done"), st.sem("down_free")
        DOWN0, HIDDEN0, FREE0 = 2 * G, C, 2
        block = st.block()

        @block.sync
        def _(sp):
            sp.sem_inc(down_done, DOWN0)
            with sp.Fori(0, E // 2) as i:
                for p in range(2):
                    e = i * 2 + p
                    sp.wait_ge(down_done, e * G + (DOWN0 - G))
                    sp.dma_start(w1[p][:], a["moe_W1"][bass.ds(e, 1), :, :].rearrange("e p f -> (e p) f")).then_inc(weights_in[p], 16)
                    sp.dma_start(w2[p][:], a["moe_W2"][bass.ds(e, 1), :, :, :].rearrange("e p c d -> (e p) c d")).then_inc(weights_in[p], 16)
                    sp.dma_start(b1[p][:], a["moe_b1"][bass.ds(e, 1), :, :].rearrange("e p c -> (e p) c")).then_inc(weights_in[p], 16)

        @block.tensor
        def _(pe):
            with pe.Fori(0, E // 2) as i:
                for p in range(2):
                    e = i * 2 + p

                    def raise_group(g):
                        for c in range(C):
                            pe.wait_ge(hidden_done, e * (G * C) + (C * g + c + 1))
                            nc.tensor.matmul(up[c][:], w1[p][:, 128 * c:128 * c + 128],
                                             core.xnT[:, 512 * g:512 * g + 512], start=True, stop=True).then_inc(up_done, 1)

                    def lower_group(g):
                        pe.wait_ge(hidden_done, e * (G * C) + (C * g + C + HIDDEN0))
                        pe.wait_ge(down_free, e * G + (g + 1))
                        for k in range(4):
                            for c in range(C):
                                last = nc.tensor.matmul(down[g % 2][:, k, :], hidden[g % 2][:, c, 128 * k:128 * k + 128],
                                                        w2[p][:, c, :], start=(c == 0), stop=(c == C - 1))
                        last.then_inc(down_done, 1)

                    pe.wait_ge(weights_in[p], i * 48 + 48)
                    raise_group(0)
                    for g in range(1, G):
                        raise_group(g)
                        lower_group(g - 1)
                    lower_group(G - 1)

        @block.scalar
        def _(act):
            act.sem_inc(hidden_done, HIDDEN0)
            with act.Fori(0, E // 2) as i:
                for p in range(2):
                    e = i * 2 + p
                    act.wait_ge(weights_in[p], i * 48 + 48)
                    for g in range(G):
                        act.wait_ge(down_done, e * G + (g - 1 + DOWN0))
                        for c in range(C):
                            act.wait_ge(up_done, e * (G * C) + (C * g + c + 1))
                            nc.scalar.activation(hidden[g % 2][:, c, :], up[c][:], ACT.Silu, bias=b1[p][:, c:c + 1]).then_inc(hidden_done, 1)

        @block.vector
        def _(dve):
            dve.sem_inc(down_free, FREE0)
            route = core.route[:].rearrange("p t e -> p (t e)")
            with dve.Fori(0, E // 2) as i:
                for p in range(2):
                    e = i * 2 + p
                    for g in range(G):
                        dve.wait_ge(down_done, e * G + (g + 1 + DOWN0))
                        for k in range(4):
                            t = 4 * g + k
                            last = nc.vector.scalar_tensor_tensor(core.x[:, t, :], down[g % 2][:, k, :],
                                                                  route[:, bass.ds(e + E * t, 1)], core.x[:, t, :],
                                                                  ALU.mult, ALU.add)
                        last.then_inc(down_free, 1)


def tiles_in_pairs(engine, first, last, body):
    assert first == 0 and last == T
    for t in (0, 1):
        body(t, t)
    with engine.Fori(1, T // 2 - 1) as i:
        for p in range(2):
            body(i * 2 + p, p)
    for t in (T - 2, T - 1):
        body(t, t % 2)


def head_attention(nc, core, name, w, masked):
    H, DK = 16, 8
    SCALE = DK ** -0.5
    V1 = DK + 1
    HALF = T - 2
    with Step(nc, name) as st:
        dup = [st.sb(f"dup{p}", [128, 2, 2, S]) for p in range(2)]
        q = [st.sb(f"q{p}", [128, 128]) for p in range(2)]
        k = [st.sb(f"k{p}", [128, 128]) for p in range(2)]
        keys = [st.sb(f"keys{p}", [128, 8, 2, S]) for p in range(2)]
        values = [st.sb(f"values{p}", [128, H // 2, 2, 2, V1]) for p in range(2)]
        top = [st.sb(f"top{p}", [128, H]) for p in range(2)]
        shifted = [st.sb(f"shifted{p}", [128, H, S]) for p in range(2)]
        prob = [st.sb(f"prob{p}", [128, H, S]) for p in range(2)]
        probT = [st.sb(f"probT{p}", [128, H // 2, 128]) for p in range(2)]
        inv = [st.sb(f"inv{p}", [128, H]) for p in range(2)]
        mixed = [st.sb(f"mixed{p}", [128, 128]) for p in range(2)]
        mixedT = [st.sb(f"mixedT{p}", [128, 128]) for p in range(2)]
        score = [st.ps(f"score{p}", [128, H, S]) for p in range(2)]
        turned = [st.ps(f"turned{j}", [128, 4, 128]) for j in range(2)]
        joint = st.ps("joint", [128, 512])
        pv = st.ps("pv", [128, H // 2, 2, 2, V1])
        s = {n: st.sem(n) for n in (
            "values_set", "dup_done", "proj_done", "q_done", "k_done", "values_done", "keys_done", "score_done",
            "top_done", "shifted_done", "prob_done", "turned_a", "turned_b", "probT_a", "probT_b", "pv_done",
            "inv_done", "mixed_done", "mixed_turned", "mixedT_done", "out_done", "added")}
        block = st.block()

        @block.gpsimd
        def _(pool):
            for p in range(2):
                last = nc.gpsimd.memset(values[p][:], 0.0)
            last.then_inc(s["values_set"], 1)
            pool.wait_ge(s["values_set"], 1)
            for p in range(2):
                for g in range(2):
                    last = nc.gpsimd.memset(values[p][64 * g:64 * g + 64, :, :, g, DK:V1], 1.0)
            last.then_inc(s["values_set"], 1)

            def body(t, p):
                pool.wait_ge(s["k_done"], t + 1)
                if not isinstance(t, int) or t >= 2:
                    pool.wait_ge(s["score_done"], t - 1)
                nc.gpsimd.tensor_tensor(keys[p][:].rearrange("p h b s -> p h (b s)"),
                                        k[p][:].unsqueeze(1).broadcast_to([128, 8, 128]),
                                        core.head_of[:].unsqueeze(2).broadcast_to([128, 8, 128]),
                                        ALU.mult).then_inc(s["keys_done"], 1)

            pool.wait_ge(core.loaded["head_of"], 16)
            tiles_in_pairs(pool, 0, T, body)

        @block.tensor
        def _(pe):
            pe.wait_ge(core.loaded[w["name"]], w["loads"])

            def project(t, p):
                tok = bass.ds(t * 128, 128)
                pe.wait_ge(s["dup_done"], t + 1)
                if not (isinstance(t, int) and t < 3):
                    pe.wait_ge(s["added"], t - 2)
                nc.tensor.matmul(joint[:, 0:128], w["Wq"][:], core.xnT[:, tok], start=True, stop=True)
                nc.tensor.matmul(joint[:, 128:256], w["Wk"][:], core.ctxT[:, tok], start=True, stop=True)
                for b in range(2):
                    o = joint[:, 256 + 128 * b:384 + 128 * b]
                    last = nc.tensor.matmul(o, dup[p][:, b].rearrange("p c s -> p (c s)"), w["Wv"][:], start=True, stop=not w["bv"])
                    if w["bv"]:
                        last = nc.tensor.matmul(o, core.ones[0:1, :], w["bv"][:], start=False, stop=True)
                last.then_inc(s["proj_done"], 1)

            def wait_for_scores(t):
                pe.wait_ge(s["keys_done"], t + 1)
                pe.wait_ge(s["q_done"], t + 1)
                if not (isinstance(t, int) and t < 2):
                    pe.wait_ge(s["shifted_done"], t - 1)

            def scores(t, p):
                for r in range(2):
                    rows = slice(64 * r, 64 * r + 64)
                    for b in range(2):
                        last = nc.tensor.matmul(score[p][64 * b:64 * b + 64, 8 * r:8 * r + 8, :], q[p][rows, 64 * b:64 * b + 64],
                                                keys[p][rows, :, b, :], start=True, stop=not masked)
                if masked:
                    for r in range(2):
                        bias = core.mask_bias[:, bass.ds(t * S, S)].unsqueeze(1).broadcast_to([128, 8, S])
                        last = nc.tensor.matmul(score[p][:, 8 * r:8 * r + 8, :], core.ident16[:], bias, start=False, stop=True)
                last.then_inc(s["score_done"], 1)

            def turn(t, p):
                pe.wait_ge(s["prob_done"], t + 1)
                for j in range(2):
                    if not (isinstance(t, int) and t < 1):
                        pe.wait_ge(s["probT_a" if j == 0 else "probT_b"], t)
                    for i in range(4):
                        m = 4 * j + i
                        last = nc.tensor.transpose(turned[j][:, i, :], prob[p][:, 2 * m:2 * m + 2, :], core.ident[:])
                    last.then_inc(s["turned_a" if j == 0 else "turned_b"], 1)

            def mix(t, p):
                pe.wait_ge(s["probT_a"], t + 1)
                pe.wait_ge(s["probT_b"], t + 1)
                if not (isinstance(t, int) and t < 1):
                    pe.wait_ge(s["mixed_done"], t)
                for m in range(H // 2):
                    last = nc.tensor.matmul(pv[:, m], probT[p][:, m, :], values[p][:, m], start=True, stop=True)
                last.then_inc(s["pv_done"], 1)

            def turn_mixed(t, p):
                pe.wait_ge(s["mixed_done"], t + 1)
                n = t + 3 if not isinstance(t, int) else min(t + 3, T)
                pe.wait_ge(s["values_done"], n)
                nc.tensor.transpose(joint[:, 0:128], mixed[p][:], core.ident[:]).then_inc(s["mixed_turned"], 1)

            def output(t, p):
                pe.wait_ge(s["mixedT_done"], t + 1)
                last = nc.tensor.matmul(joint[:, 128:256], mixedT[p][:], w["Wo"][:], start=True, stop=False)
                nc.tensor.matmul(joint[:, 128:256], core.ones[0:1, :], w["bo"][:], start=False, stop=True).then_inc(s["out_done"], 1)

            def body(t, p):
                static = isinstance(t, int)
                if not (static and t + 1 >= T):
                    wait_for_scores(t + 1)
                if not (static and t < 1):
                    turn_mixed(t - 1, 1 - p)
                if not (static and t + 1 >= T):
                    scores(t + 1, 1 - p)
                turn(t, p)
                if not (static and t < 1):
                    output(t - 1, 1 - p)
                mix(t, p)
                if not (static and t + 2 >= T):
                    project(t + 2, p)

            pe.wait_ge(core.loaded["ctxT"], 16)
            project(0, 0)
            pe.wait_ge(s["values_done"], 1)
            project(1, 1)
            wait_for_scores(0)
            scores(0, 0)
            tiles_in_pairs(pe, 0, T, body)
            turn_mixed(T - 1, 1)
            output(T - 1, 1)

        @block.scalar
        def _(act):
            act.wait_ge(s["values_set"], 2)
            act.wait_ge(core.loaded[w["name"]], w["loads"])

            def evacuate(t, p):
                act.wait_ge(s["proj_done"], t + 1)
                if not (isinstance(t, int) and t < 2):
                    act.wait_ge(s["score_done"], t - 1)
                nc.scalar.activation(q[p][:], joint[:, 0:128], ACT.Identity, bias=w["bq"][:, 0:1]).then_inc(s["q_done"], 1)
                if not (isinstance(t, int) and t < 2):
                    act.wait_ge(s["keys_done"], t - 1)
                nc.scalar.activation(k[p][:], joint[:, 128:256], ACT.Identity, bias=w["bk"][:, 0:1]).then_inc(s["k_done"], 1)
                if not (isinstance(t, int) and t < 2):
                    act.wait_ge(s["pv_done"], t - 1)
                for g in range(2):
                    rows = slice(64 * g, 64 * g + 64)
                    src = joint[rows, 256:512].rearrange("p (b m g d) -> p g m b d", b=2, g=2, d=DK)
                    last = nc.scalar.activation(values[p][rows, :, :, g, 0:DK], src[:, g], ACT.Copy)
                last.then_inc(s["values_done"], 1)

            def body(t, p):
                static = isinstance(t, int)
                act.wait_ge(s["shifted_done"], t + 1)
                if not (static and t < 2):
                    act.wait_ge(s["turned_b"], t - 1)
                nc.scalar.activation(prob[p][:], shifted[p][:], ACT.Exp, scale=SCALE).then_inc(s["prob_done"], 1)
                if not (static and t < 1):
                    act.wait_ge(s["mixed_turned"], t)
                    nc.scalar.activation(mixedT[1 - p][:], joint[:, 0:128], ACT.Copy).then_inc(s["mixedT_done"], 1)
                act.wait_ge(s["turned_a"], t + 1)
                if not (static and t < 2):
                    act.wait_ge(s["pv_done"], t - 1)
                nc.scalar.activation(probT[p][:, 0:4, :], turned[0][:], ACT.Copy).then_inc(s["probT_a"], 1)
                if not (static and t + 2 >= T):
                    evacuate(t + 2, p)

            evacuate(0, 0)
            evacuate(1, 1)
            tiles_in_pairs(act, 0, T, body)
            act.wait_ge(s["mixed_turned"], T)
            nc.scalar.activation(mixedT[1][:], joint[:, 0:128], ACT.Copy).then_inc(s["mixedT_done"], 1)

        @block.vector
        def _(dve):
            def duplicate(t, p):
                if not (isinstance(t, int) and t < 2):
                    dve.wait_ge(s["proj_done"], t - 1)
                src = core.ctxT[:, bass.ds(t * 128, 128)].rearrange("p (b s) -> p b s", b=2)
                for c in range(2):
                    last = nc.vector.tensor_scalar_mul(dup[p][:, :, c, :], src, 1.0)
                last.then_inc(s["dup_done"], 1)

            def add(t, p):
                dve.wait_ge(s["out_done"], t + 1)
                xs = core.xflat[:, bass.ds(t * D, D)]
                nc.vector.tensor_tensor(xs, joint[:, 128:256], xs, ALU.add).then_inc(s["added"], 1)

            def body(t, p):
                static = isinstance(t, int)
                dve.wait_ge(s["score_done"], t + 1)
                nc.vector.tensor_reduce(top[p][:], score[p][:], AX.X, ALU.max).then_inc(s["top_done"], 1)
                dve.wait_ge(s["top_done"], t + 1)
                if not (static and t < 2):
                    dve.wait_ge(s["prob_done"], t - 1)
                nc.vector.tensor_tensor(shifted[p][:], score[p][:], top[p][:].unsqueeze(2).broadcast_to([128, H, S]),
                                        ALU.subtract).then_inc(s["shifted_done"], 1)
                if not (static and t + 2 >= T):
                    duplicate(t + 2, p)
                dve.wait_ge(s["turned_b"], t + 1)
                if not (static and t < 2):
                    dve.wait_ge(s["pv_done"], t - 1)
                nc.vector.tensor_copy(probT[p][:, 4:8, :], turned[1][:]).then_inc(s["probT_b"], 1)
                if not (static and t < 1):
                    add(t - 1, 1 - p)
                dve.wait_ge(s["pv_done"], t + 1)
                for b in range(2):
                    rows = slice(64 * b, 64 * b + 64)
                    nc.vector.reciprocal(inv[p][rows, :].rearrange("p (m g) -> p m g", g=2),
                                         pv[rows, :, b, :, DK]).then_inc(s["inv_done"], 1)
                dve.wait_ge(s["inv_done"], t * 2 + 2)
                if not (static and t < 2):
                    dve.wait_ge(s["mixed_turned"], t - 1)
                for b in range(2):
                    rows = slice(64 * b, 64 * b + 64)
                    o = mixed[p][rows, :].rearrange("p (m g d) -> p m g d", g=2, d=DK)
                    r = inv[p][rows, :].rearrange("p (m g) -> p m g", g=2).unsqueeze(3).broadcast_to([64, H // 2, 2, DK])
                    last = nc.vector.tensor_tensor(o, pv[rows, :, b, :, 0:DK], r, ALU.mult)
                last.then_inc(s["mixed_done"], 1)

            dve.wait_ge(core.loaded["ctxT"], 16)
            duplicate(0, 0)
            duplicate(1, 1)
            tiles_in_pairs(dve, 0, T, body)
            add(T - 1, 1)


def l2_attention(nc, core):
    with Step(nc, "mask") as st:
        zero = st.sb("zero", [128, T * S])
        zero_done = st.sem("zero_done")
        block = st.block()

        @block.vector
        def _(dve):
            dve.wait_ge(core.loaded["mask"], 16)
            nc.vector.tensor_copy(zero[:], core.mask[:].rearrange("p t s -> p (t s)")).then_inc(zero_done, 1)
            dve.wait_ge(zero_done, 1)
            nc.vector.tensor_scalar(core.mask_bias[:], zero[:], 0.0, -1e20, ALU.is_equal, ALU.mult)

    head_attention(nc, core, "l2", core.l2, True)


def l3_attention(nc, core):
    head_attention(nc, core, "l3", core.l3, False)


def soft_moe(nc, core):
    a = core.a
    CH, X4 = 16, 4
    top = core.soft_top
    with ExitStack() as life:
        core.soft_down = life.enter_context(nc.sbuf_tensor("soft_down", [128, N], F32))
        with Step(nc, "softpre") as st:
            phi = st.sb("phi", [128, CH, 128])
            waste = st.sb("waste", [128, CH * 128])
            down = st.sb("down", [128, T])
            sums = st.sb("sums", [128, T])
            diag = st.sb("diag", [128, T, 128])
            logit = [st.ps(f"logit{p}", [128, CH * 128]) for p in range(2)]
            phi_in, logit_done, top_done = st.sem("phi_in"), st.sem("logit_done"), st.sem("top_done")
            exp_done, diag_done, spread_done = st.sem("exp_done"), st.sem("diag_done"), st.sem("spread_done")
            block = st.block()

            @block.sync
            def _(sp):
                sp.dma_start(phi[:], a["soft_phi"].rearrange("c d s -> d c s")).then_inc(phi_in, 16)

            @block.tensor
            def _(pe):
                pe.wait_ge(phi_in, 16)
                for t in range(T):
                    if t >= 2:
                        pe.wait_ge(exp_done, t - 1)
                    for g in range(G):
                        last = nc.tensor.matmul(logit[t % 2][:, 512 * g:512 * g + 512], core.xnT[:, 128 * t:128 * t + 128],
                                                phi[:, 4 * g:4 * g + 4, :], start=True, stop=True)
                    last.then_inc(logit_done, 1)
                pe.wait_ge(diag_done, T)
                pe.wait_ge(exp_done, T)
                for g in range(G):
                    last = nc.tensor.matmul(logit[0][:, 512 * g:512 * g + 512], core.ones[:], diag[:, 4 * g:4 * g + 4, :],
                                            start=True, stop=True)
                last.then_inc(spread_done, 1)

            @block.vector
            def _(dve):
                for t in range(T):
                    dve.wait_ge(logit_done, t + 1)
                    nc.vector.tensor_reduce(down[:, t:t + 1], logit[t % 2][:], AX.X, ALU.max, negate=True).then_inc(top_done, 1)
                for t in range(T):
                    dve.wait_ge(top_done, t + 1)
                    nc.vector.tensor_scalar_mul(diag[:, t, :], core.ident[:], down[:, t:t + 1]).then_inc(diag_done, 1)
                dve.wait_ge(exp_done, T)
                nc.vector.reciprocal(top[:], sums[:])
                dve.wait_ge(spread_done, 1)
                nc.vector.tensor_copy(core.soft_down[:], logit[0][:])

            @block.scalar
            def _(act):
                for t in range(T):
                    act.wait_ge(top_done, t + 1)
                    if t:
                        act.wait_ge(exp_done, t)
                    nc.scalar.activation(waste[:], logit[t % 2][:], ACT.Exp, bias=down[:, t:t + 1],
                                         accum_out=sums[:, t:t + 1]).then_inc(exp_done, 1)

        result = life.enter_context(nc.sbuf_tensor("soft_result", [128, N], F32))
        with Step(nc, "soft") as st:
            phi = [st.sb(f"phi{p}", [128, 128]) for p in range(2)]
            W = [st.sb(f"W{p}", [128, X4, D]) for p in range(2)]
            bias = [st.sb(f"bias{p}", [128, X4]) for p in range(2)]
            logit = st.sb("logit", [128, B, S])
            spread = st.sb("spread", [128, B, S])
            share = st.sb("share", [128, B, S])
            peak = st.sb("peak", [128, S])
            total = st.sb("total", [128, S])
            inv = st.sb("inv", [128, S])
            given = st.sb("given", [128, T, 128])
            slots = st.sb("slots", [128, 2, T, 128])
            outsT = st.sb("outsT", [128, 2, T, 128])
            outs = st.sb("outs", [128, 2, T, D])
            comb = [st.sb(f"comb{p}", [128, N]) for p in range(2)]
            acc = st.ps("acc", [128, N])
            ring = [st.ps(f"ring{i}", [128, 512]) for i in range(4)]
            s = {n: st.sem(n) for n in (
                "phi0", "phi1", "W0", "W1", "lt_done", "dt_done", "sl_done", "ot_done", "ou_done", "acc_done",
                "lt_read", "dt_read", "sl_a", "sl_d", "ot_a", "ot_d", "ou_a", "ou_d",
                "peak_done", "sub_done", "exp_done", "total_done", "inv_done", "share_done", "low_done", "comb_done",
                "result_done")}
            block = st.block()

            def later(t, n):
                return not isinstance(t, int) or t >= n

            def not_last(t):
                return not (isinstance(t, int) and t + 1 >= CH)

            @block.sync
            def _(sp):
                def body(c, p):
                    if later(c, 2):
                        sp.wait_ge(s["lt_done"], c * 4 - 4)
                    sp.dma_start(phi[p][:], a["soft_phi"][bass.ds(c, 1), :, :].rearrange("c d s -> (c d) s")).then_inc(s[f"phi{p}"], 16)
                    if later(c, 2):
                        sp.wait_ge(s["ot_a"], c * 4 - 4)
                        sp.wait_ge(s["ot_d"], c * 4 - 4)
                    sp.dma_start(W[p][:], a["soft_W"][bass.ds(c, 1), :, :, :].rearrange("c d n e -> (c d) n e")).then_inc(s[f"W{p}"], 16)
                    sp.dma_start(bias[p][:], a["soft_b"][bass.ds(c, 1), :, :].rearrange("c e n -> (c e) n")).then_inc(s[f"W{p}"], 16)

                tiles_in_pairs(sp, 0, CH, body)

            def loads(c, p, unit):
                return (c // 2 + 1) * unit if isinstance(c, int) else (c - p) * (unit // 2) + unit

            @block.tensor
            def _(pe):
                def logits(c, p):
                    pe.wait_ge(s[f"phi{p}"], loads(c, p, 16))
                    for g in range(G):
                        if later(c, 2):
                            pe.wait_ge(s["ou_a" if g % 2 == 0 else "ou_d"], c * 4 - 8 + 3 + g // 2)
                        elif later(c, 1):
                            pe.wait_ge(s["lt_read"], g + 1)
                        nc.tensor.matmul(ring[g][:], phi[p][:], core.xnT[:, 512 * g:512 * g + 512], start=True,
                                         stop=True).then_inc(s["lt_done"], 1)

                def body(c, p):
                    if not_last(c):
                        logits(c + 1, 1 - p)
                    pe.wait_ge(s["share_done"], c + 1)
                    for g in range(G):
                        if not_last(c):
                            pe.wait_ge(s["lt_read"], c * 4 + 4 + g + 1)
                        else:
                            pe.wait_ge(s["ou_a" if g % 2 == 0 else "ou_d"], c * 4 - 4 + 3 + g // 2)
                        for k in range(4):
                            t = 4 * g + k
                            last = nc.tensor.transpose(ring[g][:, 128 * k:128 * k + 128], share[:, 2 * t:2 * t + 2, :], core.ident[:])
                        last.then_inc(s["dt_done"], 1)
                    for j in range(8):
                        q, r = divmod(j, 2)
                        rows = slice(64 * r, 64 * r + 64)
                        pe.wait_ge(s["dt_read"], c * 4 + max(q, j if j < 4 else 0) + 1)
                        if j >= 4:
                            pe.wait_ge(s["sl_a" if j % 2 == 0 else "sl_d"], c * 4 + (j - 4) // 2 + 1)
                        for k in range(4):
                            t = 4 * q + k
                            last = nc.tensor.matmul(ring[j % 4][:, 128 * k:128 * k + 128], core.xn[rows, t, :],
                                                    given[rows, t, :], start=True, stop=True)
                        last.then_inc(s["sl_done"], 1)
                    pe.wait_ge(s[f"W{p}"], loads(c, p, 32))
                    for j in range(8):
                        h, n = divmod(j, 4)
                        if j < 4:
                            pe.wait_ge(s["sl_a"], c * 4 + 3 + (n // 2 if n % 2 == 0 else 0))
                            pe.wait_ge(s["sl_d"], c * 4 + 3 + (n // 2 if n % 2 == 1 else 0))
                        else:
                            pe.wait_ge(s["sl_a"], c * 4 + 4)
                            pe.wait_ge(s["sl_d"], c * 4 + 4)
                            pe.wait_ge(s["ot_a" if j % 2 == 0 else "ot_d"], c * 4 + (j - 4) // 2 + 1)
                        nc.tensor.matmul(ring[j % 4][:], W[p][:, n, :], slots[:, :, 8 * h:8 * h + 8, 32 * n:32 * n + 32],
                                         start=True, stop=True).then_inc(s["ot_done"], 1)
                    for j in range(8):
                        q, r = divmod(j, 2)
                        pe.wait_ge(s["ot_a"], c * 4 + (3 + j // 2 if j < 4 and j % 2 == 0 else 2 if j < 4 else 4))
                        pe.wait_ge(s["ot_d"], c * 4 + (3 + j // 2 if j < 4 and j % 2 == 1 else 2 if j < 4 else 4))
                        if j >= 4:
                            pe.wait_ge(s["ou_a" if j % 2 == 0 else "ou_d"], c * 4 + (j - 4) // 2 + 1)
                        for k in range(4):
                            t = 4 * q + k
                            last = nc.tensor.transpose(ring[j % 4][:, 128 * k:128 * k + 128], outsT[:, r, t, :], core.ident[:])
                        last.then_inc(s["ou_done"], 1)
                    pe.wait_ge(s["comb_done"], c + 1)
                    first = isinstance(c, int) and c == 0
                    for q in range(4):
                        for r in range(2):
                            pe.wait_ge(s["ou_a" if r == 0 else "ou_d"], c * 4 + q + 1)
                            for k in range(4):
                                t = 4 * q + k
                                b = 2 * t + r
                                last = nc.tensor.matmul(acc[:, S * b:S * b + S], outs[:, r, t, :], comb[p][:, S * b:S * b + S],
                                                        start=first and r == 0 and k == 0, stop=False, skip_group_check=True)
                    last.then_inc(s["acc_done"], 1)

                logits(0, 0)
                tiles_in_pairs(pe, 0, CH, body)

            @block.gpsimd
            def _(pool):
                def lower(c, p):
                    pool.wait_ge(s["lt_read"], c * 4 + 4)
                    if later(c, 2):
                        pool.wait_ge(s["acc_done"], c - 1)
                    nc.gpsimd.tensor_tensor(comb[p][:], logit[:].rearrange("p b s -> p (b s)"), core.soft_down[:],
                                            ALU.add).then_inc(s["low_done"], 1)

                def divide(c):
                    pool.wait_ge(s["inv_done"], c + 1)
                    if later(c, 1):
                        pool.wait_ge(s["dt_done"], c * 4)
                    nc.gpsimd.tensor_tensor(share[:], spread[:], inv[:].unsqueeze(1).broadcast_to([128, B, S]),
                                            ALU.mult).then_inc(s["share_done"], 1)

                lower(0, 0)
                divide(0)

                def body(c, p):
                    if not_last(c):
                        lower(c + 1, 1 - p)
                        divide(c + 1)

                tiles_in_pairs(pool, 0, CH, body)

            @block.scalar
            def _(act):
                def take_logits(c):
                    if later(c, 1):
                        act.wait_ge(s["sub_done"], c)
                        act.wait_ge(s["low_done"], c)
                    for g in range(G):
                        act.wait_ge(s["lt_done"], c * 4 + g + 1)
                        nc.scalar.activation(logit[:, 8 * g:8 * g + 8, :].rearrange("p b s -> p (b s)"), ring[g][:],
                                             ACT.Copy).then_inc(s["lt_read"], 1)

                def exp_comb(c, p):
                    act.wait_ge(s["low_done"], c + 1)
                    nc.scalar.activation(comb[p][:], comb[p][:], ACT.Exp).then_inc(s["comb_done"], 1)

                def exp_spread(c):
                    act.wait_ge(s["sub_done"], c + 1)
                    nc.scalar.activation(spread[:], spread[:], ACT.Exp).then_inc(s["exp_done"], 1)

                def body(c, p):
                    if not_last(c):
                        take_logits(c + 1)
                    if later(c, 1):
                        act.wait_ge(s["ot_done"], c * 8)
                    for j in (0, 2, 4, 6):
                        act.wait_ge(s["sl_done"], c * 8 + j + 1)
                        nc.scalar.activation(slots[:, 0, 2 * j:2 * j + 4, :], ring[j % 4][:], ACT.Copy).then_inc(s["sl_a"], 1)
                    if not_last(c):
                        exp_spread(c + 1)
                    act.wait_ge(s[f"W{p}"], loads(c, p, 32))
                    if later(c, 1):
                        act.wait_ge(s["ou_done"], c * 8)
                    for j in (0, 2, 4, 6):
                        h, n = divmod(j, 4)
                        act.wait_ge(s["ot_done"], c * 8 + j + 1)
                        nc.scalar.activation(outsT[:, :, 8 * h:8 * h + 8, 32 * n:32 * n + 32],
                                             ring[j % 4][:].rearrange("p (r t s) -> p r t s", r=2, s=32),
                                             ACT.Identity, bias=bias[p][:, n:n + 1]).then_inc(s["ot_a"], 1)
                    if later(c, 1):
                        act.wait_ge(s["acc_done"], c)
                    for j in (0, 2, 4, 6):
                        act.wait_ge(s["ou_done"], c * 8 + j + 1)
                        nc.scalar.activation(outs[:, 0, 2 * j:2 * j + 4, :], ring[j % 4][:], ACT.Copy).then_inc(s["ou_a"], 1)
                    if not_last(c):
                        exp_comb(c + 1, 1 - p)

                take_logits(0)
                exp_spread(0)
                exp_comb(0, 0)
                tiles_in_pairs(act, 0, CH, body)

            @block.vector
            def _(dve):
                by_token = lambda v: v[:].rearrange("p b s -> p s b")
                all_batches = lambda v: v[:].unsqueeze(1).broadcast_to([128, B, S])

                def largest(c):
                    dve.wait_ge(s["lt_read"], c * 4 + 4)
                    nc.vector.tensor_reduce(peak[:], by_token(logit), AX.X, ALU.max).then_inc(s["peak_done"], 1)

                def subtract(c):
                    dve.wait_ge(s["peak_done"], c + 1)
                    if later(c, 1):
                        dve.wait_ge(s["share_done"], c)
                    nc.vector.tensor_tensor(spread[:], logit[:], all_batches(peak), ALU.subtract).then_inc(s["sub_done"], 1)

                def sum_up(c):
                    dve.wait_ge(s["exp_done"], c + 1)
                    nc.vector.tensor_reduce(total[:], by_token(spread), AX.X, ALU.add).then_inc(s["total_done"], 1)
                    dve.wait_ge(s["total_done"], c + 1)
                    nc.vector.reciprocal(inv[:], total[:]).then_inc(s["inv_done"], 1)

                def body(c, p):
                    if later(c, 1):
                        dve.wait_ge(s["sl_done"], c * 8)
                    for g in range(G):
                        dve.wait_ge(s["dt_done"], c * 4 + g + 1)
                        nc.vector.tensor_copy(given[:, 4 * g:4 * g + 4, :], ring[g][:]).then_inc(s["dt_read"], 1)
                    if later(c, 1):
                        dve.wait_ge(s["ot_done"], c * 8)
                    if not_last(c):
                        largest(c + 1)
                    for j in (1, 3, 5, 7):
                        if j == 5 and not_last(c):
                            subtract(c + 1)
                        dve.wait_ge(s["sl_done"], c * 8 + j + 1)
                        nc.vector.tensor_copy(slots[:, 1, 2 * j - 2:2 * j + 2, :], ring[j % 4][:]).then_inc(s["sl_d"], 1)
                    dve.wait_ge(s[f"W{p}"], loads(c, p, 32))
                    if later(c, 1):
                        dve.wait_ge(s["ou_done"], c * 8)
                    for j in (1, 3, 5, 7):
                        h, n = divmod(j, 4)
                        if j == 5 and not_last(c):
                            sum_up(c + 1)
                        dve.wait_ge(s["ot_done"], c * 8 + j + 1)
                        nc.vector.tensor_scalar_add(outsT[:, :, 8 * h:8 * h + 8, 32 * n:32 * n + 32],
                                                    ring[j % 4][:].rearrange("p (r t s) -> p r t s", r=2, s=32),
                                                    bias[p][:, n:n + 1]).then_inc(s["ot_d"], 1)
                    if later(c, 1):
                        dve.wait_ge(s["acc_done"], c)
                    for j in (1, 3, 5, 7):
                        dve.wait_ge(s["ou_done"], c * 8 + j + 1)
                        nc.vector.tensor_copy(outs[:, 1, 2 * j - 2:2 * j + 2, :], ring[j % 4][:]).then_inc(s["ou_d"], 1)

                largest(0)
                subtract(0)
                sum_up(0)
                tiles_in_pairs(dve, 0, CH, body)
                dve.wait_ge(s["acc_done"], CH)
                nc.vector.tensor_copy(result[:], acc[:])

        with Step(nc, "softend") as st:
            turned = [st.ps(f"turned{g}", [128, 4, 128]) for g in range(G)]
            turned_done = st.sem("turned_done")
            block = st.block()

            @block.tensor
            def _(pe):
                for t in range(T):
                    last = nc.tensor.transpose(turned[t // 4][:, t % 4, :], result[:, 128 * t:128 * t + 128], core.ident[:])
                    if t % 4 == 3:
                        last.then_inc(turned_done, 1)

            @block.vector
            def _(dve):
                for t in range(T):
                    dve.wait_ge(turned_done, t // 4 + 1)
                    nc.vector.scalar_tensor_tensor(core.x[:, t, :], turned[t // 4][:, t % 4, :], top[:, t:t + 1],
                                                   core.x[:, t, :], ALU.mult, ALU.add)


def code_moe(nc, core):
    E, HID, K = 6, 64, 6
    with Step(nc, "codes") as st:
        z_ps = st.ps("z_ps", [128, T, E])
        code = st.sb("code", [128, T, K])
        both = st.sb("both", [128, T, E, K])
        dot = st.sb("dot", [128, T, E])
        temp = st.sb("temp", [128, 2])
        logits = st.sb("logits", [128, T, E])
        z_done, code_done, step = st.sem("z_done"), st.sem("code_done"), st.sem("step")
        gap_done, exp_done, weights_done = st.sem("gap_done"), st.sem("exp_done"), st.sem("weights_done")
        share = []
        block = st.block()

        @block.tensor
        def _(pe):
            pe.wait_ge(core.loaded["code"], core.code_loads)
            for t in range(T):
                last = nc.tensor.matmul(z_ps[:, t, :], core.xnT[:, 128 * t:128 * t + 128], core.code_w[:], start=True, stop=True)
            last.then_inc(z_done, 1)

        @block.vector
        def _(dve):
            dve.wait_ge(core.loaded["code"], core.code_loads)
            nc.vector.tensor_scalar_max(temp[:, 0:1], core.code_temp[:], 0.1).then_inc(step, 1)
            dve.wait_ge(step, 1)
            nc.vector.reciprocal(temp[:, 1:2], temp[:, 0:1]).then_inc(step, 1)
            dve.wait_ge(code_done, 1)
            for e in range(E):
                last = nc.vector.tensor_tensor(both[:, :, e, :], code[:],
                                               core.anchors[:, e, :].unsqueeze(1).broadcast_to([128, T, K]), ALU.mult)
            last.then_inc(step, 1)
            dve.wait_ge(step, 3)
            nc.vector.tensor_reduce(dot[:], both[:], AX.X, ALU.add).then_inc(step, 1)
            dve.wait_ge(step, 4)
            nc.vector.tensor_scalar(logits[:], dot[:], 6.0, 0.5, ALU.subtract, ALU.mult).then_inc(step, 1)
            dve.wait_ge(step, 5)
            nc.vector.tensor_scalar_mul(logits[:], logits[:], temp[:, 1:2]).then_inc(step, 1)
            dve.wait_ge(step, 6)
            first = core.first6[:].unsqueeze(1).broadcast_to([128, T, E])
            share.append(choose_two(nc, st, dve, (gap_done, exp_done), weights_done, logits, first, core.code_route[:], E))

        @block.scalar
        def _(act):
            act.wait_ge(z_done, 1)
            nc.scalar.activation(code[:], z_ps[:], ACT.Tanh, scale=1.0 / 0.3).then_inc(code_done, 1)
            act.wait_ge(gap_done, 1)
            nc.scalar.activation(share[0][:, 1], share[0][:, 0], ACT.Exp).then_inc(exp_done, 1)

    with Step(nc, "codex") as st:
        P = E // 2
        up = [st.ps(f"up{i}", [128, 512]) for i in range(4)]
        hidden = [st.sb(f"hidden{i}", [128, P, 512]) for i in range(2)]
        down = [st.ps(f"down{i}", [128, 4, D]) for i in range(4)]
        up_done, hidden_done, down_done = st.sem("up_done"), st.sem("hidden_done"), st.sem("down_done")
        added = st.sem("added")
        block = st.block()

        @block.tensor
        def _(pe):
            def raise_group(g):
                for c in range(P):
                    n = P * g + c
                    if n >= 4:
                        pe.wait_ge(hidden_done, n - 3)
                    nc.tensor.matmul(up[n % 4][:], core.code_w1[:, 128 * c:128 * c + 128], core.xnT[:, 512 * g:512 * g + 512],
                                     start=True, stop=True).then_inc(up_done, 1)

            raise_group(0)
            for g in range(G):
                if g + 1 < G:
                    raise_group(g + 1)
                for c in range(P):
                    pe.wait_ge(hidden_done, P * g + c + 1)
                    n = P * g + c
                    if n >= 2:
                        pe.wait_ge(added, 2 * n - 2)
                    for k in range(4):
                        for r in range(2):
                            rows = slice(HID * r, HID * r + HID)
                            last = nc.tensor.matmul(down[2 * (n % 2) + r][:, k, :], hidden[g % 2][rows, c, 128 * k:128 * k + 128],
                                                    core.code_w2[rows, c, :], start=True, stop=True)
                    last.then_inc(down_done, 1)

        @block.scalar
        def _(act):
            for g in range(G):
                for c in range(P):
                    n = P * g + c
                    act.wait_ge(up_done, n + 1)
                    if g >= 2:
                        act.wait_ge(down_done, P * (g - 2) + c + 1)
                    nc.scalar.activation(hidden[g % 2][:, c, :], up[n % 4][:], ACT.Gelu_apprx_tanh).then_inc(hidden_done, 1)

        @block.vector
        def _(dve):
            for g in range(G):
                for c in range(P):
                    n = P * g + c
                    dve.wait_ge(down_done, n + 1)
                    for r in range(2):
                        e = 2 * c + r
                        if n or r:
                            dve.wait_ge(added, 2 * n + r)
                        for k in range(4):
                            t = 4 * g + k
                            last = nc.vector.scalar_tensor_tensor(core.x[:, t, :], down[2 * (n % 2) + r][:, k, :],
                                                                  core.code_route[:, t, e:e + 1], core.x[:, t, :],
                                                                  ALU.mult, ALU.add)
                        last.then_inc(added, 1)


def prepare(nc, core, sb, load):
    a = core.a
    if 1 in STAGES:
        core.w1T = sb("w1T", [128, 512])
        core.w2T = sb("w2T", [128, 4, D])
        core.conv = sb("conv", [128, 4, 4])
        core.bit_mean = sb("bit_mean", [128, 2])
        core.bit_scale = sb("bit_scale", [128, 2])
        core.bit_w = sb("bit_w", [128, 2, 512], BF16)
        load("w1T", core.w1T[:], a["bit_w1T"])
        load("w2T", core.w2T[:], a["bit_w2T"])
        load("conv", core.conv[:], a["bit_conv"])
    if 3 in STAGES:
        core.Wg, core.bg, core.b2 = sb("Wg", [128, 8]), sb("bg", [1, 8]), sb("b2", [8, D])
        core.route = sb("route", [128, T, 8])
        core.first8 = sb("first8", [128, 8])
        load("gate", core.Wg[:], a["moe_Wg"])
        load("gate", core.bg[:], a["moe_bg"])
        load("gate", core.b2[:], a["moe_b2"])
        load("first8", core.first8[:], a["first8"])

    for n, key in ((4, "l2"), (6, "l3")):
        if n in STAGES:
            w = {"name": key}
            for part in ("Wq", "Wk", "Wv", "Wo"):
                w[part] = sb(f"{key}_{part}", [128, D])
                load(key, w[part][:], a[f"{key}_{part}"])
            w["bo"] = sb(f"{key}_bo", [1, D])
            load(key, w["bo"][:], a[f"{key}_bo"])
            w["loads"] = 16 * 5
            w["bv"] = None
            if key == "l3":
                w["bv"], w["bq"], w["bk"] = sb("l3_bv", [1, D]), sb("l3_bq", [128, 1]), sb("l3_bk", [128, 1])
                for part in ("bv", "bq", "bk"):
                    load(key, w[part][:], a[f"l3_{part}"])
                w["loads"] += 48
                core.l3 = w
            else:
                w["bq"] = w["bk"] = core.zero
                core.l2 = w
    if 4 in STAGES or 6 in STAGES:
        core.head_of = sb("head_of", [128, 8])
        load("head_of", core.head_of[:], a["head_of"])
    if 4 in STAGES:
        core.mask = sb("mask", [128, T, S], I32)
        core.mask_bias = sb("mask_bias", [128, T * S], BF16)
        load("mask", core.mask[:], a["mask"])
    if 2 in STAGES:
        w = core.l1 = {"loads": 16 * 7}
        for part in ("Wk", "Wq", "Wv", "Wu"):
            w[part] = sb(f"l1_{part}", [128, D])
            load("l1", w[part][:], a[f"l1_{part}"])
        w["bu"] = sb("l1_bu", [1, D])
        core.spread = sb("spread", [128, 4, 4, 128])
        core.parity = sb("parity", [128, 2])
        load("l1", w["bu"][:], a["l1_bu"])
        load("l1", core.spread[:], a["spread"])
        load("l1", core.parity[:], a["parity"])
    if 7 in STAGES:
        core.code_loads = 16 * 6
        core.code_w, core.code_temp = sb("code_w", [128, 6]), sb("code_temp", [128, 1])
        core.code_w1, core.code_w2 = sb("code_w1", [128, 384]), sb("code_w2", [128, 3, D])
        core.anchors, core.first6 = sb("anchors", [128, 6, 6]), sb("first6", [128, 6])
        core.code_route = sb("code_route", [128, T, 6])
        for part in ("w", "temp", "w1", "w2"):
            load("code", {"w": core.code_w, "temp": core.code_temp, "w1": core.code_w1, "w2": core.code_w2}[part][:], a[f"code_{part}"])
        load("code", core.anchors[:], a["code_anchors"])
        load("code", core.first6[:], a["first6"])
    if 5 in STAGES:
        core.soft_top = sb("soft_top", [128, T])


def layout(v):
    import numpy as np

    out = {"x": v["x"], "ctx_1024": v["ctx_1024"]}
    out["ctxT"] = v["ctx_1024"].reshape(N, D).T
    out["ident"] = np.eye(128, dtype=np.float32)
    out["ones"] = np.ones((128, 128), np.float32)
    out["eps"] = np.full((128, 1), EPS, np.float32)
    out["ident16"] = np.eye(128).astype(mybir.dt.np(BF16))
    out["bit_w1T"] = v["L0_ffn_w1"].T
    out["bit_w2T"] = v["L0_ffn_w2"].T.reshape(4, 128, D).transpose(1, 0, 2)
    taps = np.concatenate([v["L0_ffn_conv_w"].reshape(512, 3), v["L0_ffn_conv_b"][:, None]], 1)
    out["bit_conv"] = taps.reshape(4, 128, 4).transpose(1, 0, 2)
    out["moe_Wg"], out["moe_bg"], out["moe_b2"] = v["L1_ffn_Wg"], v["L1_ffn_bg"][None], v["L1_ffn_b2"]
    out["moe_W1"] = v["L1_ffn_W1"]
    out["moe_W2"] = v["L1_ffn_W2"].reshape(8, 4, 128, D).transpose(0, 2, 1, 3)
    out["moe_b1"] = v["L1_ffn_b1"].reshape(8, 4, 128).transpose(0, 2, 1)
    out["first8"] = np.broadcast_to(np.arange(8, 0, -1, dtype=np.float32), (128, 8))
    out["zero"] = np.zeros((128, 1), np.float32)
    for k in "qkv":
        out[f"l2_W{k}"] = v[f"L2_xattn_W{k}"].transpose(1, 0, 2).reshape(D, D)
        out[f"l3_W{k}"] = v[f"L3_xattn_W{k}"]
    out["l2_Wo"], out["l2_bo"] = v["L2_xattn_Wo"].T, v["L2_xattn_bo"][None]
    out["l3_Wo"], out["l3_bo"], out["l3_bv"] = v["L3_xattn_Wo"], v["L3_xattn_bo"][None], v["L3_xattn_bv"][None]
    out["l3_bq"], out["l3_bk"] = v["L3_xattn_bq"][:, None], v["L3_xattn_bk"][:, None]
    out["head_of"] = (np.arange(128)[:, None] // 8 % 8 == np.arange(8)).astype(np.float32)
    out["mask"] = v["mask_Bx1xSxS2_ik0"].reshape(T, 128, S).transpose(1, 0, 2)
    for k in "kqvu":
        out[f"l1_W{k}"] = v[f"L1_xattn_W{k}"].T
    out["l1_bu"] = v["L1_xattn_bu"][None]
    row, col = np.arange(128)[:, None, None, None], np.arange(128)
    pair, quarter = np.arange(4)[:, None, None], np.arange(4)[:, None]
    out["spread"] = ((row // 32 == pair) & (4 * (row % 32) + quarter == col)).astype(np.float32)
    out["parity"] = (np.arange(128)[:, None] // 16 % 2 == np.arange(2)).astype(np.float32)
    out["code_w"] = v["L3_ffn_proj_w"].T
    out["code_temp"] = np.broadcast_to(v["L3_ffn_routing_temp"].reshape(1, 1), (128, 1))
    out["code_w1"] = v["L3_ffn_w1"].transpose(1, 0, 2).reshape(D, 384)
    out["code_w2"] = v["L3_ffn_w2"].reshape(3, 128, D).transpose(1, 0, 2)
    out["code_anchors"] = np.broadcast_to(v["L3_ffn_anchors"], (128, 6, 6))
    out["first6"] = np.broadcast_to(np.arange(6, 0, -1, dtype=np.float32), (128, 6))
    out["soft_phi"] = v["L2_ffn_phi"].reshape(D, 16, 128).transpose(1, 0, 2)
    out["soft_W"] = v["L2_ffn_W"].reshape(16, 4, D, D).transpose(0, 2, 1, 3)
    out["soft_b"] = v["L2_ffn_b"].reshape(16, 4, D).transpose(0, 2, 1)
    return out


def clear_semaphores(nc):
    done = sorted(nc.released_uncleared_semaphores)
    if not done:
        return
    with nc.Block() as block:
        @block.gpsimd
        def _(pool):
            start = done[0]
            for at, sem in enumerate(done):
                if at + 1 == len(done) or done[at + 1] != sem + 1:
                    pool.sem_clear(range(start, sem + 1))
                    start = done[at + 1] if at + 1 < len(done) else 0


def build(nc, a):
    core = Core()
    with ExitStack() as life:
        def sb(name, shape, dt=F32):
            return life.enter_context(nc.sbuf_tensor(name, shape, dt))

        core.x = sb("x_tok", [128, T, D])
        core.xflat = core.x[:].rearrange("p t d -> p (t d)")
        core.xn = sb("xn_tok", [128, T, D])
        core.xnT = sb("xnT", [128, N])
        core.ctxT = sb("ctxT", [128, N])
        core.ident = sb("ident", [128, 128])
        core.ones = sb("ones", [128, 128])
        core.eps = sb("eps", [128, 1])
        core.wait_x = core.wait_consts = True
        core.a = a
        core.loaded = {}
        loads = []

        def load(name, dst, src):
            if name not in core.loaded:
                core.loaded[name] = life.enter_context(nc.semaphore(f"loaded_{name}"))
            loads.append((dst, src, core.loaded[name]))

        load("x", core.x[:], a["x"].rearrange("(t h) s d -> (h s) t d", h=2))
        load("consts", core.ident[:], a["ident"])
        loads.append((core.ones[:], a["ones"], core.loaded["consts"]))
        loads.append((core.eps[:], a["eps"], core.loaded["consts"]))
        core.ident16 = sb("ident16", [128, 128], BF16)
        loads.append((core.ident16[:], a["ident16"], core.loaded["consts"]))
        core.zero = sb("zero", [128, 1])
        loads.append((core.zero[:], a["zero"], core.loaded["consts"]))
        core.consts_count = 80
        load("ctxT", core.ctxT[:], a["ctxT"])
        prepare(nc, core, sb, load)
        with nc.Block() as block:
            @block.sync
            def _(sp):
                for dst, src, sem in loads:
                    sp.dma_start(dst, src).then_inc(sem, 16)

        if 0 in STAGES:
            with nc.sbuf_tensor("ctx_tok", [128, T, D], F32) as ctx_tok, nc.semaphore("loaded_ctx") as ctx_in:
                core.ctx_tok = ctx_tok
                core.loaded["ctx"] = ctx_in
                with nc.Block() as block:
                    @block.sync
                    def _(sp):
                        sp.dma_start(ctx_tok[:], a["ctx_1024"].rearrange("(t h) s d -> (h s) t d", h=2)).then_inc(ctx_in, 16)
                costs = nc.dram_tensor("costs", [B, S, S], F32, kind="Internal").ap()
                path = nc.dram_tensor("path", [B, S, S], F32, kind="Internal").ap()
                layernorm(nc, core, "ln0")
                warp_costs(nc, core, costs)
                warp_path(nc, core, costs, path)
                warp_add(nc, core, path)
        for n, stage in enumerate((bit_ffn, l1_attention, moe, l2_attention, soft_moe, l3_attention, code_moe)):
            if n + 1 in STAGES:
                if n + 1 in (2, 4, 5, 6):
                    clear_semaphores(nc)
                layernorm(nc, core, f"ln{n + 1}")
                stage(nc, core)
        with nc.semaphore("stored") as stored, nc.Block() as block:
            @block.sync
            def _(sp):
                sp.dma_start(a["out"].rearrange("(t h) s d -> (h s) t d", h=2), core.x[:]).then_inc(stored, 16)
                sp.wait_ge(stored, 16)


def kernel(**inputs):
    import numpy as np
    import concourse.bacc as bacc
    from concourse.bass_utils import run_bass_kernel_spmd

    nc = bacc.Bacc("TRN2", target_bir_lowering=False, num_devices=1)
    arrays, a = {}, {}
    laid = layout({k: np.asarray(v) for k, v in inputs.items()})
    for name, v in laid.items():
        v = np.ascontiguousarray(v)
        arrays[f"in_{name}"] = v
        a[name] = nc.dram_tensor(f"in_{name}", v.shape, mybir.dt.from_np(v.dtype), kind="ExternalInput").ap()
    a["out"] = nc.dram_tensor("out_x", (B, S, D), F32, kind="ExternalOutput").ap()
    build(nc, a)
    return run_bass_kernel_spmd(nc, [arrays], core_ids=[0]).results[0]["out_x"]
```

```python
from contextlib import ExitStack

import concourse.bass as bass
from concourse import mybir

STAGES = [0, 1, 2, 3, 4, 5, 6, 7]

F32 = mybir.dt.float32
BF16 = mybir.dt.bfloat16
I32 = mybir.dt.int32
ALU = mybir.AluOpType
ACT = mybir.ActivationFunctionType
AX = mybir.AxisListType

B, S, D = 32, 64, 128
N = B * S
T = N // 128
G = 4
BIG = 1e30
EPS = 1e-5
ROUND = 1.5 * 2.0 ** 23


class Core:
    pass


class Step:

    def __init__(self, nc, name):
        self.nc, self.name, self.ctx = nc, name, ExitStack()

    def __enter__(self):
        return self

    def __exit__(self, *exc):
        self.ctx.close()

    def sb(self, name, shape, dt=F32):
        return self.ctx.enter_context(self.nc.sbuf_tensor(f"{self.name}_{name}", shape, dt))

    def ps(self, name, shape, dt=F32):
        return self.ctx.enter_context(self.nc.psum_tensor(f"{self.name}_{name}", shape, dt))

    def sem(self, name):
        return self.ctx.enter_context(self.nc.semaphore(f"{self.name}_{name}"))

    def block(self):
        return self.ctx.enter_context(self.nc.Block())


def layernorm(nc, core, name):
    x, xn, xnT = core.x, core.xn, core.xnT
    with Step(nc, name) as st:
        stats = st.sb("stats", [128, T, 6])
        meanvar = st.sb("meanvar", [128, T, 2])
        std = st.sb("std", [128, T])
        rstd = st.sb("rstd", [128, T])
        turned = [st.ps(f"turned{i}", [128, 512]) for i in range(G)]
        shift = st.sb("shift", [128, T])
        idle = st.sb("idle", [128, 1])
        stats_done = st.sem("stats_done")
        var_done = st.sem("var_done")
        std_done = st.sem("std_done")
        rstd_done = st.sem("rstd_done")
        shift_done = st.sem("shift_done")
        xn_v, xn_a = st.sem("xn_v"), st.sem("xn_a")
        turned_done = st.sem("turned_done")
        block = st.block()

        @block.vector
        def _(dve):
            def statistics(g):
                for t in range(4 * g, 4 * g + 4):
                    last = nc.vector.bn_stats(stats[:, t, :], x[:, t, :])
                last.then_inc(stats_done, 1)

            def variances(g):
                dve.wait_ge(stats_done, g + 1)
                for t in range(4 * g, 4 * g + 4):
                    last = nc.vector.bn_aggr(meanvar[:, t, :], stats[:, t, :])
                last.then_inc(var_done, 1)

            def normalise(g):
                cols = slice(4 * g, 4 * g + 4)
                dve.wait_ge(std_done, g + 1)
                nc.vector.reciprocal(rstd[:, cols], std[:, cols]).then_inc(rstd_done, 1)
                dve.wait_ge(rstd_done, g + 1)
                nc.vector.scalar_tensor_tensor(shift[:, cols], meanvar[:, cols, 0], -1.0, rstd[:, cols],
                                               ALU.mult, ALU.mult).then_inc(shift_done, 1)
                for t in (4 * g, 4 * g + 1):
                    nc.vector.tensor_scalar(xn[:, t, :], x[:, t, :], meanvar[:, t, 0:1], rstd[:, t:t + 1],
                                            ALU.subtract, ALU.mult).then_inc(xn_v, 1)

            if core.wait_x:
                dve.wait_ge(core.loaded["x"], 16)
            statistics(0)
            for g in range(G):
                if g + 1 < G:
                    statistics(g + 1)
                variances(g)
                if g:
                    normalise(g - 1)
            normalise(G - 1)
            for g in range(G // 2, G):
                dve.wait_ge(turned_done, g + 1)
                nc.vector.tensor_copy(xnT[:, 512 * g:512 * g + 512], turned[g][:])

        @block.scalar
        def _(act):
            if core.wait_consts:
                act.wait_ge(core.loaded["consts"], core.consts_count)
            nc.scalar.activation(idle[:], core.eps[:], ACT.Sqrt)
            for g in range(G):
                act.wait_ge(var_done, g + 1)
                nc.scalar.activation(std[:, 4 * g:4 * g + 4], meanvar[:, 4 * g:4 * g + 4, 1], ACT.Sqrt,
                                     bias=core.eps[:, 0:1]).then_inc(std_done, 1)
                if g:
                    act.wait_ge(shift_done, g)
                    for t in (4 * g - 2, 4 * g - 1):
                        nc.scalar.activation(xn[:, t, :], x[:, t, :], ACT.Identity, scale=rstd[:, t:t + 1],
                                             bias=shift[:, t:t + 1]).then_inc(xn_a, 1)
            act.wait_ge(shift_done, G)
            for t in (T - 2, T - 1):
                nc.scalar.activation(xn[:, t, :], x[:, t, :], ACT.Identity, scale=rstd[:, t:t + 1],
                                     bias=shift[:, t:t + 1]).then_inc(xn_a, 1)
            for g in range(G // 2):
                act.wait_ge(turned_done, g + 1)
                nc.scalar.activation(xnT[:, 512 * g:512 * g + 512], turned[g][:], ACT.Copy)

        @block.tensor
        def _(pe):
            if core.wait_consts:
                pe.wait_ge(core.loaded["consts"], core.consts_count)
            for t in range(T):
                g, k = divmod(t, 4)
                pe.wait_ge(xn_v if k < 2 else xn_a, 2 * g + k % 2 + 1)
                last = nc.tensor.transpose(turned[g][:, 128 * k:128 * k + 128], xn[:, t, :], core.ident[:])
                if k == 3:
                    last.then_inc(turned_done, 1)
    core.wait_x = core.wait_consts = False


def warp_costs(nc, core, costs_dram):
    ctx, ctxT, xnT = core.ctx_tok, core.ctxT, core.xnT
    with Step(nc, "costs") as st:
        xsq = st.sb("xsq", [128, N])
        csq = st.sb("csq", [128, T, D])
        ctx_norm = st.sb("ctx_norm", [128, T])
        norms = st.sb("norms", [128, T, S])
        dist2 = st.sb("dist2", [128, T, S])
        root = st.sb("root", [128, T, S])
        inv = st.sb("inv", [128, T, S])
        cost = st.sb("cost", [128, T, S])
        dots = st.ps("dots", [128, T, S])
        xnorm = st.ps("xnorm", [128, T, S])
        xsq_done = st.sem("xsq_done")
        xnorm_done = st.sem("xnorm_done")
        dots_done = st.sem("dots_done")
        dist2_done = st.sem("dist2_done")
        root_done = st.sem("root_done")
        vector_step = st.sem("vector_step")
        cost_done = st.sem("cost_done")
        cost_out = st.sem("cost_out")
        block = st.block()

        @block.scalar
        def _(act):
            nc.scalar.activation(xsq[:], xnT[:], ACT.Square).then_inc(xsq_done, 1)
            act.wait_ge(dist2_done, 1)
            nc.scalar.activation(root[:], dist2[:], ACT.Sqrt).then_inc(root_done, 1)

        @block.tensor
        def _(pe):
            pe.wait_ge(core.loaded["ctxT"], 16)
            for t in range(T):
                for h in range(2):
                    tok = slice(128 * t + S * h, 128 * t + S * h + S)
                    last = nc.tensor.matmul(dots[S * h:S * h + S, t, :], ctxT[:, tok], xnT[:, tok], start=True, stop=True)
            last.then_inc(dots_done, 1)
            pe.wait_ge(xsq_done, 1)
            sq = xsq[:].rearrange("p (t h j) -> p t h j", h=2, j=S)
            for h in range(2):
                for k in range(2):
                    last = nc.tensor.matmul(xnorm[S * h:S * h + S, 8 * k:8 * k + 8, :], core.ones[:, 0:S],
                                            sq[:, 8 * k:8 * k + 8, h, :], start=True, stop=True)
            last.then_inc(xnorm_done, 1)

        @block.vector
        def _(dve):
            n = 0

            dve.wait_ge(core.loaded["ctx"], 16)
            nc.vector.tensor_tensor(csq[:], ctx[:], ctx[:], ALU.mult).then_inc(vector_step, 1)
            dve.wait_ge(vector_step, 1)
            nc.vector.tensor_reduce(ctx_norm[:], csq[:], AX.X, ALU.add).then_inc(vector_step, 1)
            dve.wait_ge(vector_step, 2)
            dve.wait_ge(xnorm_done, 1)
            nc.vector.tensor_tensor(norms[:], xnorm[:], ctx_norm[:].unsqueeze(2).broadcast_to([128, T, S]),
                                    ALU.add).then_inc(vector_step, 1)
            dve.wait_ge(vector_step, 3)
            dve.wait_ge(dots_done, 1)
            nc.vector.scalar_tensor_tensor(dist2[:], dots[:], -2.0, norms[:], ALU.mult, ALU.add).then_inc(vector_step, 1)
            dve.wait_ge(vector_step, 4)
            nc.vector.tensor_scalar_max(dist2[:], dist2[:], 0.0).then_inc(dist2_done, 1)
            dve.wait_ge(root_done, 1)
            nc.vector.tensor_scalar_max(inv[:], root[:], 1e-30).then_inc(vector_step, 1)
            dve.wait_ge(vector_step, 5)
            nc.vector.reciprocal(cost[:], inv[:]).then_inc(vector_step, 1)
            dve.wait_ge(vector_step, 6)
            nc.vector.tensor_tensor(inv[:], dist2[:], cost[:], ALU.mult).then_inc(vector_step, 1)
            dve.wait_ge(vector_step, 7)
            nc.vector.tensor_tensor(norms[:], inv[:], root[:], ALU.add).then_inc(vector_step, 1)
            dve.wait_ge(vector_step, 8)
            nc.vector.tensor_scalar_mul(cost[:], norms[:], 0.5).then_inc(cost_done, 1)

        @block.sync
        def _(sp):
            sp.wait_ge(cost_done, 1)
            sp.dma_start(costs_dram.rearrange("(t h) i j -> (h i) t j", h=2), cost[:]).then_inc(cost_out, 16)
            sp.wait_ge(cost_out, 16)


def warp_path(nc, core, costs_dram, path_dram):
    W = S + 1
    with Step(nc, "warp") as st:
        cost = st.sb("cost", [B, S, S])
        table = st.sb("table", [B, W, W])
        best = st.sb("best", [B, S, S])
        left = st.sb("left", [B, S, W])
        over = st.sb("over", [B, 2, 8, S])
        stay = st.sb("stay", [B, 8, S])
        diag = st.sb("diag", [B, 8, S])
        go = st.sb("go", [B, 2, S, S])
        path = st.sb("path", [B, S, S])
        leave = st.sb("leave", [B, 2, W])
        enter = st.sb("enter", [B, S])
        cost_in = st.sem("cost_in")
        border_done = st.sem("border_done")
        corner_done = st.sem("corner_done")
        best_done = st.sem("best_done")
        row_done = st.sem("row_done")
        over_done = st.sem("over_done")
        left_done = st.sem("left_done")
        stay_done = st.sem("stay_done")
        diag_done = st.sem("diag_done")
        godiag_done = st.sem("godiag_done")
        goup_done = st.sem("goup_done")
        leave_done = st.sem("leave_done")
        enter_done = st.sem("enter_done")
        path_done = st.sem("path_done")
        path_out = st.sem("path_out")
        R = 8
        block = st.block()

        @block.sync
        def _(sp):
            sp.dma_start(cost[:], costs_dram).then_inc(cost_in, 16)
            sp.wait_ge(path_done, S)
            sp.dma_start(path_dram, path[:]).then_inc(path_out, 16)
            sp.wait_ge(path_out, 16)

        @block.gpsimd
        def _(pool):
            nc.gpsimd.memset(left[:, :, 0:1], 0.0)
            nc.gpsimd.memset(leave[:], 0.0)
            for c in range(S // R):
                rows, up, here = slice(c * R, c * R + R), slice(c * R, c * R + R), slice(c * R + 1, c * R + R + 1)
                pool.wait_ge(row_done, c * R + R)
                nc.gpsimd.tensor_tensor(over[:, 0], table[:, here, 0:S], best[:, rows, :],
                                        ALU.subtract).then_inc(over_done, 1)
                nc.gpsimd.tensor_tensor(over[:, 1], table[:, up, 0:S], table[:, up, 1:W],
                                        ALU.subtract).then_inc(over_done, 1)
                pool.wait_ge(over_done, 2 * c + 2)
                nc.gpsimd.tensor_scalar(left[:, rows, 1:W], over[:, 0, :, ::-1], 0.0, None,
                                        ALU.is_lt).then_inc(left_done, 1)
                nc.gpsimd.tensor_scalar(stay[:], over[:, 0, :, ::-1], 0.0, None, ALU.is_ge).then_inc(stay_done, 1)
                nc.gpsimd.tensor_scalar(diag[:], over[:, 1, :, ::-1], 0.0, None, ALU.is_le).then_inc(diag_done, 1)
                pool.wait_ge(stay_done, c + 1)
                pool.wait_ge(diag_done, c + 1)
                nc.gpsimd.tensor_tensor(go[:, 0, rows, :], stay[:], diag[:], ALU.mult).then_inc(godiag_done, 1)
                pool.wait_ge(godiag_done, c + 1)
                nc.gpsimd.tensor_tensor(go[:, 1, rows, :], stay[:], go[:, 0, rows, :],
                                        ALU.subtract).then_inc(goup_done, 1)

        @block.vector
        def _(dve):
            nc.vector.memset(table[:], BIG).then_inc(border_done, 1)
            dve.wait_ge(border_done, 1)
            nc.vector.memset(table[:, 0, 0:1], 0.0).then_inc(corner_done, 1)
            nc.vector.memset(enter[:, 1:S], 0.0)
            nc.vector.memset(enter[:, 0:1], 1.0).then_inc(corner_done, 1)
            dve.wait_ge(corner_done, 2)
            dve.wait_ge(cost_in, 16)
            flat = table[:].rearrange("b i j -> b (i j)")
            fcost = cost[:].rearrange("b i j -> b (i j)")
            fbest = best[:].rearrange("b i j -> b (i j)")
            for i in range(S):
                row, above, here = i * S, i * W, (i + 1) * W + 1
                if i:
                    dve.wait_ge(row_done, i)
                nc.vector.tensor_tensor(fbest[:, row:row + S], flat[:, above:above + S],
                                        flat[:, above + 1:above + 1 + S], ALU.min).then_inc(best_done, 1)
                dve.wait_ge(best_done, i + 1)
                nc.vector.tensor_tensor_scan(flat[:, here:here + S], fbest[:, row:row + S],
                                             fcost[:, row:row + S], BIG, ALU.min, ALU.add).then_inc(row_done, 1)
            for k in range(S):
                row = S - 1 - k
                if k == 0:
                    dve.wait_ge(goup_done, S // R)
                if k:
                    dve.wait_ge(enter_done, k)
                nc.vector.tensor_tensor_scan(path[:, row, :], left[:, row, 0:S], enter[:],
                                             0.0, ALU.mult, ALU.add).then_inc(path_done, 1)
                dve.wait_ge(path_done, k + 1)
                nc.vector.tensor_tensor(leave[:, :, 1:W], go[:, :, row, :],
                                        path[:, row, :].unsqueeze(1).broadcast_to([B, 2, S]),
                                        ALU.mult).then_inc(leave_done, 1)
                dve.wait_ge(leave_done, k + 1)
                nc.vector.tensor_tensor(enter[:], leave[:, 1, 1:W], leave[:, 0, 0:S], ALU.add).then_inc(enter_done, 1)


def warp_add(nc, core, path_dram):
    with Step(nc, "expand") as st:
        back = st.sb("back", [128, T, S])
        path = st.sb("path", [128, T, S])
        moved = [st.ps(f"moved{i}", [128, 8 // 2, D]) for i in range(8)]
        path_in = st.sem("path_in")
        path_turned = st.sem("path_turned")
        moved_done = st.sem("moved_done")
        block = st.block()

        @block.sync
        def _(sp):
            sp.dma_start(back[:], path_dram.rearrange("(t h) i j -> (h i) t j", h=2)).then_inc(path_in, 16)

        @block.scalar
        def _(act):
            act.wait_ge(path_in, 16)
            nc.scalar.activation(path[:], back[:, :, ::-1], ACT.Copy).then_inc(path_turned, 1)

        @block.tensor
        def _(pe):
            pe.wait_ge(path_turned, 1)
            for t in range(T):
                for h in range(2):
                    half = slice(S * h, S * h + S)
                    nc.tensor.matmul(moved[2 * (t // 4) + h][half, t % 4, :], path[half, t, :],
                                     core.ctx_tok[half, t, :], start=True, stop=True).then_inc(moved_done, 1)

        @block.vector
        def _(dve):
            for q in range(T // 4):
                dve.wait_ge(moved_done, 8 * q + 8)
                for h in range(2):
                    half = slice(S * h, S * h + S)
                    xs = core.x[half, 4 * q:4 * q + 4, :]
                    nc.vector.tensor_tensor(xs, moved[2 * q + h][half], xs, ALU.add)


def bit_ffn(nc, core):
    H, C = 512, 4
    w1T, w2T, conv = core.w1T, core.w2T, core.conv
    with ExitStack() as life:
        core.wholeT = life.enter_context(nc.sbuf_tensor("wholeT", [128, N], BF16))
        core.row_step = life.enter_context(nc.sbuf_tensor("row_step", [128, N], F32))
        with Step(nc, "bitw") as st:
            sums = st.sb("sums", [128, 2])
            core_scale = [core.bit_mean, core.bit_scale]
            scaled = st.sb("scaled", [128, 2, H])
            total = st.ps("total", [128, 2])
            sums_done, total_done = st.sem("sums_done"), st.sem("total_done")
            mean_done, scale_done = st.sem("mean_done"), st.sem("scale_done")
            scaled_done, clipped = st.sem("scaled_done"), st.sem("clipped")
            peak = st.sb("peak", [128, T])
            per = st.sb("per", [128, T])
            lifted = st.sb("lifted", [128, T, D])
            whole = st.sb("whole", [128, T, D], BF16)
            peak_done, floor_done, per_done = st.sem("peak_done"), st.sem("floor_done"), st.sem("per_done")
            inv_done, lifted_done, whole_done = st.sem("inv_done"), st.sem("lifted_done"), st.sem("whole_done")
            turned = [st.ps(f"turned{i}", [128, 512], BF16) for i in range(2)]
            turned_done, taken = st.sem("turned_done"), st.sem("taken")
            diag = st.sb("diag", [128, T, 128])
            diag_done, spread_done = st.sem("diag_done"), st.sem("spread_done")
            spread = [st.ps(f"spread{i}", [128, 512]) for i in range(4)]
            block = st.block()

            @block.vector
            def _(dve):
                dve.wait_ge(core.loaded["w1T"], 16)
                nc.vector.tensor_reduce(sums[:, 0:1], w1T[:], AX.X, ALU.add, apply_absolute_value=True)
                dve.wait_ge(core.loaded["w2T"], 16)
                nc.vector.tensor_reduce(sums[:, 1:2], w2T[:].rearrange("p c d -> p (c d)"), AX.X, ALU.add,
                                        apply_absolute_value=True).then_inc(sums_done, 1)
                dve.wait_ge(total_done, 1)
                nc.vector.tensor_scalar(core.bit_mean[:], total[:], 1.0 / (H * D), EPS, ALU.mult, ALU.max).then_inc(mean_done, 1)
                dve.wait_ge(mean_done, 1)
                nc.vector.reciprocal(core.bit_scale[:], core.bit_mean[:]).then_inc(scale_done, 1)
                dve.wait_ge(scale_done, 1)
                for n, w in enumerate((w1T[:], w2T[:].rearrange("p c d -> p (c d)"))):
                    nc.vector.tensor_scalar(scaled[:, n, :], w, core.bit_scale[:, n:n + 1], ROUND, ALU.mult,
                                            ALU.add).then_inc(scaled_done, 1)
                dve.wait_ge(scaled_done, 2)
                nc.vector.tensor_scalar(scaled[:], scaled[:], ROUND, 1.0, ALU.subtract, ALU.min).then_inc(clipped, 1)
                dve.wait_ge(clipped, 1)
                nc.vector.tensor_scalar_max(core.bit_w[:], scaled[:], -1.0)
                nc.vector.tensor_reduce(peak[:], core.xn[:], AX.X, ALU.max, apply_absolute_value=True).then_inc(peak_done, 1)
                dve.wait_ge(peak_done, 1)
                nc.vector.tensor_scalar_max(peak[:], peak[:], EPS).then_inc(floor_done, 1)
                dve.wait_ge(floor_done, 1)
                nc.vector.reciprocal(per[:], peak[:]).then_inc(inv_done, 1)
                dve.wait_ge(inv_done, 1)
                nc.vector.tensor_scalar_mul(per[:], per[:], 127.0).then_inc(per_done, 1)
                dve.wait_ge(per_done, 1)
                for t in range(T):
                    nc.vector.tensor_scalar(lifted[:, t, :], core.xn[:, t, :], per[:, t:t + 1], ROUND, ALU.mult,
                                            ALU.add).then_inc(lifted_done, 1)
                nc.vector.tensor_scalar(peak[:], peak[:], 1.0 / 127.0, core.bit_mean[:, 0:1], ALU.mult,
                                        ALU.mult).then_inc(lifted_done, 1)
                dve.wait_ge(lifted_done, T + 1)
                nc.vector.tensor_scalar_sub(whole[:], lifted[:], ROUND).then_inc(whole_done, 1)
                for t in range(T):
                    nc.vector.tensor_scalar_mul(diag[:, t, :], core.ident[:], peak[:, t:t + 1]).then_inc(diag_done, 1)
                for g in range(G):
                    dve.wait_ge(spread_done, g + 1)
                    nc.vector.tensor_copy(core.row_step[:, 512 * g:512 * g + 512], spread[g][:])

            @block.tensor
            def _(pe):
                pe.wait_ge(sums_done, 1)
                nc.tensor.matmul(total[:], core.ones[:], sums[:], start=True, stop=True).then_inc(total_done, 1)
                pe.wait_ge(whole_done, 1)
                for t in range(T):
                    g = t // 4
                    if t % 4 == 0 and g >= 2:
                        pe.wait_ge(taken, g - 1)
                    last = nc.tensor.transpose(turned[g % 2][:, 128 * (t % 4):128 * (t % 4) + 128], whole[:, t, :],
                                               core.ident16[:])
                    if t % 4 == 3:
                        last.then_inc(turned_done, 1)
                pe.wait_ge(diag_done, T)
                for g in range(G):
                    nc.tensor.matmul(spread[g][:], core.ones[:], diag[:, 4 * g:4 * g + 4, :], start=True,
                                     stop=True).then_inc(spread_done, 1)

            @block.scalar
            def _(act):
                for g in range(G):
                    act.wait_ge(turned_done, g + 1)
                    nc.scalar.activation(core.wholeT[:, 512 * g:512 * g + 512], turned[g % 2][:], ACT.Copy).then_inc(taken, 1)

        NB = 8
        with Step(nc, "bit") as st:
            up = [st.ps(f"up{i}", [128, 512]) for i in range(2)]
            h = st.sb("h", [128, 2, NB, S])
            mid = st.sb("mid", [128, 2, NB, S])
            act_out = st.sb("act_out", [128, C, 512])
            tok = [st.ps(f"tok{i}", [128, H]) for i in range(2)]
            peak = st.sb("peak", [128, 2])
            per = st.sb("per", [128, 2])
            lifted = st.sb("lifted", [128, H])
            whole = st.sb("whole", [128, 2, H], BF16)
            wholeT_ps = [st.ps(f"wholeT{i}", [128, H], BF16) for i in range(2)]
            wholeT = st.sb("wholeT", [128, 2, H], BF16)
            down = [st.ps(f"down{i}", [128, D]) for i in range(2)]
            up_done, h_done, mid_done = st.sem("up_done"), st.sem("h_done"), st.sem("mid_done")
            before_done, conv_done, silu_done = st.sem("before_done"), st.sem("conv_done"), st.sem("silu_done")
            tok_done, peak_done, floor_done = st.sem("tok_done"), st.sem("peak_done"), st.sem("floor_done")
            inv_done, per_done, lifted_done = st.sem("inv_done"), st.sem("per_done"), st.sem("lifted_done")
            whole_done, turned_done, taken = st.sem("whole_done"), st.sem("turned_done"), st.sem("taken")
            down_done, added = st.sem("down_done"), st.sem("added")
            block = st.block()

            def add_tile(dve, t):
                b = t % 2
                dve.wait_ge(down_done, t + 1)
                nc.vector.scalar_tensor_tensor(core.x[:, t, :], down[b][:], peak[:, b:b + 1], core.x[:, t, :],
                                               ALU.mult, ALU.add).then_inc(added, 1)

            @block.tensor
            def _(pe):
                def raise_chunk(i):
                    g, c = divmod(i, C)
                    if i >= 2:
                        pe.wait_ge(h_done, i - 1)
                    nc.tensor.matmul(up[i % 2][:], core.bit_w[:, 0, 128 * c:128 * c + 128],
                                     core.wholeT[:, 512 * g:512 * g + 512], start=True, stop=True).then_inc(up_done, 1)

                def turn_tile(t):
                    g, k = divmod(t, 4)
                    pe.wait_ge(silu_done, C * g + C)
                    if t >= 2:
                        pe.wait_ge(lifted_done, t - 1)
                    for c in range(C):
                        last = nc.tensor.transpose(tok[t % 2][:, 128 * c:128 * c + 128],
                                                   act_out[:, c, 128 * k:128 * k + 128], core.ident[:])
                    last.then_inc(tok_done, 1)

                def finish_tile(t):
                    pe.wait_ge(whole_done, t + 1)
                    if t >= 2:
                        pe.wait_ge(taken, t - 1)
                    for c in range(C):
                        last = nc.tensor.transpose(wholeT_ps[t % 2][:, 128 * c:128 * c + 128],
                                                   whole[:, t % 2, 128 * c:128 * c + 128], core.ident16[:])
                    last.then_inc(turned_done, 1)
                    pe.wait_ge(taken, t + 1)
                    if t >= 2:
                        pe.wait_ge(added, t - 1)
                    for c in range(C):
                        last = nc.tensor.matmul(down[t % 2][:], wholeT[:, t % 2, 128 * c:128 * c + 128],
                                                core.bit_w[:, 1, 128 * c:128 * c + 128], start=(c == 0), stop=(c == C - 1))
                    last.then_inc(down_done, 1)

                for g in range(G):
                    for c in range(C):
                        raise_chunk(C * g + c)
                    for k in range(4):
                        turn_tile(4 * g + k)
                        if k:
                            finish_tile(4 * g + k - 1)
                    finish_tile(4 * g + 3)

            @block.vector
            def _(dve):
                dve.wait_ge(core.loaded["conv"], 16)
                for g in range(G):
                    for c in range(C):
                        i = C * g + c
                        b = i % 2
                        dve.wait_ge(up_done, i + 1)
                        nc.vector.tensor_tensor(h[:, b].rearrange("p b s -> p (b s)"), up[b][:],
                                                core.row_step[:, 512 * g:512 * g + 512], ALU.mult).then_inc(h_done, 1)
                        dve.wait_ge(h_done, i + 1)
                        dve.wait_ge(mid_done, i + 1)
                        nc.vector.scalar_tensor_tensor(mid[:, b, :, 1:S], h[:, b, :, 0:S - 1], conv[:, c, 0:1],
                                                       mid[:, b, :, 1:S], ALU.mult, ALU.add).then_inc(before_done, 1)
                        dve.wait_ge(before_done, i + 1)
                        nc.vector.scalar_tensor_tensor(mid[:, b, :, 0:S - 1], h[:, b, :, 1:S], conv[:, c, 2:3],
                                                       mid[:, b, :, 0:S - 1], ALU.mult, ALU.add).then_inc(conv_done, 1)
                    for k in range(4):
                        t = 4 * g + k
                        b = t % 2
                        dve.wait_ge(tok_done, t + 1)
                        if t >= 2:
                            dve.wait_ge(added, t - 1)
                        nc.vector.tensor_reduce(peak[:, b:b + 1], tok[b][:], AX.X, ALU.max,
                                                apply_absolute_value=True).then_inc(peak_done, 1)
                        dve.wait_ge(peak_done, t + 1)
                        nc.vector.tensor_scalar_max(peak[:, b:b + 1], peak[:, b:b + 1], EPS).then_inc(floor_done, 1)
                        dve.wait_ge(floor_done, t + 1)
                        nc.vector.reciprocal(per[:, b:b + 1], peak[:, b:b + 1]).then_inc(inv_done, 1)
                        dve.wait_ge(inv_done, t + 1)
                        nc.vector.tensor_scalar_mul(per[:, b:b + 1], per[:, b:b + 1], 127.0).then_inc(per_done, 1)
                        nc.vector.tensor_scalar(peak[:, b:b + 1], peak[:, b:b + 1], 1.0 / 127.0,
                                                core.bit_mean[:, 1:2], ALU.mult, ALU.mult).then_inc(per_done, 1)
                        dve.wait_ge(per_done, 2 * t + 2)
                        nc.vector.tensor_scalar(lifted[:], tok[b][:], per[:, b:b + 1], ROUND, ALU.mult,
                                                ALU.add).then_inc(lifted_done, 1)
                        dve.wait_ge(lifted_done, t + 1)
                        if t >= 2:
                            dve.wait_ge(turned_done, t - 1)
                        nc.vector.tensor_scalar_sub(whole[:, b, :], lifted[:], ROUND).then_inc(whole_done, 1)
                        if k:
                            add_tile(dve, t - 1)
                    add_tile(dve, 4 * g + 3)

            @block.scalar
            def _(act):
                act.wait_ge(core.loaded["conv"], 16)
                for g in range(G):
                    for c in range(C):
                        i = C * g + c
                        b = i % 2
                        act.wait_ge(h_done, i + 1)
                        nc.scalar.activation(mid[:, b], h[:, b], ACT.Identity, bias=conv[:, c, 3:4],
                                             scale=conv[:, c, 1:2]).then_inc(mid_done, 1)
                        act.wait_ge(conv_done, i + 1)
                        if g:
                            act.wait_ge(tok_done, 4 * g)
                        nc.scalar.activation(act_out[:, c, :], mid[:, b].rearrange("p b s -> p (b s)"),
                                             ACT.Silu).then_inc(silu_done, 1)
                    for k in range(4):
                        t = 4 * g + k
                        act.wait_ge(turned_done, t + 1)
                        if t >= 2:
                            act.wait_ge(down_done, t - 1)
                        nc.scalar.activation(wholeT[:, t % 2, :], wholeT_ps[t % 2][:], ACT.Copy).then_inc(taken, 1)


def l1_attention(nc, core):
    H, DK, Q = 8, 16, 4
    SCALE = DK ** -0.5
    V1 = DK + 1
    wk, wq, wv, wu, bu = core.l1["Wk"], core.l1["Wq"], core.l1["Wv"], core.l1["Wu"], core.l1["bu"]
    with ExitStack() as life:
        asked = life.enter_context(nc.sbuf_tensor("l1_asked", [128, G, H, 2, DK, Q], F32))
        keys = life.enter_context(nc.sbuf_tensor("l1_keys", [128, G, 2, Q, D], F32))
        values = life.enter_context(nc.sbuf_tensor("l1_values", [128, B, Q, 2, V1], F32))
        with Step(nc, "l1prep") as st:
            by_head_keys = st.sb("by_head_keys", [128, G, H, DK, Q])
            xq = st.sb("xq", [128, Q, B, DK])
            cq = st.sb("cq", [128, Q, B, DK])
            moved = [st.ps(f"moved{i}", [128, 4, 8, DK]) for i in range(2)]
            part = [st.ps(f"part{i}", [128, Q, D]) for i in range(4)]
            by_head_done = st.sem("by_head_done")
            moved_done, moved_read, set_done = st.sem("moved_done"), st.sem("moved_read"), st.sem("set_done")
            part_done, q_read, v_read, k_read = st.sem("part_done"), st.sem("q_read"), st.sem("v_read"), st.sem("k_read")
            xq_done, cq_done = st.sem("xq_done"), st.sem("cq_done")
            block = st.block()

            @block.gpsimd
            def _(pool):
                nc.gpsimd.memset(values[:], 0.0).then_inc(set_done, 1)
                pool.wait_ge(set_done, 1)
                for g in range(2):
                    last = nc.gpsimd.memset(values[64 * g:64 * g + 64, :, :, g, DK:V1], 1.0)
                last.then_inc(set_done, 1)

            @block.tensor
            def _(pe):
                pe.wait_ge(core.loaded["l1"], core.l1["loads"])
                pe.wait_ge(core.loaded["ctxT"], 16)
                pe.wait_ge(xq_done, 1)
                pe.wait_ge(cq_done, 1)
                n = 0
                for g in range(G):
                    for src, w in ((xq, wq), (cq, wv), (cq, wk)):
                        if n >= 4:
                            pe.wait_ge((q_read, v_read, by_head_done)[(n - 4) % 3], (n - 4) // 3 + 1)
                        for q in range(Q):
                            last = nc.tensor.matmul(part[n % 4][:, q, :], src[:, q, 8 * g:8 * g + 8, :], w[:], start=True, stop=True)
                        last.then_inc(part_done, 1)
                        n += 1
                for g in range(G):
                    pe.wait_ge(by_head_done, g + 1)
                    if g >= 2:
                        pe.wait_ge(moved_read, g - 1)
                    for m in range(4):
                        last = nc.tensor.transpose(moved[g % 2][:, m], by_head_keys[:, g, 2 * m:2 * m + 2], core.ident[:])
                    last.then_inc(moved_done, 1)

            def by_head(bank):
                return bank[:].rearrange("p q (h d) -> p h d q", h=H)

            @block.scalar
            def _(act):
                nc.scalar.activation(xq[:].rearrange("p q b k -> p b q k"),
                                     core.xnT[:].rearrange("p (b q k) -> p b q k", q=Q, k=DK), ACT.Copy).then_inc(xq_done, 1)
                for g in range(G):
                    act.wait_ge(part_done, 3 * g + 1)
                    nc.scalar.activation(asked[:, g, :, 0], by_head(part[(3 * g) % 4]), ACT.Copy).then_inc(q_read, 1)
                    act.wait_ge(part_done, 3 * g + 2)
                    nc.scalar.activation(asked[:, g, :, 1], by_head(part[(3 * g + 1) % 4]), ACT.Copy).then_inc(v_read, 1)
                    act.wait_ge(k_read, g + 1)
                    nc.scalar.activation(by_head_keys[:, g], by_head(part[(3 * g + 2) % 4]), ACT.Copy).then_inc(by_head_done, 1)
                act.wait_ge(set_done, 2)
                for g in range(G):
                    act.wait_ge(moved_done, g + 1)
                    for i in range(2):
                        rows = slice(64 * i, 64 * i + 64)
                        last = nc.scalar.activation(values[rows, 8 * g:8 * g + 8, :, i, 0:DK],
                                                    moved[g % 2][rows].rearrange("p m b k -> p b m k"), ACT.Copy)
                    last.then_inc(moved_read, 1)

            @block.vector
            def _(dve):
                dve.wait_ge(core.loaded["ctxT"], 16)
                nc.vector.tensor_copy(cq[:].rearrange("p q b k -> p b q k"),
                                      core.ctxT[:].rearrange("p (b q k) -> p b q k", q=Q, k=DK)).then_inc(cq_done, 1)
                dve.wait_ge(core.loaded["l1"], core.l1["loads"])
                for g in range(G):
                    dve.wait_ge(part_done, 3 * g + 3)
                    for r in range(2):
                        last = nc.vector.tensor_scalar_mul(keys[:, g, r], part[(3 * g + 2) % 4][:], core.parity[:, r:r + 1])
                    last.then_inc(k_read, 1)

        with Step(nc, "l1") as st:
            top = [st.sb(f"top{p}", [128, H, 2]) for p in range(2)]
            shifted = [st.sb(f"shifted{p}", [128, H, 2, S]) for p in range(2)]
            prob = [st.sb(f"prob{p}", [128, 2 * H, S]) for p in range(2)]
            probT = [st.sb(f"probT{p}", [128, 8, 128]) for p in range(2)]
            inv = [st.sb(f"inv{p}", [128, 2 * H]) for p in range(2)]
            mixed = [st.sb(f"mixed{p}", [128, 2, 128]) for p in range(2)]
            mixedT = [st.sb(f"mixedT{p}", [128, 2, 2, S]) for p in range(2)]
            score = [st.ps(f"score{p}", [128, H, 2, S]) for p in range(2)]
            turned = [st.ps(f"turned{j}", [128, 4, 128]) for j in range(2)]
            joint = st.ps("joint", [128, 512])
            pv = st.ps("pv", [128, 8, 2, V1])
            s = {n: st.sem(n) for n in (
                "score_done", "top_done", "shifted_done", "prob_done", "turned_a", "turned_b", "probT_a", "probT_b",
                "pv_done", "inv_done", "mixed_done", "mixed_turned", "mixedT_done", "out_done", "added")}
            block = st.block()
            there = lambda t: 0 <= t < T

            @block.tensor
            def _(pe):
                def scores(t, half):
                    p, g, rows = t % 2, t // 4, slice(32 * (t % 4), 32 * (t % 4) + 32)
                    if t >= 2 and half == 0:
                        pe.wait_ge(s["shifted_done"], t - 1)
                    for h in range(4 * half, 4 * half + 4):
                        f = slice(DK * h, DK * h + DK)
                        last = nc.tensor.matmul(score[p][:, h, :, :], asked[rows, g, h].rearrange("p a d q -> p (a d q)"),
                                                keys[rows, g, :, :, f].rearrange("p j q d -> p j d q"), start=True, stop=True)
                    if half == 1:
                        last.then_inc(s["score_done"], 1)

                def turn(t, j):
                    pe.wait_ge(s["prob_done"], t + 1)
                    if t:
                        pe.wait_ge(s["probT_a" if j == 0 else "probT_b"], t)
                    for i in range(4):
                        m = 4 * j + i
                        last = nc.tensor.transpose(turned[j][:, i, :], prob[t % 2][:, 2 * m:2 * m + 2, :], core.ident[:])
                    last.then_inc(s["turned_a" if j == 0 else "turned_b"], 1)

                def mix(t):
                    pe.wait_ge(s["probT_a"], t + 1)
                    pe.wait_ge(s["probT_b"], t + 1)
                    if t:
                        pe.wait_ge(s["mixed_done"], t)
                    for m in range(8):
                        last = nc.tensor.matmul(pv[:, m], probT[t % 2][:, m, :], values[:, 2 * t + m // 4, m % 4], start=True, stop=True)
                    last.then_inc(s["pv_done"], 1)

                def turn_mixed(t):
                    pe.wait_ge(s["mixed_done"], t + 1)
                    if t:
                        pe.wait_ge(s["added"], t)
                    for j in range(2):
                        last = nc.tensor.transpose(joint[:, 128 * j:128 * j + 128], mixed[t % 2][:, j, :], core.ident[:])
                    last.then_inc(s["mixed_turned"], 1)

                def output(t):
                    pe.wait_ge(s["mixedT_done"], t + 1)
                    for j in range(2):
                        o = joint[64 * j:64 * j + 64, 256:384]
                        for c in range(2):
                            nc.tensor.matmul(o, mixedT[t % 2][:, j, c, :], wu[:], start=(c == 0), stop=False)
                        last = nc.tensor.matmul(o, core.ones[0:1, 0:S], bu[:], start=False, stop=True)
                    last.then_inc(s["out_done"], 1)

                for t in range(-1, T + 2):
                    if there(t + 1):
                        scores(t + 1, 0)
                    if there(t - 1):
                        mix(t - 1)
                    if there(t + 1):
                        scores(t + 1, 1)
                    if there(t - 2):
                        output(t - 2)
                    if there(t):
                        turn(t, 1)
                    if there(t - 1):
                        turn_mixed(t - 1)
                    if there(t):
                        turn(t, 0)

            @block.scalar
            def _(act):
                def copy_mixed(t):
                    act.wait_ge(s["mixed_turned"], t + 1)
                    nc.scalar.activation(mixedT[t % 2][:].rearrange("p j c s -> p (j c s)"), joint[:, 0:256], ACT.Copy).then_inc(s["mixedT_done"], 1)

                def copy_turned(t):
                    act.wait_ge(s["turned_a"], t + 1)
                    if t >= 2:
                        act.wait_ge(s["pv_done"], t - 1)
                    nc.scalar.activation(probT[t % 2][:, 0:4, :], turned[0][:], ACT.Copy).then_inc(s["probT_a"], 1)

                def exponentiate(t):
                    act.wait_ge(s["shifted_done"], t + 1)
                    if t >= 2:
                        act.wait_ge(s["turned_a"], t - 1)
                    nc.scalar.activation(prob[t % 2][:].rearrange("p (j h) s -> p h j s", h=H), shifted[t % 2][:],
                                         ACT.Exp, scale=SCALE).then_inc(s["prob_done"], 1)

                for t in range(-1, T + 1):
                    if there(t - 1):
                        copy_mixed(t - 1)
                    if there(t):
                        copy_turned(t)
                    if there(t + 1):
                        exponentiate(t + 1)

            @block.vector
            def _(dve):
                def add(t):
                    dve.wait_ge(s["out_done"], t + 1)
                    nc.vector.tensor_tensor(core.x[:, t, :], joint[:, 256:384], core.x[:, t, :], ALU.add).then_inc(s["added"], 1)

                def divide(t):
                    p = t % 2
                    dve.wait_ge(s["pv_done"], t + 1)
                    nc.vector.reciprocal(inv[p][:].rearrange("p (m g) -> p m g", g=2), pv[:, :, :, DK]).then_inc(s["inv_done"], 1)
                    dve.wait_ge(s["inv_done"], t + 1)
                    if t >= 2:
                        dve.wait_ge(s["mixed_turned"], t - 1)
                    nc.vector.scalar_tensor_tensor(mixed[p][:].rearrange("p j (h d) -> p (j h) d", d=DK),
                                                   pv[:].rearrange("p m g v -> p (m g) v")[:, :, 0:DK], 0.5,
                                                   inv[p][:].unsqueeze(2).broadcast_to([128, 2 * H, DK]),
                                                   ALU.mult, ALU.mult).then_inc(s["mixed_done"], 1)

                def shift(t):
                    p = t % 2
                    dve.wait_ge(s["score_done"], t + 1)
                    nc.vector.tensor_reduce(top[p][:], score[p][:], AX.X, ALU.max).then_inc(s["top_done"], 1)
                    dve.wait_ge(s["top_done"], t + 1)
                    if t >= 2:
                        dve.wait_ge(s["prob_done"], t - 1)
                    nc.vector.tensor_tensor(shifted[p][:], score[p][:], top[p][:].unsqueeze(3).broadcast_to([128, H, 2, S]),
                                            ALU.subtract).then_inc(s["shifted_done"], 1)

                def copy_turned(t):
                    dve.wait_ge(s["turned_b"], t + 1)
                    if t >= 2:
                        dve.wait_ge(s["pv_done"], t - 1)
                    nc.vector.tensor_copy(probT[t % 2][:, 4:8, :], turned[1][:]).then_inc(s["probT_b"], 1)

                for t in range(-1, T + 2):
                    if there(t - 1):
                        divide(t - 1)
                    if there(t - 2):
                        add(t - 2)
                    if there(t + 1):
                        shift(t + 1)
                    if there(t):
                        copy_turned(t)

def choose_two(nc, st, dve, act_exp, done, logits, first, weights, E):
    K = T * E
    top = st.sb("top", [128, 2, T])
    equal = st.sb("equal", [128, T, E])
    rank = st.sb("rank", [128, T])
    pick = [st.sb(f"pick{i}", [128, T, E]) for i in range(2)]
    rest = st.sb("rest", [128, T, E])
    step = st.sem("choose_step")
    n = 0
    wide = lambda v: v.unsqueeze(2).broadcast_to([128, T, E])

    for i, src in enumerate((logits, rest)):
        nc.vector.tensor_reduce(top[:, i, :], src[:], AX.X, ALU.max).then_inc(step, 1)
        dve.wait_ge(step, n + 1)
        nc.vector.tensor_tensor(equal[:], src[:], wide(top[:, i, :]), ALU.is_equal).then_inc(step, 1)
        dve.wait_ge(step, n + 2)
        nc.vector.tensor_tensor(equal[:], equal[:], first, ALU.mult).then_inc(step, 1)
        dve.wait_ge(step, n + 3)
        nc.vector.tensor_reduce(rank[:], equal[:], AX.X, ALU.max).then_inc(step, 1)
        dve.wait_ge(step, n + 4)
        nc.vector.tensor_tensor(pick[i][:], equal[:], wide(rank[:]), ALU.is_equal).then_inc(step, 1)
        dve.wait_ge(step, n + 5)
        n += 5
        if i == 0:
            nc.vector.scalar_tensor_tensor(rest[:], pick[0][:], -3e38, src[:], ALU.mult, ALU.add).then_inc(step, 1)
            dve.wait_ge(step, n + 1)
            n += 1
    share = st.sb("share", [128, 4, T])
    nc.vector.tensor_tensor(share[:, 0], top[:, 1], top[:, 0], ALU.subtract).then_inc(act_exp[0], 1)
    dve.wait_ge(act_exp[1], 1)
    nc.vector.tensor_scalar_add(share[:, 2], share[:, 1], 1.0).then_inc(step, 1)
    dve.wait_ge(step, n + 1)
    nc.vector.reciprocal(share[:, 3], share[:, 2]).then_inc(step, 1)
    dve.wait_ge(step, n + 2)
    nc.vector.tensor_tensor(share[:, 2], share[:, 1], share[:, 3], ALU.mult).then_inc(step, 1)
    nc.vector.tensor_tensor(pick[0][:], pick[0][:], wide(share[:, 3]), ALU.mult).then_inc(step, 1)
    dve.wait_ge(step, n + 3)
    nc.vector.tensor_tensor(pick[1][:], pick[1][:], wide(share[:, 2]), ALU.mult).then_inc(step, 1)
    dve.wait_ge(step, n + 5)
    nc.vector.tensor_tensor(weights, pick[0][:], pick[1][:], ALU.add).then_inc(done, 1)
    return share


def moe(nc, core):
    E, F, C = 8, 512, 4
    a = core.a
    with Step(nc, "gate") as st:
        gates_ps = st.ps("gates_ps", [128, T, E])
        gates = st.sb("gates", [128, T, E])
        small = st.sb("small", [1, E])
        gates_done, gates_read = st.sem("gates_done"), st.sem("gates_read")
        gap_done, exp_done, weights_done = st.sem("gap_done"), st.sem("exp_done"), st.sem("weights_done")
        turned_done, weightsT_done = st.sem("turned_done"), st.sem("weightsT_done")
        bias_done, bias_free = st.sem("bias_done"), st.sem("bias_free")
        turned = st.ps("turned", [E, 512])
        weightsT = st.sb("weightsT", [E, N])
        bias = [st.ps(f"bias{i}", [128, 4, D]) for i in range(2)]
        block = st.block()
        share = []

        @block.tensor
        def _(pe):
            pe.wait_ge(core.loaded["gate"], 48)
            for t in range(T):
                nc.tensor.matmul(gates_ps[:, t, :], core.xnT[:, 128 * t:128 * t + 128], core.Wg[:], start=True, stop=False)
                last = nc.tensor.matmul(gates_ps[:, t, :], core.ones[0:1, :], core.bg[:], start=False, stop=True)
            last.then_inc(gates_done, 1)
            pe.wait_ge(weights_done, 1)
            for g in range(G):
                if g:
                    pe.wait_ge(weightsT_done, g)
                for k in range(4):
                    last = nc.tensor.transpose(turned[:, 128 * k:128 * k + 128], core.route[:, 4 * g + k, :], core.ident[:])
                last.then_inc(turned_done, 1)
                pe.wait_ge(weightsT_done, g + 1)
                if g >= 2:
                    pe.wait_ge(bias_free, g - 1)
                for k in range(4):
                    t = 4 * g + k
                    last = nc.tensor.matmul(bias[g % 2][:, k, :], weightsT[:, 128 * t:128 * t + 128], core.b2[:], start=True, stop=True)
                last.then_inc(bias_done, 1)

        @block.vector
        def _(dve):
            dve.wait_ge(gates_done, 1)
            nc.vector.tensor_scalar_mul(gates[:], gates_ps[:], 1.0 / (1.0 + 1e-6)).then_inc(gates_read, 1)
            dve.wait_ge(gates_read, 1)
            dve.wait_ge(core.loaded["first8"], 16)
            first = core.first8[:].unsqueeze(1).broadcast_to([128, T, E])
            share.append(choose_two(nc, st, dve, (gap_done, exp_done), weights_done, gates, first, core.route[:], E))
            for g in range(G):
                dve.wait_ge(bias_done, g + 1)
                nc.vector.tensor_tensor(core.x[:, 4 * g:4 * g + 4, :], bias[g % 2][:], core.x[:, 4 * g:4 * g + 4, :],
                                        ALU.add).then_inc(bias_free, 1)

        @block.scalar
        def _(act):
            act.wait_ge(gap_done, 1)
            nc.scalar.activation(share[0][:, 1], share[0][:, 0], ACT.Exp).then_inc(exp_done, 1)
            for g in range(G):
                act.wait_ge(turned_done, g + 1)
                nc.scalar.activation(weightsT[:, 512 * g:512 * g + 512], turned[:], ACT.Copy).then_inc(weightsT_done, 1)

    with Step(nc, "expert") as st:
        w1 = [st.sb(f"w1_{p}", [128, F]) for p in range(2)]
        w2 = [st.sb(f"w2_{p}", [128, C, D]) for p in range(2)]
        b1 = [st.sb(f"b1_{p}", [128, C]) for p in range(2)]
        up = [st.ps(f"up{i}", [128, 512]) for i in range(4)]
        hidden = [st.sb(f"hidden{i}", [128, C, 512]) for i in range(2)]
        down = [st.ps(f"down{i}", [128, 4, D]) for i in range(2)]
        weights_in = [st.sem(f"weights_in{p}") for p in range(2)]
        up_done, hidden_done = st.sem("up_done"), st.sem("hidden_done")
        down_done, down_free = st.sem("down_done"), st.sem("down_free")
        DOWN0, HIDDEN0, FREE0 = 2 * G, C, 2
        block = st.block()

        @block.sync
        def _(sp):
            sp.sem_inc(down_done, DOWN0)
            with sp.Fori(0, E // 2) as i:
                for p in range(2):
                    e = i * 2 + p
                    sp.wait_ge(down_done, e * G + (DOWN0 - G))
                    sp.dma_start(w1[p][:], a["moe_W1"][bass.ds(e, 1), :, :].rearrange("e p f -> (e p) f")).then_inc(weights_in[p], 16)
                    sp.dma_start(w2[p][:], a["moe_W2"][bass.ds(e, 1), :, :, :].rearrange("e p c d -> (e p) c d")).then_inc(weights_in[p], 16)
                    sp.dma_start(b1[p][:], a["moe_b1"][bass.ds(e, 1), :, :].rearrange("e p c -> (e p) c")).then_inc(weights_in[p], 16)

        @block.tensor
        def _(pe):
            with pe.Fori(0, E // 2) as i:
                for p in range(2):
                    e = i * 2 + p

                    def raise_group(g):
                        for c in range(C):
                            pe.wait_ge(hidden_done, e * (G * C) + (C * g + c + 1))
                            nc.tensor.matmul(up[c][:], w1[p][:, 128 * c:128 * c + 128],
                                             core.xnT[:, 512 * g:512 * g + 512], start=True, stop=True).then_inc(up_done, 1)

                    def lower_group(g):
                        pe.wait_ge(hidden_done, e * (G * C) + (C * g + C + HIDDEN0))
                        pe.wait_ge(down_free, e * G + (g + 1))
                        for k in range(4):
                            for c in range(C):
                                last = nc.tensor.matmul(down[g % 2][:, k, :], hidden[g % 2][:, c, 128 * k:128 * k + 128],
                                                        w2[p][:, c, :], start=(c == 0), stop=(c == C - 1))
                        last.then_inc(down_done, 1)

                    pe.wait_ge(weights_in[p], i * 48 + 48)
                    raise_group(0)
                    for g in range(1, G):
                        raise_group(g)
                        lower_group(g - 1)
                    lower_group(G - 1)

        @block.scalar
        def _(act):
            act.sem_inc(hidden_done, HIDDEN0)
            with act.Fori(0, E // 2) as i:
                for p in range(2):
                    e = i * 2 + p
                    act.wait_ge(weights_in[p], i * 48 + 48)
                    for g in range(G):
                        act.wait_ge(down_done, e * G + (g - 1 + DOWN0))
                        for c in range(C):
                            act.wait_ge(up_done, e * (G * C) + (C * g + c + 1))
                            nc.scalar.activation(hidden[g % 2][:, c, :], up[c][:], ACT.Silu, bias=b1[p][:, c:c + 1]).then_inc(hidden_done, 1)

        @block.vector
        def _(dve):
            dve.sem_inc(down_free, FREE0)
            route = core.route[:].rearrange("p t e -> p (t e)")
            with dve.Fori(0, E // 2) as i:
                for p in range(2):
                    e = i * 2 + p
                    for g in range(G):
                        dve.wait_ge(down_done, e * G + (g + 1 + DOWN0))
                        for k in range(4):
                            t = 4 * g + k
                            last = nc.vector.scalar_tensor_tensor(core.x[:, t, :], down[g % 2][:, k, :],
                                                                  route[:, bass.ds(e + E * t, 1)], core.x[:, t, :],
                                                                  ALU.mult, ALU.add)
                        last.then_inc(down_free, 1)


def tiles_in_pairs(engine, first, last, body):
    assert first == 0 and last == T
    for t in (0, 1):
        body(t, t)
    with engine.Fori(1, T // 2 - 1) as i:
        for p in range(2):
            body(i * 2 + p, p)
    for t in (T - 2, T - 1):
        body(t, t % 2)


def head_attention(nc, core, name, w, masked):
    H, DK = 16, 8
    SCALE = DK ** -0.5
    V1 = DK + 1
    with Step(nc, name) as st:
        dup = [st.sb(f"dup{p}", [128, 2, 2, S]) for p in range(2)]
        q = [st.sb(f"q{p}", [128, 128]) for p in range(2)]
        k = [st.sb(f"k{p}", [128, 128]) for p in range(2)]
        keys = [st.sb(f"keys{p}", [128, 8, 2, S]) for p in range(2)]
        values = [st.sb(f"values{p}", [128, H // 2, 2, 2, V1]) for p in range(2)]
        top = [st.sb(f"top{p}", [128, H]) for p in range(2)]
        shifted = [st.sb(f"shifted{p}", [128, H, S]) for p in range(2)]
        prob = [st.sb(f"prob{p}", [128, H, S]) for p in range(2)]
        probT = [st.sb(f"probT{p}", [128, H // 2, 128]) for p in range(2)]
        inv = [st.sb(f"inv{p}", [128, H]) for p in range(2)]
        mixed = [st.sb(f"mixed{p}", [128, 128]) for p in range(2)]
        mixedT = [st.sb(f"mixedT{p}", [128, 128]) for p in range(2)]
        score = [st.ps(f"score{p}", [128, H, S]) for p in range(2)]
        turned = [st.ps(f"turned{j}", [128, 4, 128]) for j in range(2)]
        joint = st.ps("joint", [128, 512])
        pv = st.ps("pv", [128, H // 2, 2, 2, V1])
        s = {n: st.sem(n) for n in (
            "values_set", "dup_done", "qk_done", "v_done", "q_done", "k_done", "values_done", "keys_done", "score_done",
            "top_done", "shifted_done", "prob_done", "turned_a", "turned_b", "probT_a", "probT_b", "pv_done",
            "inv_done", "mixed_done", "mixed_turned", "mixedT_done", "out_done", "added")}
        block = st.block()

        def there(t):
            return not isinstance(t, int) or 0 <= t < T

        def begun(t):
            return not isinstance(t, int) or t >= 0

        def last_of(count):
            return min(count, T) if isinstance(count, int) else count

        def run(engine, body):
            for t in range(-3, 4):
                body(t, t % 2)
            with engine.Fori(2, T // 2 - 2) as i:
                for p in range(2):
                    body(i * 2 + p, p)
            for t in range(T - 4, T + 2):
                body(t, t % 2)

        @block.gpsimd
        def _(pool):
            for p in range(2):
                last = nc.gpsimd.memset(values[p][:], 0.0)
            last.then_inc(s["values_set"], 1)
            pool.wait_ge(s["values_set"], 1)
            for p in range(2):
                for g in range(2):
                    last = nc.gpsimd.memset(values[p][64 * g:64 * g + 64, :, :, g, DK:V1], 1.0)
            last.then_inc(s["values_set"], 1)

            def spread_keys(t, p):
                pool.wait_ge(s["k_done"], t + 1)
                if begun(t - 2):
                    pool.wait_ge(s["score_done"], t - 1)
                nc.gpsimd.tensor_tensor(keys[p][:].rearrange("p h b s -> p h (b s)"),
                                        k[p][:].unsqueeze(1).broadcast_to([128, 8, 128]),
                                        core.head_of[:].unsqueeze(2).broadcast_to([128, 8, 128]),
                                        ALU.mult).then_inc(s["keys_done"], 1)

            def body(t, p):
                if there(t + 3):
                    spread_keys(t + 3, 1 - p)

            pool.wait_ge(core.loaded["head_of"], 16)
            run(pool, body)

        @block.tensor
        def _(pe):
            pe.wait_ge(core.loaded[w["name"]], w["loads"])

            def project(t, p):
                if isinstance(t, int) and -3 < t < 1:
                    pe.wait_ge(s["k_done"], t + 3)
                    if t >= 0:
                        pe.wait_ge(s["values_done"], t + 1)
                if begun(t - 1):
                    pe.wait_ge(s["mixedT_done"], last_of(t))
                if there(t + 3):
                    tok = bass.ds((t + 3) * 128, 128)
                    nc.tensor.matmul(joint[:, 0:128], w["Wq"][:], core.xnT[:, tok], start=True, stop=True)
                    nc.tensor.matmul(joint[:, 128:256], w["Wk"][:], core.ctxT[:, tok], start=True,
                                     stop=True).then_inc(s["qk_done"], 1)
                if there(t + 1):
                    pe.wait_ge(s["dup_done"], t + 2)
                    for b in range(2):
                        o = joint[:, 256 + 128 * b:384 + 128 * b]
                        last = nc.tensor.matmul(o, dup[1 - p][:, b].rearrange("p c s -> p (c s)"), w["Wv"][:], start=True,
                                                stop=not w["bv"])
                        if w["bv"]:
                            last = nc.tensor.matmul(o, core.ones[0:1, :], w["bv"][:], start=False, stop=True)
                    last.then_inc(s["v_done"], 1)

            def wait_for_scores(t):
                pe.wait_ge(s["keys_done"], t + 1)
                pe.wait_ge(s["q_done"], t + 1)
                if begun(t - 2):
                    pe.wait_ge(s["shifted_done"], t - 1)

            def scores(t, p, r):
                rows = slice(64 * r, 64 * r + 64)
                for b in range(2):
                    last = nc.tensor.matmul(score[p][64 * b:64 * b + 64, 8 * r:8 * r + 8, :], q[p][rows, 64 * b:64 * b + 64],
                                            keys[p][rows, :, b, :], start=True, stop=not masked)
                if masked:
                    bias = core.mask_bias[:, bass.ds(t * S, S)].unsqueeze(1).broadcast_to([128, 8, S])
                    last = nc.tensor.matmul(score[p][:, 8 * r:8 * r + 8, :], core.ident16[:], bias, start=False, stop=True)
                if r == 1:
                    last.then_inc(s["score_done"], 1)

            def turn(t, p, j):
                pe.wait_ge(s["prob_done"], t + 1)
                if begun(t - 1):
                    pe.wait_ge(s["probT_a" if j == 0 else "probT_b"], t)
                for i in range(4):
                    m = 4 * j + i
                    last = nc.tensor.transpose(turned[j][:, i, :], prob[p][:, 2 * m:2 * m + 2, :], core.ident[:])
                last.then_inc(s["turned_a" if j == 0 else "turned_b"], 1)

            def mix(t, p):
                pe.wait_ge(s["values_done"], t + 1)
                pe.wait_ge(s["probT_a"], t + 1)
                pe.wait_ge(s["probT_b"], t + 1)
                if begun(t - 1):
                    pe.wait_ge(s["mixed_done"], t)
                for m in range(H // 2):
                    last = nc.tensor.matmul(pv[:, m], probT[p][:, m, :], values[p][:, m], start=True, stop=True)
                last.then_inc(s["pv_done"], 1)

            def turn_mixed(t, p):
                pe.wait_ge(s["mixed_done"], t + 1)
                if begun(t - 1):
                    pe.wait_ge(s["added"], t)
                else:
                    pe.wait_ge(s["k_done"], t + 4)
                    pe.wait_ge(s["values_done"], t + 2)
                nc.tensor.transpose(joint[:, 0:128], mixed[p][:], core.ident[:]).then_inc(s["mixed_turned"], 1)

            def output(t, p):
                pe.wait_ge(s["k_done"], last_of(t + 5))
                pe.wait_ge(s["values_done"], last_of(t + 3))
                pe.wait_ge(s["mixedT_done"], t + 1)
                last = nc.tensor.matmul(joint[:, 128:256], mixedT[p][:], w["Wo"][:], start=True, stop=False)
                nc.tensor.matmul(joint[:, 128:256], core.ones[0:1, :], w["bo"][:], start=False, stop=True).then_inc(s["out_done"], 1)

            def body(t, p):
                if there(t + 1):
                    scores(t + 1, 1 - p, 0)
                if there(t - 1):
                    mix(t - 1, 1 - p)
                if there(t - 2):
                    output(t - 2, p)
                if there(t):
                    turn(t, p, 1)
                if there(t + 1):
                    scores(t + 1, 1 - p, 1)
                if there(t - 1):
                    turn_mixed(t - 1, 1 - p)
                if there(t):
                    turn(t, p, 0)
                if there(t + 2):
                    wait_for_scores(t + 2)
                project(t, p)

            pe.wait_ge(core.loaded["ctxT"], 16)
            run(pe, body)

        @block.scalar
        def _(act):
            act.wait_ge(s["values_set"], 2)
            act.wait_ge(core.loaded[w["name"]], w["loads"])

            def take_qk(t, p):
                act.wait_ge(s["qk_done"], t + 1)
                if begun(t - 2):
                    act.wait_ge(s["v_done"], t - 1)
                    act.wait_ge(s["score_done"], t - 1)
                nc.scalar.activation(q[p][:], joint[:, 0:128], ACT.Identity, bias=w["bq"][:, 0:1]).then_inc(s["q_done"], 1)
                if begun(t - 2):
                    act.wait_ge(s["keys_done"], t - 1)
                nc.scalar.activation(k[p][:], joint[:, 128:256], ACT.Identity, bias=w["bk"][:, 0:1]).then_inc(s["k_done"], 1)

            def take_values(t, p):
                act.wait_ge(s["v_done"], t + 1)
                if begun(t - 2):
                    act.wait_ge(s["pv_done"], t - 1)
                for g in range(2):
                    rows = slice(64 * g, 64 * g + 64)
                    src = joint[rows, 256:512].rearrange("p (b m g d) -> p g m b d", b=2, g=2, d=DK)
                    last = nc.scalar.activation(values[p][rows, :, :, g, 0:DK], src[:, g], ACT.Copy)
                last.then_inc(s["values_done"], 1)

            def body(t, p):
                if there(t - 1):
                    act.wait_ge(s["mixed_turned"], t)
                    if begun(t - 3):
                        act.wait_ge(s["out_done"], t - 2)
                    nc.scalar.activation(mixedT[1 - p][:], joint[:, 0:128], ACT.Copy).then_inc(s["mixedT_done"], 1)
                if there(t):
                    act.wait_ge(s["turned_a"], t + 1)
                    if begun(t - 2):
                        act.wait_ge(s["pv_done"], t - 1)
                    nc.scalar.activation(probT[p][:, 0:4, :], turned[0][:], ACT.Copy).then_inc(s["probT_a"], 1)
                if there(t + 1):
                    act.wait_ge(s["shifted_done"], t + 2)
                    if begun(t - 1):
                        act.wait_ge(s["turned_a"], t)
                    nc.scalar.activation(prob[1 - p][:], shifted[1 - p][:], ACT.Exp, scale=SCALE).then_inc(s["prob_done"], 1)
                if there(t + 3):
                    take_qk(t + 3, 1 - p)
                if there(t + 1):
                    take_values(t + 1, 1 - p)

            run(act, body)

        @block.vector
        def _(dve):
            def duplicate(t, p):
                if begun(t - 2):
                    dve.wait_ge(s["v_done"], t - 1)
                src = core.ctxT[:, bass.ds(t * 128, 128)].rearrange("p (b s) -> p b s", b=2)
                for c in range(2):
                    last = nc.vector.tensor_scalar_mul(dup[p][:, :, c, :], src, 1.0)
                last.then_inc(s["dup_done"], 1)

            def divide(t, p):
                dve.wait_ge(s["pv_done"], t + 1)
                for b in range(2):
                    rows = slice(64 * b, 64 * b + 64)
                    nc.vector.reciprocal(inv[p][rows, :].rearrange("p (m g) -> p m g", g=2),
                                         pv[rows, :, b, :, DK]).then_inc(s["inv_done"], 1)
                dve.wait_ge(s["inv_done"], t * 2 + 2)
                if begun(t - 2):
                    dve.wait_ge(s["mixed_turned"], t - 1)
                for b in range(2):
                    rows = slice(64 * b, 64 * b + 64)
                    o = mixed[p][rows, :].rearrange("p (m g d) -> p m g d", g=2, d=DK)
                    r = inv[p][rows, :].rearrange("p (m g) -> p m g", g=2).unsqueeze(3).broadcast_to([64, H // 2, 2, DK])
                    last = nc.vector.tensor_tensor(o, pv[rows, :, b, :, 0:DK], r, ALU.mult)
                last.then_inc(s["mixed_done"], 1)

            def add(t, p):
                dve.wait_ge(s["out_done"], t + 1)
                xs = core.xflat[:, bass.ds(t * D, D)]
                nc.vector.tensor_tensor(xs, joint[:, 128:256], xs, ALU.add).then_inc(s["added"], 1)

            def shift(t, p):
                dve.wait_ge(s["score_done"], t + 1)
                nc.vector.tensor_reduce(top[p][:], score[p][:], AX.X, ALU.max).then_inc(s["top_done"], 1)
                dve.wait_ge(s["top_done"], t + 1)
                if begun(t - 2):
                    dve.wait_ge(s["prob_done"], t - 1)
                nc.vector.tensor_tensor(shifted[p][:], score[p][:], top[p][:].unsqueeze(2).broadcast_to([128, H, S]),
                                        ALU.subtract).then_inc(s["shifted_done"], 1)

            def body(t, p):
                if there(t - 1):
                    divide(t - 1, 1 - p)
                if there(t + 2):
                    duplicate(t + 2, p)
                if there(t - 2):
                    add(t - 2, p)
                if there(t):
                    dve.wait_ge(s["turned_b"], t + 1)
                    if begun(t - 2):
                        dve.wait_ge(s["pv_done"], t - 1)
                    nc.vector.tensor_copy(probT[p][:, 4:8, :], turned[1][:]).then_inc(s["probT_b"], 1)
                if there(t + 1):
                    shift(t + 1, 1 - p)

            dve.wait_ge(core.loaded["ctxT"], 16)
            run(dve, body)


def l2_attention(nc, core):
    with Step(nc, "mask") as st:
        zero = st.sb("zero", [128, T * S])
        zero_done = st.sem("zero_done")
        block = st.block()

        @block.vector
        def _(dve):
            dve.wait_ge(core.loaded["mask"], 16)
            nc.vector.tensor_copy(zero[:], core.mask[:].rearrange("p t s -> p (t s)")).then_inc(zero_done, 1)
            dve.wait_ge(zero_done, 1)
            nc.vector.tensor_scalar(core.mask_bias[:], zero[:], 0.0, -1e20, ALU.is_equal, ALU.mult)

    head_attention(nc, core, "l2", core.l2, True)


def l3_attention(nc, core):
    head_attention(nc, core, "l3", core.l3, False)


def soft_moe(nc, core):
    a = core.a
    CH, X4 = 16, 4
    top = core.soft_top
    with ExitStack() as life:
        core.soft_down = life.enter_context(nc.sbuf_tensor("soft_down", [128, N], F32))
        with Step(nc, "softpre") as st:
            phi = st.sb("phi", [128, CH, 128])
            waste = st.sb("waste", [128, CH * 128])
            down = st.sb("down", [128, T])
            sums = st.sb("sums", [128, 2, T])
            sum_of_both = st.sb("sum_of_both", [128, T])
            diag = st.sb("diag", [128, T, 128])
            logit = [st.ps(f"logit{p}", [128, CH * 128]) for p in range(2)]
            phi_in, logit_done, top_done = st.sem("phi_in"), st.sem("logit_done"), st.sem("top_done")
            sum_done = st.sem("sum_done")
            exp_done, diag_done, spread_done = st.sem("exp_done"), st.sem("diag_done"), st.sem("spread_done")
            block = st.block()

            @block.sync
            def _(sp):
                sp.dma_start(phi[:], a["soft_phi"].rearrange("c d s -> d c s")).then_inc(phi_in, 16)

            @block.tensor
            def _(pe):
                pe.wait_ge(phi_in, 16)
                for t in range(T):
                    for g in range(G):
                        if t >= 2 and g % 2 == 0:
                            pe.wait_ge(exp_done, 2 * t - 3 + g // 2)
                        last = nc.tensor.matmul(logit[t % 2][:, 512 * g:512 * g + 512], core.xnT[:, 128 * t:128 * t + 128],
                                                phi[:, 4 * g:4 * g + 4, :], start=True, stop=True)
                    last.then_inc(logit_done, 1)
                pe.wait_ge(diag_done, T)
                pe.wait_ge(exp_done, 2 * T)
                for g in range(G):
                    last = nc.tensor.matmul(logit[0][:, 512 * g:512 * g + 512], core.ones[:], diag[:, 4 * g:4 * g + 4, :],
                                            start=True, stop=True)
                last.then_inc(spread_done, 1)

            @block.vector
            def _(dve):
                for t in range(T):
                    dve.wait_ge(logit_done, t + 1)
                    nc.vector.tensor_reduce(down[:, t:t + 1], logit[t % 2][:], AX.X, ALU.max, negate=True).then_inc(top_done, 1)
                for t in range(T):
                    dve.wait_ge(top_done, t + 1)
                    nc.vector.tensor_scalar_mul(diag[:, t, :], core.ident[:], down[:, t:t + 1]).then_inc(diag_done, 1)
                dve.wait_ge(exp_done, 2 * T)
                nc.vector.tensor_tensor(sum_of_both[:], sums[:, 0], sums[:, 1], ALU.add).then_inc(sum_done, 1)
                dve.wait_ge(sum_done, 1)
                nc.vector.reciprocal(top[:], sum_of_both[:])
                dve.wait_ge(spread_done, 1)
                nc.vector.tensor_copy(core.soft_down[:], logit[0][:])

            @block.scalar
            def _(act):
                for t in range(T):
                    act.wait_ge(top_done, t + 1)
                    for h in range(2):
                        half = slice(CH * 64 * h, CH * 64 * h + CH * 64)
                        if t:
                            act.wait_ge(exp_done, 2 * t - 1 + h)
                        nc.scalar.activation(waste[:, half], logit[t % 2][:, half], ACT.Exp, bias=down[:, t:t + 1],
                                             accum_out=sums[:, h, t:t + 1]).then_inc(exp_done, 1)

        result = life.enter_context(nc.sbuf_tensor("soft_result", [128, N], F32))
        with Step(nc, "soft") as st:
            phi = [st.sb(f"phi{p}", [128, 128]) for p in range(2)]
            W = [st.sb(f"W{p}", [128, X4, D]) for p in range(2)]
            bias = [st.sb(f"bias{p}", [128, X4]) for p in range(2)]
            logit = st.sb("logit", [128, B, S])
            spread = st.sb("spread", [128, B, S])
            share = st.sb("share", [128, B, S])
            peak = st.sb("peak", [128, S])
            total = st.sb("total", [128, S])
            inv = st.sb("inv", [128, S])
            given = st.sb("given", [128, T, 128])
            slots = st.sb("slots", [128, 2, T, 128])
            outsT = st.sb("outsT", [128, 2, T, 128])
            outs = st.sb("outs", [128, 2, T, D])
            comb = [st.sb(f"comb{p}", [128, N]) for p in range(2)]
            acc = st.ps("acc", [128, N])
            ring = [st.ps(f"ring{i}", [128, 512]) for i in range(4)]
            s = {n: st.sem(n) for n in (
                "phi0", "phi1", "W0", "W1", "lt_done", "dt_done", "sl_done", "ot_done", "ou_done", "acc_done",
                "lt_read", "dt_read", "sl_a", "sl_d", "ot_a", "ot_d", "ou_a", "ou_d",
                "peak_done", "sub_done", "exp_done", "total_done", "inv_done", "share_done", "low_done", "comb_done",
                "result_done")}
            block = st.block()

            def later(t, n):
                return not isinstance(t, int) or t >= n

            def not_last(t):
                return not (isinstance(t, int) and t + 1 >= CH)

            @block.sync
            def _(sp):
                def body(c, p):
                    if later(c, 2):
                        sp.wait_ge(s["lt_done"], c * 4 - 4)
                    sp.dma_start(phi[p][:], a["soft_phi"][bass.ds(c, 1), :, :].rearrange("c d s -> (c d) s")).then_inc(s[f"phi{p}"], 16)
                    if later(c, 2):
                        sp.wait_ge(s["ot_a"], c * 4 - 4)
                        sp.wait_ge(s["ot_d"], c * 4 - 4)
                    sp.dma_start(W[p][:], a["soft_W"][bass.ds(c, 1), :, :, :].rearrange("c d n e -> (c d) n e")).then_inc(s[f"W{p}"], 16)
                    sp.dma_start(bias[p][:], a["soft_b"][bass.ds(c, 1), :, :].rearrange("c e n -> (c e) n")).then_inc(s[f"W{p}"], 16)

                tiles_in_pairs(sp, 0, CH, body)

            def loads(c, p, unit):
                return (c // 2 + 1) * unit if isinstance(c, int) else (c - p) * (unit // 2) + unit

            @block.tensor
            def _(pe):
                def logits(c, p, groups):
                    pe.wait_ge(s[f"phi{p}"], loads(c, p, 16))
                    for g in groups:
                        if later(c, 2):
                            pe.wait_ge(s["ou_a" if g % 2 == 0 else "ou_d"], c * 4 - 8 + 3 + g // 2)
                        elif later(c, 1):
                            pe.wait_ge(s["lt_read"], g + 1)
                        nc.tensor.matmul(ring[g][:], phi[p][:], core.xnT[:, 512 * g:512 * g + 512], start=True,
                                         stop=True).then_inc(s["lt_done"], 1)

                def turn_shares(c, g):
                    if not_last(c):
                        pe.wait_ge(s["lt_read"], c * 4 + 4 + g + 1)
                    else:
                        pe.wait_ge(s["ou_a" if g % 2 == 0 else "ou_d"], c * 4 - 4 + 3 + g // 2)
                    for k in range(4):
                        t = 4 * g + k
                        last = nc.tensor.transpose(ring[g][:, 128 * k:128 * k + 128], share[:, 2 * t:2 * t + 2, :], core.ident[:])
                    last.then_inc(s["dt_done"], 1)

                def gather(c, p, j):
                    q, r = divmod(j, 2)
                    pe.wait_ge(s["ou_a" if r == 0 else "ou_d"], c * 4 + q + 1)
                    first = isinstance(c, int) and c == 0
                    for k in range(4):
                        b = 2 * (4 * q + k) + r
                        last = nc.tensor.matmul(acc[:, S * b:S * b + S], outs[:, r, 4 * q + k, :], comb[p][:, S * b:S * b + S],
                                                start=first and r == 0 and k == 0, stop=False, skip_group_check=True)
                    return last

                def body(c, p):
                    if not_last(c):
                        logits(c + 1, 1 - p, (0, 1))
                    pe.wait_ge(s["share_done"], c + 1)
                    for g in range(G):
                        turn_shares(c, g)
                        if not_last(c) and g < 2:
                            logits(c + 1, 1 - p, (g + 2,))
                    for j in range(8):
                        q, r = divmod(j, 2)
                        rows = slice(64 * r, 64 * r + 64)
                        pe.wait_ge(s["dt_read"], c * 4 + max(q, j if j < 4 else 0) + 1)
                        if j >= 4:
                            pe.wait_ge(s["sl_a" if j % 2 == 0 else "sl_d"], c * 4 + (j - 4) // 2 + 1)
                        for k in range(4):
                            t = 4 * q + k
                            last = nc.tensor.matmul(ring[j % 4][:, 128 * k:128 * k + 128], core.xn[rows, t, :],
                                                    given[rows, t, :], start=True, stop=True)
                        last.then_inc(s["sl_done"], 1)
                    pe.wait_ge(s[f"W{p}"], loads(c, p, 32))
                    for j in range(8):
                        h, n = divmod(j, 4)
                        if j < 4:
                            pe.wait_ge(s["sl_a"], c * 4 + 3 + (n // 2 if n % 2 == 0 else 0))
                            pe.wait_ge(s["sl_d"], c * 4 + 3 + (n // 2 if n % 2 == 1 else 0))
                        else:
                            pe.wait_ge(s["sl_a"], c * 4 + 4)
                            pe.wait_ge(s["sl_d"], c * 4 + 4)
                            pe.wait_ge(s["ot_a" if j % 2 == 0 else "ot_d"], c * 4 + (j - 4) // 2 + 1)
                        nc.tensor.matmul(ring[j % 4][:], W[p][:, n, :], slots[:, :, 8 * h:8 * h + 8, 32 * n:32 * n + 32],
                                         start=True, stop=True).then_inc(s["ot_done"], 1)
                    pe.wait_ge(s["comb_done"], c + 1)
                    for j in range(8):
                        q, r = divmod(j, 2)
                        pe.wait_ge(s["ot_a"], c * 4 + (3 + j // 2 if j < 4 and j % 2 == 0 else 2 if j < 4 else 4))
                        pe.wait_ge(s["ot_d"], c * 4 + (3 + j // 2 if j < 4 and j % 2 == 1 else 2 if j < 4 else 4))
                        if j >= 4:
                            pe.wait_ge(s["ou_a" if j % 2 == 0 else "ou_d"], c * 4 + (j - 4) // 2 + 1)
                        for k in range(4):
                            t = 4 * q + k
                            last = nc.tensor.transpose(ring[j % 4][:, 128 * k:128 * k + 128], outsT[:, r, t, :], core.ident[:])
                        last.then_inc(s["ou_done"], 1)
                        if j >= 2:
                            gather(c, p, j - 2)
                    gather(c, p, 6)
                    gather(c, p, 7).then_inc(s["acc_done"], 1)

                logits(0, 0, range(G))
                tiles_in_pairs(pe, 0, CH, body)

            @block.gpsimd
            def _(pool):
                def lower(c, p):
                    pool.wait_ge(s["lt_read"], c * 4 + 4)
                    if later(c, 2):
                        pool.wait_ge(s["acc_done"], c - 1)
                    nc.gpsimd.tensor_tensor(comb[p][:], logit[:].rearrange("p b s -> p (b s)"), core.soft_down[:],
                                            ALU.add).then_inc(s["low_done"], 1)

                def divide(c):
                    pool.wait_ge(s["inv_done"], c + 1)
                    if later(c, 1):
                        pool.wait_ge(s["dt_done"], c * 4)
                    nc.gpsimd.tensor_tensor(share[:], spread[:], inv[:].unsqueeze(1).broadcast_to([128, B, S]),
                                            ALU.mult).then_inc(s["share_done"], 1)

                lower(0, 0)

                def body(c, p):
                    if not_last(c):
                        lower(c + 1, 1 - p)
                        divide(c + 1)

                tiles_in_pairs(pool, 0, CH, body)

            @block.scalar
            def _(act):
                def take_logits(c):
                    if later(c, 1):
                        act.wait_ge(s["sub_done"], c)
                        act.wait_ge(s["low_done"], c)
                    for g in range(G):
                        act.wait_ge(s["lt_done"], c * 4 + g + 1)
                        nc.scalar.activation(logit[:, 8 * g:8 * g + 8, :].rearrange("p b s -> p (b s)"), ring[g][:],
                                             ACT.Copy).then_inc(s["lt_read"], 1)

                def exp_comb(c, p):
                    act.wait_ge(s["low_done"], c + 1)
                    nc.scalar.activation(comb[p][:], comb[p][:], ACT.Exp).then_inc(s["comb_done"], 1)

                def exp_spread(c):
                    act.wait_ge(s["sub_done"], c + 1)
                    nc.scalar.activation(spread[:], spread[:], ACT.Exp).then_inc(s["exp_done"], 1)

                def body(c, p):
                    if not_last(c):
                        take_logits(c + 1)
                    if later(c, 1):
                        act.wait_ge(s["ot_done"], c * 8)
                    for j in (0, 2, 4, 6):
                        act.wait_ge(s["sl_done"], c * 8 + j + 1)
                        nc.scalar.activation(slots[:, 0, 2 * j:2 * j + 4, :], ring[j % 4][:], ACT.Copy).then_inc(s["sl_a"], 1)
                    if not_last(c):
                        exp_spread(c + 1)
                    act.wait_ge(s[f"W{p}"], loads(c, p, 32))
                    if later(c, 1):
                        act.wait_ge(s["ou_done"], c * 8)
                    for j in (0, 2, 4, 6):
                        h, n = divmod(j, 4)
                        act.wait_ge(s["ot_done"], c * 8 + j + 1)
                        nc.scalar.activation(outsT[:, :, 8 * h:8 * h + 8, 32 * n:32 * n + 32],
                                             ring[j % 4][:].rearrange("p (r t s) -> p r t s", r=2, s=32),
                                             ACT.Identity, bias=bias[p][:, n:n + 1]).then_inc(s["ot_a"], 1)
                    if later(c, 1):
                        act.wait_ge(s["acc_done"], c)
                    for j in (0, 2, 4, 6):
                        act.wait_ge(s["ou_done"], c * 8 + j + 1)
                        nc.scalar.activation(outs[:, 0, 2 * j:2 * j + 4, :], ring[j % 4][:], ACT.Copy).then_inc(s["ou_a"], 1)
                    if not_last(c):
                        exp_comb(c + 1, 1 - p)

                take_logits(0)
                exp_spread(0)
                exp_comb(0, 0)
                tiles_in_pairs(act, 0, CH, body)

            @block.vector
            def _(dve):
                by_token = lambda v: v[:].rearrange("p b s -> p s b")
                all_batches = lambda v: v[:].unsqueeze(1).broadcast_to([128, B, S])

                def largest(c):
                    dve.wait_ge(s["lt_read"], c * 4 + 4)
                    nc.vector.tensor_reduce(peak[:], by_token(logit), AX.X, ALU.max).then_inc(s["peak_done"], 1)

                def subtract(c):
                    dve.wait_ge(s["peak_done"], c + 1)
                    if later(c, 1):
                        dve.wait_ge(s["share_done"], c)
                    nc.vector.tensor_tensor(spread[:], logit[:], all_batches(peak), ALU.subtract).then_inc(s["sub_done"], 1)

                def sum_up(c):
                    dve.wait_ge(s["exp_done"], c + 1)
                    nc.vector.tensor_reduce(total[:], by_token(spread), AX.X, ALU.add).then_inc(s["total_done"], 1)
                    dve.wait_ge(s["total_done"], c + 1)
                    nc.vector.reciprocal(inv[:], total[:]).then_inc(s["inv_done"], 1)

                def body(c, p):
                    if later(c, 1):
                        dve.wait_ge(s["sl_done"], c * 8)
                    for g in range(G):
                        dve.wait_ge(s["dt_done"], c * 4 + g + 1)
                        nc.vector.tensor_copy(given[:, 4 * g:4 * g + 4, :], ring[g][:]).then_inc(s["dt_read"], 1)
                    if later(c, 1):
                        dve.wait_ge(s["ot_done"], c * 8)
                    if not_last(c):
                        largest(c + 1)
                    for j in (1, 3, 5, 7):
                        if j == 5 and not_last(c):
                            subtract(c + 1)
                        dve.wait_ge(s["sl_done"], c * 8 + j + 1)
                        nc.vector.tensor_copy(slots[:, 1, 2 * j - 2:2 * j + 2, :], ring[j % 4][:]).then_inc(s["sl_d"], 1)
                    dve.wait_ge(s[f"W{p}"], loads(c, p, 32))
                    if later(c, 1):
                        dve.wait_ge(s["ou_done"], c * 8)
                    for j in (1, 3, 5, 7):
                        h, n = divmod(j, 4)
                        if j == 5 and not_last(c):
                            sum_up(c + 1)
                        dve.wait_ge(s["ot_done"], c * 8 + j + 1)
                        nc.vector.tensor_scalar_add(outsT[:, :, 8 * h:8 * h + 8, 32 * n:32 * n + 32],
                                                    ring[j % 4][:].rearrange("p (r t s) -> p r t s", r=2, s=32),
                                                    bias[p][:, n:n + 1]).then_inc(s["ot_d"], 1)
                    if later(c, 1):
                        dve.wait_ge(s["acc_done"], c)
                    for j in (1, 3, 5, 7):
                        dve.wait_ge(s["ou_done"], c * 8 + j + 1)
                        nc.vector.tensor_copy(outs[:, 1, 2 * j - 2:2 * j + 2, :], ring[j % 4][:]).then_inc(s["ou_d"], 1)

                largest(0)
                subtract(0)
                sum_up(0)
                dve.wait_ge(s["inv_done"], 1)
                nc.vector.tensor_tensor(share[:], spread[:], all_batches(inv), ALU.mult).then_inc(s["share_done"], 1)
                tiles_in_pairs(dve, 0, CH, body)
                dve.wait_ge(s["acc_done"], CH)
                nc.vector.tensor_copy(result[:], acc[:])

        with Step(nc, "softend") as st:
            turned = [st.ps(f"turned{g}", [128, 4, 128]) for g in range(G)]
            turned_done = st.sem("turned_done")
            block = st.block()

            @block.tensor
            def _(pe):
                for t in range(T):
                    last = nc.tensor.transpose(turned[t // 4][:, t % 4, :], result[:, 128 * t:128 * t + 128], core.ident[:])
                    if t % 4 == 3:
                        last.then_inc(turned_done, 1)

            @block.vector
            def _(dve):
                for t in range(T):
                    dve.wait_ge(turned_done, t // 4 + 1)
                    nc.vector.scalar_tensor_tensor(core.x[:, t, :], turned[t // 4][:, t % 4, :], top[:, t:t + 1],
                                                   core.x[:, t, :], ALU.mult, ALU.add)


def code_moe(nc, core):
    E, HID, K = 6, 64, 6
    with Step(nc, "codes") as st:
        z_ps = st.ps("z_ps", [128, T, E])
        code = st.sb("code", [128, T, K])
        both = st.sb("both", [128, T, E, K])
        dot = st.sb("dot", [128, T, E])
        temp = st.sb("temp", [128, 2])
        logits = st.sb("logits", [128, T, E])
        z_done, code_done, step = st.sem("z_done"), st.sem("code_done"), st.sem("step")
        gap_done, exp_done, weights_done = st.sem("gap_done"), st.sem("exp_done"), st.sem("weights_done")
        share = []
        block = st.block()

        @block.tensor
        def _(pe):
            pe.wait_ge(core.loaded["code"], core.code_loads)
            for t in range(T):
                last = nc.tensor.matmul(z_ps[:, t, :], core.xnT[:, 128 * t:128 * t + 128], core.code_w[:], start=True, stop=True)
            last.then_inc(z_done, 1)

        @block.vector
        def _(dve):
            dve.wait_ge(core.loaded["code"], core.code_loads)
            nc.vector.tensor_scalar_max(temp[:, 0:1], core.code_temp[:], 0.1).then_inc(step, 1)
            dve.wait_ge(step, 1)
            nc.vector.reciprocal(temp[:, 1:2], temp[:, 0:1]).then_inc(step, 1)
            dve.wait_ge(code_done, 1)
            for e in range(E):
                last = nc.vector.tensor_tensor(both[:, :, e, :], code[:],
                                               core.anchors[:, e, :].unsqueeze(1).broadcast_to([128, T, K]), ALU.mult)
            last.then_inc(step, 1)
            dve.wait_ge(step, 3)
            nc.vector.tensor_reduce(dot[:], both[:], AX.X, ALU.add).then_inc(step, 1)
            dve.wait_ge(step, 4)
            nc.vector.tensor_scalar(logits[:], dot[:], 6.0, 0.5, ALU.subtract, ALU.mult).then_inc(step, 1)
            dve.wait_ge(step, 5)
            nc.vector.tensor_scalar_mul(logits[:], logits[:], temp[:, 1:2]).then_inc(step, 1)
            dve.wait_ge(step, 6)
            first = core.first6[:].unsqueeze(1).broadcast_to([128, T, E])
            share.append(choose_two(nc, st, dve, (gap_done, exp_done), weights_done, logits, first, core.code_route[:], E))

        @block.scalar
        def _(act):
            act.wait_ge(z_done, 1)
            nc.scalar.activation(code[:], z_ps[:], ACT.Tanh, scale=1.0 / 0.3).then_inc(code_done, 1)
            act.wait_ge(gap_done, 1)
            nc.scalar.activation(share[0][:, 1], share[0][:, 0], ACT.Exp).then_inc(exp_done, 1)

    with Step(nc, "codex") as st:
        P = E // 2
        up = [st.ps(f"up{i}", [128, 512]) for i in range(4)]
        hidden = [st.sb(f"hidden{i}", [128, P, 512]) for i in range(2)]
        down = [st.ps(f"down{i}", [128, 4, D]) for i in range(4)]
        up_done, hidden_done, down_done = st.sem("up_done"), st.sem("hidden_done"), st.sem("down_done")
        added = st.sem("added")
        block = st.block()

        @block.tensor
        def _(pe):
            def raise_group(g):
                for c in range(P):
                    n = P * g + c
                    if n >= 4:
                        pe.wait_ge(hidden_done, n - 3)
                    nc.tensor.matmul(up[n % 4][:], core.code_w1[:, 128 * c:128 * c + 128], core.xnT[:, 512 * g:512 * g + 512],
                                     start=True, stop=True).then_inc(up_done, 1)

            raise_group(0)
            for g in range(G):
                if g + 1 < G:
                    raise_group(g + 1)
                for c in range(P):
                    pe.wait_ge(hidden_done, P * g + c + 1)
                    n = P * g + c
                    if n >= 2:
                        pe.wait_ge(added, 2 * n - 2)
                    for k in range(4):
                        for r in range(2):
                            rows = slice(HID * r, HID * r + HID)
                            last = nc.tensor.matmul(down[2 * (n % 2) + r][:, k, :], hidden[g % 2][rows, c, 128 * k:128 * k + 128],
                                                    core.code_w2[rows, c, :], start=True, stop=True)
                    last.then_inc(down_done, 1)

        @block.scalar
        def _(act):
            for g in range(G):
                for c in range(P):
                    n = P * g + c
                    act.wait_ge(up_done, n + 1)
                    if g >= 2:
                        act.wait_ge(down_done, P * (g - 2) + c + 1)
                    nc.scalar.activation(hidden[g % 2][:, c, :], up[n % 4][:], ACT.Gelu_apprx_tanh).then_inc(hidden_done, 1)

        @block.vector
        def _(dve):
            for g in range(G):
                for c in range(P):
                    n = P * g + c
                    dve.wait_ge(down_done, n + 1)
                    for r in range(2):
                        e = 2 * c + r
                        if n or r:
                            dve.wait_ge(added, 2 * n + r)
                        for k in range(4):
                            t = 4 * g + k
                            last = nc.vector.scalar_tensor_tensor(core.x[:, t, :], down[2 * (n % 2) + r][:, k, :],
                                                                  core.code_route[:, t, e:e + 1], core.x[:, t, :],
                                                                  ALU.mult, ALU.add)
                        last.then_inc(added, 1)


def prepare(nc, core, sb, load):
    a = core.a
    if 1 in STAGES:
        core.w1T = sb("w1T", [128, 512])
        core.w2T = sb("w2T", [128, 4, D])
        core.conv = sb("conv", [128, 4, 4])
        core.bit_mean = sb("bit_mean", [128, 2])
        core.bit_scale = sb("bit_scale", [128, 2])
        core.bit_w = sb("bit_w", [128, 2, 512], BF16)
        load("w1T", core.w1T[:], a["bit_w1T"])
        load("w2T", core.w2T[:], a["bit_w2T"])
        load("conv", core.conv[:], a["bit_conv"])
    if 3 in STAGES:
        core.Wg, core.bg, core.b2 = sb("Wg", [128, 8]), sb("bg", [1, 8]), sb("b2", [8, D])
        core.route = sb("route", [128, T, 8])
        core.first8 = sb("first8", [128, 8])
        load("gate", core.Wg[:], a["moe_Wg"])
        load("gate", core.bg[:], a["moe_bg"])
        load("gate", core.b2[:], a["moe_b2"])
        load("first8", core.first8[:], a["first8"])

    for n, key in ((4, "l2"), (6, "l3")):
        if n in STAGES:
            w = {"name": key}
            for part in ("Wq", "Wk", "Wv", "Wo"):
                w[part] = sb(f"{key}_{part}", [128, D])
                load(key, w[part][:], a[f"{key}_{part}"])
            w["bo"] = sb(f"{key}_bo", [1, D])
            load(key, w["bo"][:], a[f"{key}_bo"])
            w["loads"] = 16 * 5
            w["bv"] = None
            if key == "l3":
                w["bv"], w["bq"], w["bk"] = sb("l3_bv", [1, D]), sb("l3_bq", [128, 1]), sb("l3_bk", [128, 1])
                for part in ("bv", "bq", "bk"):
                    load(key, w[part][:], a[f"l3_{part}"])
                w["loads"] += 48
                core.l3 = w
            else:
                w["bq"] = w["bk"] = core.zero
                core.l2 = w
    if 4 in STAGES or 6 in STAGES:
        core.head_of = sb("head_of", [128, 8])
        load("head_of", core.head_of[:], a["head_of"])
    if 4 in STAGES:
        core.mask = sb("mask", [128, T, S], I32)
        core.mask_bias = sb("mask_bias", [128, T * S], BF16)
        load("mask", core.mask[:], a["mask"])
    if 2 in STAGES:
        w = core.l1 = {"loads": 16 * 6}
        for part in ("Wk", "Wq", "Wv", "Wu"):
            w[part] = sb(f"l1_{part}", [128, D])
            load("l1", w[part][:], a[f"l1_{part}"])
        w["bu"] = sb("l1_bu", [1, D])
        core.parity = sb("parity", [128, 2])
        load("l1", w["bu"][:], a["l1_bu"])
        load("l1", core.parity[:], a["parity"])
    if 7 in STAGES:
        core.code_loads = 16 * 6
        core.code_w, core.code_temp = sb("code_w", [128, 6]), sb("code_temp", [128, 1])
        core.code_w1, core.code_w2 = sb("code_w1", [128, 384]), sb("code_w2", [128, 3, D])
        core.anchors, core.first6 = sb("anchors", [128, 6, 6]), sb("first6", [128, 6])
        core.code_route = sb("code_route", [128, T, 6])
        for part in ("w", "temp", "w1", "w2"):
            load("code", {"w": core.code_w, "temp": core.code_temp, "w1": core.code_w1, "w2": core.code_w2}[part][:], a[f"code_{part}"])
        load("code", core.anchors[:], a["code_anchors"])
        load("code", core.first6[:], a["first6"])
    if 5 in STAGES:
        core.soft_top = sb("soft_top", [128, T])


def layout(v):
    import numpy as np

    out = {"x": v["x"], "ctx_1024": v["ctx_1024"]}
    out["ctxT"] = v["ctx_1024"].reshape(N, D).T
    out["ident"] = np.eye(128, dtype=np.float32)
    out["ones"] = np.ones((128, 128), np.float32)
    out["eps"] = np.full((128, 1), EPS, np.float32)
    out["ident16"] = np.eye(128).astype(mybir.dt.np(BF16))
    out["bit_w1T"] = v["L0_ffn_w1"].T
    out["bit_w2T"] = v["L0_ffn_w2"].T.reshape(4, 128, D).transpose(1, 0, 2)
    taps = np.concatenate([v["L0_ffn_conv_w"].reshape(512, 3), v["L0_ffn_conv_b"][:, None]], 1)
    out["bit_conv"] = taps.reshape(4, 128, 4).transpose(1, 0, 2)
    out["moe_Wg"], out["moe_bg"], out["moe_b2"] = v["L1_ffn_Wg"], v["L1_ffn_bg"][None], v["L1_ffn_b2"]
    out["moe_W1"] = v["L1_ffn_W1"]
    out["moe_W2"] = v["L1_ffn_W2"].reshape(8, 4, 128, D).transpose(0, 2, 1, 3)
    out["moe_b1"] = v["L1_ffn_b1"].reshape(8, 4, 128).transpose(0, 2, 1)
    out["first8"] = np.broadcast_to(np.arange(8, 0, -1, dtype=np.float32), (128, 8))
    out["zero"] = np.zeros((128, 1), np.float32)
    for k in "qkv":
        out[f"l2_W{k}"] = v[f"L2_xattn_W{k}"].transpose(1, 0, 2).reshape(D, D)
        out[f"l3_W{k}"] = v[f"L3_xattn_W{k}"]
    out["l2_Wo"], out["l2_bo"] = v["L2_xattn_Wo"].T, v["L2_xattn_bo"][None]
    out["l3_Wo"], out["l3_bo"], out["l3_bv"] = v["L3_xattn_Wo"], v["L3_xattn_bo"][None], v["L3_xattn_bv"][None]
    out["l3_bq"], out["l3_bk"] = v["L3_xattn_bq"][:, None], v["L3_xattn_bk"][:, None]
    out["head_of"] = (np.arange(128)[:, None] // 8 % 8 == np.arange(8)).astype(np.float32)
    out["mask"] = v["mask_Bx1xSxS2_ik0"].reshape(T, 128, S).transpose(1, 0, 2)
    for k in "kqvu":
        out[f"l1_W{k}"] = v[f"L1_xattn_W{k}"].T
    out["l1_bu"] = v["L1_xattn_bu"][None]
    row, col = np.arange(128)[:, None, None, None], np.arange(128)
    pair, quarter = np.arange(4)[:, None, None], np.arange(4)[:, None]
    out["parity"] = (np.arange(128)[:, None] // 16 % 2 == np.arange(2)).astype(np.float32)
    out["code_w"] = v["L3_ffn_proj_w"].T
    out["code_temp"] = np.broadcast_to(v["L3_ffn_routing_temp"].reshape(1, 1), (128, 1))
    out["code_w1"] = v["L3_ffn_w1"].transpose(1, 0, 2).reshape(D, 384)
    out["code_w2"] = v["L3_ffn_w2"].reshape(3, 128, D).transpose(1, 0, 2)
    out["code_anchors"] = np.broadcast_to(v["L3_ffn_anchors"], (128, 6, 6))
    out["first6"] = np.broadcast_to(np.arange(6, 0, -1, dtype=np.float32), (128, 6))
    out["soft_phi"] = v["L2_ffn_phi"].reshape(D, 16, 128).transpose(1, 0, 2)
    out["soft_W"] = v["L2_ffn_W"].reshape(16, 4, D, D).transpose(0, 2, 1, 3)
    out["soft_b"] = v["L2_ffn_b"].reshape(16, 4, D).transpose(0, 2, 1)
    return out


def clear_semaphores(nc):
    done = sorted(nc.released_uncleared_semaphores)
    if not done:
        return
    with nc.Block() as block:
        @block.gpsimd
        def _(pool):
            start = done[0]
            for at, sem in enumerate(done):
                if at + 1 == len(done) or done[at + 1] != sem + 1:
                    pool.sem_clear(range(start, sem + 1))
                    start = done[at + 1] if at + 1 < len(done) else 0


def build(nc, a):
    core = Core()
    with ExitStack() as life:
        def sb(name, shape, dt=F32):
            return life.enter_context(nc.sbuf_tensor(name, shape, dt))

        core.x = sb("x_tok", [128, T, D])
        core.xflat = core.x[:].rearrange("p t d -> p (t d)")
        core.xn = sb("xn_tok", [128, T, D])
        core.xnT = sb("xnT", [128, N])
        core.ctxT = sb("ctxT", [128, N])
        core.ident = sb("ident", [128, 128])
        core.ones = sb("ones", [128, 128])
        core.eps = sb("eps", [128, 1])
        core.wait_x = core.wait_consts = True
        core.a = a
        core.loaded = {}
        loads = []

        def load(name, dst, src):
            if name not in core.loaded:
                core.loaded[name] = life.enter_context(nc.semaphore(f"loaded_{name}"))
            loads.append((dst, src, core.loaded[name]))

        load("x", core.x[:], a["x"].rearrange("(t h) s d -> (h s) t d", h=2))
        load("consts", core.ident[:], a["ident"])
        loads.append((core.ones[:], a["ones"], core.loaded["consts"]))
        loads.append((core.eps[:], a["eps"], core.loaded["consts"]))
        core.ident16 = sb("ident16", [128, 128], BF16)
        loads.append((core.ident16[:], a["ident16"], core.loaded["consts"]))
        core.zero = sb("zero", [128, 1])
        loads.append((core.zero[:], a["zero"], core.loaded["consts"]))
        core.consts_count = 80
        load("ctxT", core.ctxT[:], a["ctxT"])
        prepare(nc, core, sb, load)
        with nc.Block() as block:
            @block.sync
            def _(sp):
                for dst, src, sem in loads:
                    sp.dma_start(dst, src).then_inc(sem, 16)

        if 0 in STAGES:
            with nc.sbuf_tensor("ctx_tok", [128, T, D], F32) as ctx_tok, nc.semaphore("loaded_ctx") as ctx_in:
                core.ctx_tok = ctx_tok
                core.loaded["ctx"] = ctx_in
                with nc.Block() as block:
                    @block.sync
                    def _(sp):
                        sp.dma_start(ctx_tok[:], a["ctx_1024"].rearrange("(t h) s d -> (h s) t d", h=2)).then_inc(ctx_in, 16)
                costs = nc.dram_tensor("costs", [B, S, S], F32, kind="Internal").ap()
                path = nc.dram_tensor("path", [B, S, S], F32, kind="Internal").ap()
                layernorm(nc, core, "ln0")
                warp_costs(nc, core, costs)
                warp_path(nc, core, costs, path)
                warp_add(nc, core, path)
        for n, stage in enumerate((bit_ffn, l1_attention, moe, l2_attention, soft_moe, l3_attention, code_moe)):
            if n + 1 in STAGES:
                if n + 1 in (2, 4, 5, 6):
                    clear_semaphores(nc)
                layernorm(nc, core, f"ln{n + 1}")
                stage(nc, core)
        with nc.semaphore("stored") as stored, nc.Block() as block:
            @block.sync
            def _(sp):
                sp.dma_start(a["out"].rearrange("(t h) s d -> (h s) t d", h=2), core.x[:]).then_inc(stored, 16)
                sp.wait_ge(stored, 16)


def kernel(**inputs):
    import numpy as np
    import concourse.bacc as bacc
    from concourse.bass_utils import run_bass_kernel_spmd

    nc = bacc.Bacc("TRN2", target_bir_lowering=False, num_devices=1)
    arrays, a = {}, {}
    laid = layout({k: np.asarray(v) for k, v in inputs.items()})
    for name, v in laid.items():
        v = np.ascontiguousarray(v)
        arrays[f"in_{name}"] = v
        a[name] = nc.dram_tensor(f"in_{name}", v.shape, mybir.dt.from_np(v.dtype), kind="ExternalInput").ap()
    a["out"] = nc.dram_tensor("out_x", (B, S, D), F32, kind="ExternalOutput").ap()
    build(nc, a)
    return run_bass_kernel_spmd(nc, [arrays], core_ids=[0]).results[0]["out_x"]
```
